# Optimizing a Trainium2 kernel written in Bass

```python
import numpy as np
import jax
import jax.numpy as jnp

def _softmax(x, axis=-1):
    return jax.nn.softmax(x, axis=axis)

def _gelu(x):
    return jax.nn.gelu(x, approximate=True)

def _silu(x):
    return jax.nn.silu(x)

def _sigmoid(x):
    return jax.nn.sigmoid(x)

def _layernorm(x, axis=-1, eps=1e-05):
    m = jnp.mean(x, axis=axis, keepdims=True)
    v = jnp.var(x, axis=axis, keepdims=True)
    return (x - m) / jnp.sqrt(v + eps)

def _scatter_add(tgt, idx, src, axis=0):
    return tgt.at[idx].add(src)

def _segment_sum(src, seg, n):
    return jax.ops.segment_sum(src, seg, n)
kernel_name = 'mk_gnn_resnorm_d4_gnn_r8_a61401'

def setup_inputs(seed: int=0):
    np.random.seed(seed)
    _w = jnp.asarray

    def _rec_inputs():
        import jax
        import jax.numpy as jnp
        _gk = jax.random.key(seed)
        x = -0.0003713 + 1 * jax.random.normal(jax.random.fold_in(_gk, 1), (6250, 128), jnp.float32)
        _s = jax.random.randint(jax.random.fold_in(_gk, 2), (50000,), 0, 6250, jnp.int32)
        _d = jax.random.randint(jax.random.fold_in(_gk, 3), (50000,), 0, 6250, jnp.int32)
        _loop = jnp.arange(6250, dtype=jnp.int32)
        src = jnp.concatenate([_s, _d, _loop])
        dst = jnp.concatenate([_d, _s, _loop])
        _o = jnp.argsort(dst, stable=True)
        src = src[_o]
        dst = dst[_o]
        edge_attr_3 = -0.000451519 + 1.00018 * jax.random.normal(jax.random.fold_in(_gk, 12), (106250, 3), jnp.float32)
        edge_attr_64 = 0.000155561 + 1.00019 * jax.random.normal(jax.random.fold_in(_gk, 13), (106250, 64), jnp.float32)
        edge_weight = jax.random.uniform(jax.random.fold_in(_gk, 15), (106250,), jnp.float32, 0.0, 0.999998)
        return (x, src, dst, edge_attr_3, edge_attr_64, edge_weight)
    x, src, dst, edge_attr_3, edge_attr_64, edge_weight = _rec_inputs()

    def _L0_gnn_setup():
        import jax, jax.numpy as jnp
        import numpy as np
        N_NODES = 12500
        N_EDGES = 100000
        IN_DIM = 128
        NUM_HEADS = 8
        HEAD_DIM = 16
        key = jax.random.key(seed)
        ks = jax.random.split(key, 10)
        scale = 1.0 / np.sqrt(IN_DIM)
        return {'x': jax.random.normal(ks[0], (N_NODES, IN_DIM), dtype=jnp.float32), 'edge_index': jax.random.randint(ks[1], (2, N_EDGES), 0, N_NODES, dtype=jnp.int64), 'virt_h': jax.random.normal(ks[2], (1, IN_DIM), dtype=jnp.float32), 'virt_edge_index': jax.random.randint(ks[3], (2, 1), 0, 1, dtype=jnp.int64), 'Wq': jax.random.normal(ks[4], (IN_DIM, NUM_HEADS * HEAD_DIM), dtype=jnp.float32) * scale, 'bq': jnp.zeros((NUM_HEADS * HEAD_DIM,), dtype=jnp.float32), 'Wk': jax.random.normal(ks[5], (IN_DIM, NUM_HEADS * HEAD_DIM), dtype=jnp.float32) * scale, 'bk': jnp.zeros((NUM_HEADS * HEAD_DIM,), dtype=jnp.float32), 'Wv': jax.random.normal(ks[6], (IN_DIM, NUM_HEADS * HEAD_DIM), dtype=jnp.float32) * scale, 'bv': jnp.zeros((NUM_HEADS * HEAD_DIM,), dtype=jnp.float32)}
    _L0_gnn_all = _L0_gnn_setup()
    _L0_gnn_in = {k: v for k, v in _L0_gnn_all.items() if k in ('virt_h', 'virt_edge_index', 'Wq', 'bq', 'Wk', 'bk', 'Wv', 'bv')}
    del _L0_gnn_all

    def _L1_gnn_setup():
        import jax, jax.numpy as jnp
        import numpy as np
        N, E, D, ED = (12500, 75000, 128, 64)
        RMS_EPS = 1.1920929e-07
        DEG_POWER = 0.5
        key = jax.random.key(seed)
        ks = jax.random.split(key, 12)
        s = 0.05
        return {'x': jax.random.normal(ks[0], (N, D), jnp.float32), 'edge_index': jax.random.randint(ks[1], (2, E), 0, N, jnp.int32), 'edge_attr': jax.random.normal(ks[2], (E, ED), jnp.float32), 'W1n': jax.random.normal(ks[3], (D, D), jnp.float32) * s, 'b1n': jnp.zeros((D,), jnp.float32), 'W2n': jax.random.normal(ks[4], (D, D), jnp.float32) * s, 'b2n': jnp.zeros((D,), jnp.float32), 'W1e': jax.random.normal(ks[5], (ED, D), jnp.float32) * s, 'b1e': jnp.zeros((D,), jnp.float32), 'W2e': jax.random.normal(ks[6], (D, D), jnp.float32) * s, 'b2e': jnp.zeros((D,), jnp.float32), 'gin_eps': jnp.float32(0.0), 'rms_w': jnp.ones((D,), jnp.float32)}
    _L1_gnn_all = _L1_gnn_setup()
    _L1_gnn_in = {k: v for k, v in _L1_gnn_all.items() if k in ('W1n', 'b1n', 'W2n', 'b2n', 'W1e', 'b1e', 'W2e', 'b2e', 'gin_eps', 'rms_w')}
    del _L1_gnn_all

    def _L2_gnn_setup():
        import jax, jax.numpy as jnp
        import numpy as np
        N = 6250
        E = 100000
        MUL = 32
        NB = 8
        R_MAX = 1.0
        AVG = 16.0
        SQ3 = 3.0 ** 0.5

        def _radial_embedding(r):
            x = jnp.clip(r / R_MAX, 0.0, 1.0)
            centers = jnp.arange(NB, dtype=jnp.float32) / (NB - 1)
            sigma = 1.0 / (NB - 1)
            emb = jnp.exp(-0.5 * ((x[:, None] - centers[None, :]) / sigma) ** 2)
            emb = emb * NB ** 0.5 * (r <= R_MAX).astype(jnp.float32)[:, None]
            return emb
        key = jax.random.key(seed)
        k = jax.random.split(key, 12)
        inp = {'node_feats': jax.random.normal(k[0], (N, 4 * MUL), dtype=jnp.float32), 'edge_vec': jax.random.normal(k[1], (E, 3), dtype=jnp.float32), 'edge_length': jax.random.uniform(k[2], (E,), dtype=jnp.float32), 'senders': jax.random.randint(k[3], (E,), 0, N, dtype=jnp.int32), 'receivers': jax.random.randint(k[4], (E,), 0, N, dtype=jnp.int32), 'num_nodes': N, 'W_up0': jax.random.normal(k[5], (MUL, MUL), dtype=jnp.float32), 'W_up1': jax.random.normal(k[6], (MUL, MUL), dtype=jnp.float32), 'mlp_w0': jax.random.normal(k[7], (NB, 64), dtype=jnp.float32) / NB ** 0.5, 'mlp_b0': jnp.zeros((64,), dtype=jnp.float32), 'mlp_w1': jax.random.normal(k[8], (64, 64), dtype=jnp.float32) / 8.0, 'mlp_b1': jnp.zeros((64,), dtype=jnp.float32), 'mlp_w2': jax.random.normal(k[9], (64, 4 * MUL), dtype=jnp.float32) / 8.0, 'mlp_b2': jnp.zeros((4 * MUL,), dtype=jnp.float32), 'W_out0': jax.random.normal(k[10], (2 * MUL, MUL), dtype=jnp.float32), 'W_out1': jax.random.normal(k[11], (2 * MUL, MUL), dtype=jnp.float32)}
        return inp
    _L2_gnn_all = _L2_gnn_setup()
    _L2_gnn_in = {k: v for k, v in _L2_gnn_all.items() if k in ('W_up0', 'W_up1', 'mlp_w0', 'mlp_b0', 'mlp_w1', 'mlp_b1', 'mlp_w2', 'mlp_b2', 'W_out0', 'W_out1')}
    del _L2_gnn_all

    def _L3_gnn_setup():
        import jax, jax.numpy as jnp
        import numpy as np
        N_NODES = 6250
        N_EDGES = 100000
        IN_FEATS = 128
        HEADS = 4
        OUT_FEATS = 32
        NEG_SLOPE = 0.2

        def _edge_softmax(e, dst, n_nodes):
            seg_max = jax.ops.segment_max(e, dst, num_segments=n_nodes)
            ex = jnp.exp(e - seg_max[dst])
            seg_sum = jax.ops.segment_sum(ex, dst, num_segments=n_nodes)
            return ex / seg_sum[dst]
        key = jax.random.key(seed)
        ks = jax.random.split(key, 9)
        HD = HEADS * OUT_FEATS
        return {'feat': jax.random.normal(ks[0], (N_NODES, IN_FEATS), dtype=jnp.float32), 'W_src': jax.random.normal(ks[1], (HD, IN_FEATS), dtype=jnp.float32) * (1.0 / np.sqrt(IN_FEATS)), 'b_src': jax.random.normal(ks[2], (HD,), dtype=jnp.float32) * 0.02, 'W_dst': jax.random.normal(ks[3], (HD, IN_FEATS), dtype=jnp.float32) * (1.0 / np.sqrt(IN_FEATS)), 'b_dst': jax.random.normal(ks[4], (HD,), dtype=jnp.float32) * 0.02, 'W_v': jax.random.normal(ks[5], (HD, IN_FEATS), dtype=jnp.float32) * (1.0 / np.sqrt(IN_FEATS)), 'b_v': jax.random.normal(ks[6], (HD,), dtype=jnp.float32) * 0.02, 'src': jax.random.randint(ks[7], (N_EDGES,), 0, N_NODES, dtype=jnp.int32), 'dst': jax.random.randint(ks[8], (N_EDGES,), 0, N_NODES, dtype=jnp.int32)}
    _L3_gnn_all = _L3_gnn_setup()
    _L3_gnn_in = {k: v for k, v in _L3_gnn_all.items() if k in ('W_src', 'b_src', 'W_dst', 'b_dst', 'W_v', 'b_v')}
    del _L3_gnn_all
    return {'x': x, 'src': src, 'dst': dst, 'edge_attr_3': edge_attr_3, 'edge_attr_64': edge_attr_64, 'edge_weight': edge_weight, 'L0_gnn_virt_h': _L0_gnn_in['virt_h'], 'L0_gnn_virt_edge_index': _L0_gnn_in['virt_edge_index'], 'L0_gnn_Wq': _L0_gnn_in['Wq'], 'L0_gnn_bq': _L0_gnn_in['bq'], 'L0_gnn_Wk': _L0_gnn_in['Wk'], 'L0_gnn_bk': _L0_gnn_in['bk'], 'L0_gnn_Wv': _L0_gnn_in['Wv'], 'L0_gnn_bv': _L0_gnn_in['bv'], 'L1_gnn_W1n': _L1_gnn_in['W1n'], 'L1_gnn_b1n': _L1_gnn_in['b1n'], 'L1_gnn_W2n': _L1_gnn_in['W2n'], 'L1_gnn_b2n': _L1_gnn_in['b2n'], 'L1_gnn_W1e': _L1_gnn_in['W1e'], 'L1_gnn_b1e': _L1_gnn_in['b1e'], 'L1_gnn_W2e': _L1_gnn_in['W2e'], 'L1_gnn_b2e': _L1_gnn_in['b2e'], 'L1_gnn_gin_eps': _L1_gnn_in['gin_eps'], 'L1_gnn_rms_w': _L1_gnn_in['rms_w'], 'L2_gnn_W_up0': _L2_gnn_in['W_up0'], 'L2_gnn_W_up1': _L2_gnn_in['W_up1'], 'L2_gnn_mlp_w0': _L2_gnn_in['mlp_w0'], 'L2_gnn_mlp_b0': _L2_gnn_in['mlp_b0'], 'L2_gnn_mlp_w1': _L2_gnn_in['mlp_w1'], 'L2_gnn_mlp_b1': _L2_gnn_in['mlp_b1'], 'L2_gnn_mlp_w2': _L2_gnn_in['mlp_w2'], 'L2_gnn_mlp_b2': _L2_gnn_in['mlp_b2'], 'L2_gnn_W_out0': _L2_gnn_in['W_out0'], 'L2_gnn_W_out1': _L2_gnn_in['W_out1'], 'L3_gnn_W_src': _L3_gnn_in['W_src'], 'L3_gnn_b_src': _L3_gnn_in['b_src'], 'L3_gnn_W_dst': _L3_gnn_in['W_dst'], 'L3_gnn_b_dst': _L3_gnn_in['b_dst'], 'L3_gnn_W_v': _L3_gnn_in['W_v'], 'L3_gnn_b_v': _L3_gnn_in['b_v']}

def reference(x, src, dst, edge_attr_3, edge_attr_64, edge_weight, L0_gnn_virt_h, L0_gnn_virt_edge_index, L0_gnn_Wq, L0_gnn_bq, L0_gnn_Wk, L0_gnn_bk, L0_gnn_Wv, L0_gnn_bv, L1_gnn_W1n, L1_gnn_b1n, L1_gnn_W2n, L1_gnn_b2n, L1_gnn_W1e, L1_gnn_b1e, L1_gnn_W2e, L1_gnn_b2e, L1_gnn_gin_eps, L1_gnn_rms_w, L2_gnn_W_up0, L2_gnn_W_up1, L2_gnn_mlp_w0, L2_gnn_mlp_b0, L2_gnn_mlp_w1, L2_gnn_mlp_b1, L2_gnn_mlp_w2, L2_gnn_mlp_b2, L2_gnn_W_out0, L2_gnn_W_out1, L3_gnn_W_src, L3_gnn_b_src, L3_gnn_W_dst, L3_gnn_b_dst, L3_gnn_W_v, L3_gnn_b_v):
    import jax
    import jax.numpy as jnp

    def _L0_gnn_ref(x, edge_index, virt_h, virt_edge_index, Wq, bq, Wk, bk, Wv, bv):
        import jax, jax.numpy as jnp
        import numpy as np
        N_NODES = 12500
        N_EDGES = 100000
        IN_DIM = 128
        NUM_HEADS = 8
        HEAD_DIM = 16
        n = x.shape[0]
        H, D = (NUM_HEADS, HEAD_DIM)
        Q = (x @ Wq + bq).reshape(n, H, D)
        K = (x @ Wk + bk).reshape(n, H, D)
        V = (x @ Wv + bv).reshape(n, H, D)
        src = edge_index[0]
        dst = edge_index[1]
        dot = jnp.sum(K[src] * Q[dst], axis=-1, keepdims=True) / np.sqrt(D).astype(np.float32)
        score = jnp.exp(jnp.clip(dot, -5.0, 5.0))
        msg = V[src] * score
        wV = jax.ops.segment_sum(msg, dst, num_segments=n)
        Z = jax.ops.segment_sum(score, dst, num_segments=n)
        h_out = (wV / (Z + 1e-06)).reshape(n, H * D)
        return h_out

    def _L1_gnn_ref(x, edge_index, edge_attr, W1n, b1n, W2n, b2n, W1e, b1e, W2e, b2e, gin_eps, rms_w):
        import jax, jax.numpy as jnp
        import numpy as np
        N, E, D, ED = (12500, 75000, 128, 64)
        RMS_EPS = 1.1920929e-07
        DEG_POWER = 0.5
        src, dst = (edge_index[0], edge_index[1])
        n = x.shape[0]
        deg = jnp.maximum(jnp.zeros((n,), x.dtype).at[dst].add(1.0), 1.0)
        edge_weight = (deg[src] * deg[dst]) ** (-DEG_POWER)
        edge_msg = jax.nn.relu(edge_attr @ W1e + b1e) @ W2e + b2e
        messages = (x[src] + edge_msg) * edge_weight[:, None]
        agg = jax.ops.segment_sum(messages, dst, num_segments=n)
        combined = (1.0 + gin_eps) * x + agg
        h = jax.nn.relu(combined @ W1n + b1n) @ W2n + b2n
        out = h + x
        out = out * jax.lax.rsqrt(jnp.mean(out * out, axis=-1, keepdims=True) + RMS_EPS) * rms_w
        return out

    def _L2_gnn_ref(node_feats, edge_vec, edge_length, senders, receivers, num_nodes, W_up0, W_up1, mlp_w0, mlp_b0, mlp_w1, mlp_b1, mlp_w2, mlp_b2, W_out0, W_out1):
        import jax, jax.numpy as jnp
        import numpy as np
        N = 6250
        E = 100000
        MUL = 32
        NB = 8
        R_MAX = 1.0
        AVG = 16.0
        SQ3 = 3.0 ** 0.5

        def _radial_embedding(r):
            x = jnp.clip(r / R_MAX, 0.0, 1.0)
            centers = jnp.arange(NB, dtype=jnp.float32) / (NB - 1)
            sigma = 1.0 / (NB - 1)
            emb = jnp.exp(-0.5 * ((x[:, None] - centers[None, :]) / sigma) ** 2)
            emb = emb * NB ** 0.5 * (r <= R_MAX).astype(jnp.float32)[:, None]
            return emb
        f32 = jnp.float32
        rhat = edge_vec / (jnp.linalg.norm(edge_vec, axis=-1, keepdims=True) + 1e-12)
        Y1 = SQ3 * rhat
        emb = _radial_embedding(edge_length)
        h = jax.nn.silu(emb @ mlp_w0 + mlp_b0)
        h = jax.nn.silu(h @ mlp_w1 + mlp_b1)
        w = (h @ mlp_w2 + mlp_b2).reshape(-1, 4, MUL)
        s = node_feats[:, :MUL]
        v = node_feats[:, MUL:].reshape(-1, MUL, 3)
        xs = s @ W_up0 / f32(MUL) ** 0.5
        xv = jnp.einsum('nmc,mk->nkc', v, W_up1) / f32(MUL) ** 0.5
        ss = xs[senders]
        vv = xv[senders]
        m0 = w[:, 0] * ss
        m1 = w[:, 1][:, :, None] * ss[:, :, None] * Y1[:, None, :]
        m2 = w[:, 2][:, :, None] * vv
        m3 = w[:, 3] * (jnp.einsum('emc,ec->em', vv, Y1) / SQ3)
        mid_s = jnp.concatenate([m0, m3], axis=1)
        mid_v = jnp.concatenate([m1, m2], axis=1)
        msg_s = jax.ops.segment_sum(mid_s, receivers, num_segments=num_nodes)
        msg_v = jax.ops.segment_sum(mid_v, receivers, num_segments=num_nodes)
        out_s = msg_s @ W_out0 / f32(2 * MUL) ** 0.5
        out_v = jnp.einsum('nmc,mk->nkc', msg_v, W_out1) / f32(2 * MUL) ** 0.5
        out = jnp.concatenate([out_s, out_v.reshape(-1, 3 * MUL)], axis=1)
        return out / max(AVG, 1e-08)

    def _L3_gnn_ref(feat, W_src, b_src, W_dst, b_dst, W_v, b_v, src, dst):
        import jax, jax.numpy as jnp
        import numpy as np
        N_NODES = 6250
        N_EDGES = 100000
        IN_FEATS = 128
        HEADS = 4
        OUT_FEATS = 32
        NEG_SLOPE = 0.2

        def _edge_softmax(e, dst, n_nodes):
            seg_max = jax.ops.segment_max(e, dst, num_segments=n_nodes)
            ex = jnp.exp(e - seg_max[dst])
            seg_sum = jax.ops.segment_sum(ex, dst, num_segments=n_nodes)
            return ex / seg_sum[dst]
        n = feat.shape[0]
        f_src = (feat @ W_src.T + b_src).reshape(n, HEADS, OUT_FEATS)
        f_dst = (feat @ W_dst.T + b_dst).reshape(n, HEADS, OUT_FEATS)
        f_v = (feat @ W_v.T + b_v).reshape(n, HEADS, OUT_FEATS)
        a = f_src[src] + f_dst[dst]
        e = jnp.where(a >= 0, a, NEG_SLOPE * a)
        sa = _edge_softmax(e, dst, n)
        m = f_v[src] * sa
        rst = jax.ops.segment_sum(m, dst, num_segments=n)
        return rst.reshape(n, HEADS * OUT_FEATS)
    edge_index = jnp.stack([src, dst])
    x = _layernorm(x + _L0_gnn_ref(x, edge_index, L0_gnn_virt_h, L0_gnn_virt_edge_index, L0_gnn_Wq, L0_gnn_bq, L0_gnn_Wk, L0_gnn_bk, L0_gnn_Wv, L0_gnn_bv), axis=-1)
    x = _layernorm(x + _L1_gnn_ref(x, edge_index, edge_attr_64, L1_gnn_W1n, L1_gnn_b1n, L1_gnn_W2n, L1_gnn_b2n, L1_gnn_W1e, L1_gnn_b1e, L1_gnn_W2e, L1_gnn_b2e, L1_gnn_gin_eps, L1_gnn_rms_w), axis=-1)
    x = _layernorm(x + _L2_gnn_ref(x, edge_attr_3, edge_weight, src, dst, 6250, L2_gnn_W_up0, L2_gnn_W_up1, L2_gnn_mlp_w0, L2_gnn_mlp_b0, L2_gnn_mlp_w1, L2_gnn_mlp_b1, L2_gnn_mlp_w2, L2_gnn_mlp_b2, L2_gnn_W_out0, L2_gnn_W_out1), axis=-1)
    x = _layernorm(x + _L3_gnn_ref(x, L3_gnn_W_src, L3_gnn_b_src, L3_gnn_W_dst, L3_gnn_b_dst, L3_gnn_W_v, L3_gnn_b_v, src, dst), axis=-1)
    return x

_drawn_inputs = setup_inputs


def setup_inputs(seed=0):
    import zlib

    import numpy as np

    out = dict(_drawn_inputs(seed))
    spreads = {'L0_gnn_bq': (0.0, 0.291),
     'L0_gnn_bk': (0.0, 2.0),
     'L0_gnn_bv': (0.0, 0.1),
     'L1_gnn_b1n': (0.0, 1.422),
     'L1_gnn_b2n': (0.0, 0.488),
     'L1_gnn_b1e': (0.0, 2.0),
     'L1_gnn_b2e': (0.0, 2.0),
     'L1_gnn_rms_w': (1.0, 0.2),
     'L2_gnn_mlp_b0': (0.0, 0.749),
     'L2_gnn_mlp_b1': (0.0, 0.408),
     'L2_gnn_mlp_b2': (0.0, 0.294)}
    factors = {'edge_attr_64': 8.0,
     'L1_gnn_W1e': 8.0,
     'L1_gnn_W2e': 4.277,
     'L3_gnn_b_src': 64.0,
     'L3_gnn_b_dst': 64.0,
     'L3_gnn_b_v': 2.831}
    for name, (base, spread) in spreads.items():
        noise = np.random.default_rng([zlib.crc32(name.encode()), seed]).standard_normal(out[name].shape)
        drawn = base * np.exp(spread * noise) if base else spread * noise
        out[name] = jnp.asarray(drawn.astype(out[name].dtype))
    for name, factor in factors.items():
        out[name] = (out[name] * factor).astype(out[name].dtype)
    return out
```

```python
from contextlib import ExitStack

import concourse.bass as bass
from concourse import mybir

P = 128
N_NODES = 6250
N_EDGES = 106250
D = 128
N_TILES = -(-N_NODES // P)
N_CHUNKS = -(-N_EDGES // P)
GROUP = 4
SLOTS = 4
N_GROUPS = -(-(N_CHUNKS + N_TILES - 1) // (GROUP * SLOTS)) * SLOTS
N_ITEMS = GROUP * N_GROUPS
ITEM_TILES = -(-N_ITEMS // P)
ITEMS_PAD = ITEM_TILES * P
BLOCK = 7
N_BLOCKS = N_TILES // BLOCK
assert N_BLOCKS * BLOCK == N_TILES
FULL_TILES = N_NODES // P
REST = N_NODES - FULL_TILES * P
HEADS0, HDIM0 = 8, 16
ED = 64
MUL, NB, RH = 32, 8, 64
SQ3 = 3.0 ** 0.5
AVG = 16.0
FAR = 1 << 20
LOW = -3.0e38
LN_EPS = 1e-5
RMS_EPS = 1.1920929e-07

F32 = mybir.dt.float32
I32 = mybir.dt.int32
ALU = mybir.AluOpType
ACT = mybir.ActivationFunctionType
AX = mybir.AxisListType
DVE_ENGINE = mybir.EngineType.DVE
PE_ENGINE = mybir.EngineType.PE
SP_ENGINE = mybir.EngineType.SP
ds = bass.ds
CLIPPED = "the setup clips tiles and chunks to their tables"

W0 = 128 + HEADS0 + 1
W1 = 2 * D + 1
W2 = 256
W3 = 256
ACC_W = max(W0, W1, W2, W3)


class Counter:

    def __init__(self, sem, by=1):
        self.sem, self.by, self.at, self.per, self.round = sem, by, 0, 0, 0

    def did(self, instruction):
        instruction.then_inc(self.sem, self.by)
        self.at += self.by
        return self, self.at


def wait(engine, *marks):
    last = {}
    for counter, at in marks:
        last[counter] = max(at, last.get(counter, 0))
    for counter, at in last.items():
        engine.wait_ge(counter.sem, counter.round * counter.per + at)


def rounds(nc, counters, engines, n, body, ready):
    for c in counters:
        c.at = c.per = c.round = 0
    body(0)
    for c in counters:
        c.per = c.at
    with nc.Fori(1, n) as b:
        for c in counters:
            c.round, c.at = b, 0
        for e in engines:
            for c in counters:
                if c.per:
                    e.wait_ge(c.sem, b * c.per)
            e.wait_ge(ready, 1)
        body(b)
    for c in counters:
        assert c.at == c.per


class Phase(ExitStack):

    def __init__(self, nc, tag):
        super().__init__()
        self.nc, self.tag, self.sems = nc, tag, []

    def sb(self, name, shape, dt=F32):
        return self.enter_context(self.nc.sbuf_tensor(f"{self.tag}_{name}", shape, dt))

    def sem(self, name):
        self.sems.append(self.nc.alloc_semaphore(f"{self.tag}_{name}"))
        return self.sems[-1]

    def end(self):
        self.nc.all_engine_barrier()
        self.nc.clear_and_free_semaphores(self.sems)
        self.nc.all_engine_barrier()


class Group:

    def __init__(self, i, slot):
        self.i, self.slot, self.n = i, slot, i * SLOTS + slot
        self.r2 = slot % 2
        self.old = lambda k: not isinstance(self.n, int) or self.n >= k


def pipeline(nc, stages):
    depth = max(lag for lag, _ in stages)
    assert depth <= SLOTS

    def step(i, v):
        for lag, fn in stages:
            u = v - lag
            g = Group(i + u // SLOTS, u % SLOTS)
            if isinstance(g.n, int) and not 0 <= g.n < N_GROUPS:
                continue
            fn(g)

    for s in range(2 * SLOTS):
        step(s // SLOTS, s % SLOTS)
    with nc.Fori(2, N_GROUPS // SLOTS) as i:
        for v in range(SLOTS):
            step(i, v)
    for s in range(N_GROUPS, N_GROUPS + depth):
        step(s // SLOTS, s % SLOTS)


def build(nc, a):
    PE, V, A, G, SP = nc.tensor, nc.vector, nc.scalar, nc.gpsimd, nc.sync
    ENGINES = (PE, V, A, G, SP)
    root = ExitStack()

    def dram(name, shape, dt=F32):
        return nc.dram_tensor(name, shape, dt).ap()

    first_col = dram("dst_heads", [2, ITEMS_PAD], I32)
    item_rows = dram("item_rows", [2, ITEMS_PAD], I32)
    local_d = dram("local_d", [P, ITEMS_PAD])
    local_last_d = dram("local_last_d", [P, ITEMS_PAD])
    src_d = dram("src_d", [P, ITEMS_PAD], I32)
    rhat_d = dram("rhat_d", [P, ITEMS_PAD, 3])
    reset_d = dram("reset_d", [ITEMS_PAD // GROUP, GROUP * P])
    emb_d = dram("emb_d", [ITEMS_PAD // 2, NB, 2, P])
    kv_t = dram("kv_t", [N_TILES * P, 2 * D])
    x1_t = dram("x1_t", [N_TILES * P, D + 1])
    up_t = dram("up_t", [N_TILES * P, D])
    fs_t = dram("fs_t", [N_TILES * P, D])
    fsv_t = dram("fsv_t", [N_TILES * P, 2 * D])

    def by_tile(table):
        return table.rearrange("(t p) d -> p t d", p=P)

    def carry(engine, sem):
        engine.sem_inc(sem, 1)

    def sb(ctx, name, shape, dt=F32):
        return ctx.enter_context(nc.sbuf_tensor(name, shape, dt))

    x = sb(root, "x", [P, N_TILES, D])
    acc = sb(root, "acc", [P, N_TILES, ACC_W])
    ident = sb(root, "ident", [P, P])
    node_iota = sb(root, "node_iota", [P, P])
    ones_row = sb(root, "ones_row", [1, P])
    tile_of = sb(root, "tile_of", [1, ITEMS_PAD], I32)
    bank = [root.enter_context(nc.psum_tensor(f"bank{i}", [P, 512], F32)) for i in range(8)]

    def counters(ctx):
        return lambda name, by=1: Counter(ctx.sem(name), by)

    def setup():
        with Phase(nc, "set") as ctx:
            make = counters(ctx)
            pe, v, act, g = make("pe"), make("v"), make("act"), make("g")
            dma = lambda name: make(name, 16)
            d_x, d_head, d_items, d_out = dma("d_x"), dma("d_head"), dma("d_items"), dma("d_out")
            d_rows, d_tile = dma("d_rows"), dma("d_tile")

            m = g.did(G.memset(x[:, FULL_TILES, :], 0.0))
            wait(SP, m)
            d_x.did(SP.dma_start(x[:, 0:FULL_TILES, :],
                                 a["x"][0:FULL_TILES * P, :].rearrange("(t p) d -> p t d", p=P)))
            x_in = d_x.did(SP.dma_start(x[0:REST, FULL_TILES, :], a["x"][FULL_TILES * P:N_NODES, :]))

            heads = sb(ctx, "heads", [1, 2, N_CHUNKS], I32)
            with nc.allow_non_contiguous_dma(reason="first and last destination of each chunk"):
                d_head.did(SP.dma_start(heads[:, 0, :], a["dst_rows"][:, 1:2].rearrange("c a -> a c")))
                heads_in = d_head.did(SP.dma_start(heads[:, 1, :],
                                                   a["dst_rows"][:, P:P + 1].rearrange("c a -> a c")))

            iota_i = sb(ctx, "iota_i", [P, P], I32)
            item_i = sb(ctx, "item_i", [P, ITEM_TILES], I32)
            m1 = g.did(G.iota(iota_i[:], pattern=[[1, P]], base=0, channel_multiplier=0))
            m2 = g.did(G.iota(item_i[:], pattern=[[P, ITEM_TILES]], base=0, channel_multiplier=1))
            g.did(G.memset(ident[:], 0.0))
            m3 = g.did(G.memset(ones_row[:], 1.0))
            wait(G, m3)
            ident_ready = g.did(G.affine_select(out=ident[:], in_=ident[:], compare_op=ALU.not_equal, fill=1.0,
                                                base=0, pattern=[[-1, P]], channel_multiplier=1))
            item_no = sb(ctx, "item_no", [P, ITEM_TILES])
            wait(V, m1, m2)
            v.did(V.tensor_copy(node_iota[:], iota_i[:]))
            v.did(V.tensor_copy(item_no[:], item_i[:]))

            tiles_i = sb(ctx, "tiles_i", [1, 2, N_CHUNKS], I32)
            tiles = sb(ctx, "tiles", [1, 2, N_CHUNKS])
            row = sb(ctx, "row", [1, 4, N_CHUNKS])
            wait(V, heads_in)
            m = v.did(V.tensor_scalar(tiles_i[:], heads[:], 7, None, ALU.arith_shift_right))
            wait(V, m)
            m = v.did(V.tensor_copy(tiles[:], tiles_i[:]))
            wait(V, m)
            m = v.did(V.tensor_scalar(row[:, 0, :], tiles[:, 1, :], float(N_TILES - 1), 1.0, ALU.min, ALU.add))
            wait(V, m)
            m = v.did(V.tensor_tensor(row[:, 0, :], row[:, 0, :], tiles[:, 0, :], ALU.subtract))
            m0 = v.did(V.memset(row[:, 1, :], 0.0))
            wait(V, m, m0)
            m = v.did(V.tensor_tensor_scan(row[:, 2, :], row[:, 1, :], row[:, 0, :], 0.0, ALU.add, ALU.add))
            wait(V, m)
            m = v.did(V.tensor_tensor(row[:, 1, :], row[:, 2, :], row[:, 0, :], ALU.subtract))
            wait(V, m)
            m = v.did(V.tensor_tensor(row[:, 2, :], tiles[:, 0, :], row[:, 1, :], ALU.subtract))
            wait(V, m)
            m0 = v.did(V.tensor_copy(row[:, 3, 0:1], row[:, 2, 0:1]))
            m = v.did(V.tensor_tensor(row[:, 3, 1:], row[:, 2, 1:], row[:, 2, 0:N_CHUNKS - 1], ALU.subtract))

            before = sb(ctx, "before", [P, N_CHUNKS])
            jump = sb(ctx, "jump", [P, N_CHUNKS])
            wait(PE, ident_ready, m0, m)
            for k, (r, lo) in enumerate([(1, 0), (1, 512), (3, 0), (3, 512)]):
                hi = min(lo + 512, N_CHUNKS)
                m = pe.did(PE.matmul(bank[k][:, 0:hi - lo], ones_row[:], row[:, r, lo:hi], start=True, stop=True))
                wait(V, m)
                to = before if r == 1 else jump
                m_rows = v.did(V.tensor_copy(to[:, lo:hi], bank[k][:, 0:hi - lo]))
            hit = sb(ctx, "hit", [P, 2, N_CHUNKS])
            found = sb(ctx, "found", [P, 2, ITEM_TILES])
            for q in range(ITEM_TILES):
                wait(V, m_rows)
                ma = v.did(V.tensor_scalar(hit[:, 0, :], before[:], item_no[:, q:q + 1], None, ALU.is_le))
                mb = v.did(V.scalar_tensor_tensor(out=hit[:, 1, :], in0=before[:], scalar=item_no[:, q:q + 1],
                                                  in1=jump[:], op0=ALU.is_le, op1=ALU.mult))
                wait(V, ma, mb)
                m_rows = v.did(V.tensor_reduce(found[:, :, q:q + 1], hit[:], AX.X, ALU.add))
            chunk = sb(ctx, "chunk", [P, ITEM_TILES])
            tile = sb(ctx, "tile", [P, ITEM_TILES])
            item_tab = sb(ctx, "item_tab", [P, 2, ITEM_TILES], I32)
            wait(V, m_rows)
            ma = v.did(V.tensor_scalar(chunk[:], found[:, 0, :], -1.0, None, ALU.add))
            mb = v.did(V.tensor_tensor(tile[:], found[:, 1, :], item_no[:], ALU.add))
            wait(V, ma, mb)
            v.did(V.tensor_copy(item_tab[:, 1, :], chunk[:]))
            v.did(V.tensor_scalar(item_tab[:, 0, :], tile[:], float(N_TILES - 1), None, ALU.min))
            tile_base = sb(ctx, "tile_base", [P, ITEM_TILES])
            m_tab = v.did(V.tensor_scalar(tile_base[:], tile[:], float(P), None, ALU.mult))
            wait(SP, m_tab)
            with nc.allow_non_contiguous_dma(reason="a small table, once"):
                d_tile.did(SP.dma_start(item_rows[0, :].rearrange("(q p) -> p q", p=P), item_tab[:, 0, :]))
                m = d_tile.did(SP.dma_start(item_rows[1, :].rearrange("(q p) -> p q", p=P), item_tab[:, 1, :]))
            wait(SP, m)
            tile_in = d_rows.did(SP.dma_start(tile_of[:], item_rows[0:1, :]))

            dst_i = sb(ctx, "dst_i", [P, ITEM_TILES, P + 2], I32)
            src_i = sb(ctx, "src_i", [P, ITEM_TILES, P], I32)
            vec = sb(ctx, "vec", [P, ITEM_TILES, 3 * P])
            length = sb(ctx, "length", [P, ITEM_TILES, P])
            wait(G, m_tab)
            for q in range(ITEM_TILES):
                at = bass.IndirectOffsetOnAxis(ap=item_tab[:, 1, q:q + 1], axis=0)
                for to, table in ((dst_i, a["dst_rows"]), (src_i, a["src_rows"]), (vec, a["vec_rows"]),
                                  (length, a["length_rows"])):
                    rows_in = d_items.did(G.indirect_dma_start(out=to[:, q, :], out_offset=None, in_=table,
                                                               in_offset=at))
            dst = sb(ctx, "dst", [P, ITEM_TILES, P + 2])
            spare = acc[:].rearrange("p t d -> p (t d)")
            by_item = spare[:, 0:6 * ITEMS_PAD].rearrange("p (k q e) -> p k q e", k=6, q=ITEM_TILES)
            assert (6 + NB) * ITEMS_PAD <= N_TILES * ACC_W
            reset = sb(ctx, "reset", [P, ITEM_TILES, P])
            tmp = sb(ctx, "tmp", [P, 2, ITEM_TILES, P])
            wait(V, rows_in)
            v.did(V.tensor_copy(by_item[:, 2], src_i[:]))
            m = v.did(V.tensor_copy(dst[:], dst_i[:]))
            wait(V, m)
            for q in range(ITEM_TILES):
                m = v.did(V.tensor_scalar(by_item[:, 0, q, :], dst[:, q, 1:P + 1], tile_base[:, q:q + 1], None,
                                          ALU.subtract))
            mb = v.did(V.tensor_tensor(reset[:], dst[:, :, 1:P + 1], dst[:, :, 0:P], ALU.not_equal))
            mc = v.did(V.tensor_tensor(tmp[:, 0], dst[:, :, 1:P + 1], dst[:, :, 2:P + 2], ALU.not_equal))
            wait(V, m, mb, mc)
            m_reset = v.did(V.tensor_scalar(reset[:], reset[:], LOW, None, ALU.mult))
            m = v.did(V.scalar_tensor_tensor(out=tmp[:, 1], in0=by_item[:, 0], scalar=1.0, in1=tmp[:, 0],
                                             op0=ALU.add, op1=ALU.mult))
            wait(V, m)
            m = v.did(V.tensor_scalar(by_item[:, 1], tmp[:, 1], -1.0, None, ALU.add))
            part = vec[:].rearrange("p q (c e) -> p q c e", c=3)
            wait(V, m)
            m = v.did(V.tensor_tensor(tmp[:, 0], part[:, :, 0, :], part[:, :, 0, :], ALU.mult))
            for c in (1, 2):
                mb = v.did(V.tensor_tensor(tmp[:, 1], part[:, :, c, :], part[:, :, c, :], ALU.mult))
                wait(V, m, mb)
                m = v.did(V.tensor_tensor(tmp[:, 0], tmp[:, 0], tmp[:, 1], ALU.add))
                wait(V, m)
            wait(A, m)
            m = act.did(A.activation(tmp[:, 1], tmp[:, 0], ACT.Sqrt))
            wait(V, m)
            m = v.did(V.tensor_scalar(tmp[:, 0], tmp[:, 1], 1e-12, None, ALU.add))
            wait(V, m)
            m = v.did(V.reciprocal(tmp[:, 1], tmp[:, 0]))
            wait(V, m)
            for c in range(3):
                m = v.did(V.tensor_tensor(by_item[:, 3 + c], part[:, :, c, :], tmp[:, 1], ALU.mult))

            wait(SP, m_reset)
            d_out.did(SP.dma_start(reset_d.rearrange("g (i e) -> (g i) e", i=GROUP)
                                   .rearrange("(q p) e -> p q e", p=P), reset[:]))

            table_f = [sb(ctx, f"table{k}", [P, ITEMS_PAD]) for k in range(2)]
            table_src = sb(ctx, "table_src", [P, ITEMS_PAD], I32)
            table_r = sb(ctx, "table_r", [P, ITEMS_PAD, 3])
            wait(PE, m)
            copies = []
            for n in range(6 * ITEM_TILES):
                k, q = n // ITEM_TILES, n % ITEM_TILES
                if n >= 8:
                    wait(PE, copies[n - 8])
                m = pe.did(PE.transpose(bank[n % 8][:, 0:P], by_item[:, k, q, :], ident[:]))
                to = (table_f + [table_src])[k][:, q * P:(q + 1) * P] if k < 3 else \
                    table_r[:, q * P:(q + 1) * P, k - 3]
                e, c = ((A, act), (V, v))[n % 2]
                wait(e, m)
                copies.append(c.did(e.tensor_copy(to, bank[n % 8][:, 0:P]) if e is V
                                    else e.activation(to, bank[n % 8][:, 0:P], ACT.Copy)))
            wait(SP, *copies)
            for to, of in ((local_d, table_f[0]), (local_last_d, table_f[1]), (src_d, table_src),
                           (rhat_d, table_r)):
                d_out.did(SP.dma_start(to, of[:]))

            clipped = sb(ctx, "clipped", [P, ITEM_TILES, P])
            inside = sb(ctx, "inside", [P, ITEM_TILES, P])
            emb = spare[:, 6 * ITEMS_PAD:(6 + NB) * ITEMS_PAD].rearrange("p (q j e) -> p q j e", q=ITEM_TILES, j=NB)
            mb = v.did(V.tensor_scalar(clipped[:], length[:], 0.0, 1.0, ALU.max, ALU.min))
            m = v.did(V.tensor_scalar(inside[:], length[:], 1.0, NB ** 0.5, ALU.is_le, ALU.mult))
            wait(V, mb, m)
            for j in range(NB):
                m = v.did(V.tensor_scalar(tmp[:, 0], clipped[:], float(NB - 1), float(-j), ALU.mult, ALU.add))
                wait(A, m)
                m = act.did(A.activation(tmp[:, 1], tmp[:, 0], ACT.Square))
                wait(A, m)
                m = act.did(A.activation(tmp[:, 1], tmp[:, 1], ACT.Exp, scale=-0.5))
                wait(V, m)
                m = v.did(V.tensor_tensor(emb[:, :, j, :], tmp[:, 1], inside[:], ALU.mult))
                wait(V, m)
            wait(SP, m)
            half = P // 2
            for q in range(ITEM_TILES):
                for b in range(2):
                    d_out.did(SP.dma_start(emb_d[q * half:(q + 1) * half, :, b, :], emb[b::2, q, :, :]))
            last = (d_out, d_out.at)
            for e in ENGINES:
                wait(e, last, x_in, tile_in)
            ctx.end()

    def node_phase(tag, body, weights=()):
        with Phase(nc, tag) as ctx:
            k = NodePhase(ctx)
            k.load(weights(ctx, k) if weights else [])
            body_fn = body(ctx, k)
            V.memset(k.small[:], 0.0).then_inc(k.ready, 1)
            V.wait_ge(k.ready, 1)
            rounds(nc, k.all, (PE, V, A), N_BLOCKS, body_fn, k.ready)
            for e in ENGINES:
                for c in k.all:
                    e.wait_ge(c.sem, c.per * N_BLOCKS)
            ctx.end()

    class NodePhase:

        def __init__(self, ctx):
            self.ctx, self.sb, self.ready = ctx, ctx.sb, ctx.sem("ready")
            self.s_carry = ctx.sem("carry")
            make = counters(ctx)
            self.pe, self.v, self.act = make("pe"), make("v"), make("act")
            self.out = make("out", 16)
            self.w = make("w", 16)
            self.prep = make("prep")
            self.all = [self.pe, self.v, self.act, self.out]
            self.small = ctx.sb("small", [P, 4, BLOCK])
            self.square = ctx.sb("square", [P, BLOCK, D])

        def load(self, pairs):
            for to, of in pairs:
                self.w.did(SP.dma_start(to, of))
            if pairs:
                for e in ENGINES:
                    wait(e, (self.w, self.w.at))

        def prepare(self, engine, instruction):
            wait(engine, self.prep.did(instruction))

        def prepared(self):
            for e in ENGINES:
                wait(e, (self.prep, self.prep.at))


        def transpose(self, of, to, ready, banks):
            wait(PE, *ready)
            done = []
            for n, (lo, hi) in enumerate(((0, 4), (4, BLOCK))):
                for j in range(lo, hi):
                    m = PE.transpose(bank[banks[n]][:, (j - lo) * P:(j - lo + 1) * P], of[:, j, :], ident[:])
                m = self.pe.did(m)
                wait(A, m)
                done.append(self.act.did(A.activation(
                    to[:, lo:hi, :], bank[banks[n]][:, 0:(hi - lo) * P].rearrange("p (t d) -> p t d", d=P),
                    ACT.Copy)))
            return done

        def project(self, pairs, ready, banks):
            wait(PE, *ready)
            out = []
            for n, (lo, hi) in enumerate(((0, 4), (4, BLOCK))):
                for j in range(lo, hi):
                    for k, (xt, w) in enumerate(pairs):
                        m = PE.matmul(bank[banks[n]][:, (j - lo) * P:(j - lo + 1) * P], xt[:, j, :], w,
                                      start=(k == 0), stop=(k == len(pairs) - 1))
                out.append((slice(lo, hi), bank[banks[n]][:, 0:(hi - lo) * P].rearrange("p (t d) -> p t d", d=P),
                            self.pe.did(m)))
            return out

        def moment(self, of, ready, eps, col):
            wait(A, *ready)
            m = self.act.did(A.activation(self.square[:], of, ACT.Square))
            wait(V, m)
            m = self.v.did(V.tensor_reduce(self.small[:, col, :], self.square[:], AX.X, ALU.add))
            wait(V, m)
            m = self.v.did(V.tensor_scalar(self.small[:, col, :], self.small[:, col, :], 1.0 / D, eps,
                                           ALU.mult, ALU.add))
            wait(A, m)
            m = self.act.did(A.activation(self.small[:, 3, :], self.small[:, col, :], ACT.Sqrt))
            wait(V, m)
            m = self.v.did(V.reciprocal(self.small[:, col, :], self.small[:, 3, :]))
            return m

        def layernorm(self, z, to, ready):
            wait(V, *ready)
            m = self.v.did(V.tensor_reduce(self.small[:, 0, :], z, AX.X, ALU.add))
            wait(V, m)
            m = self.v.did(V.tensor_scalar(self.small[:, 0, :], self.small[:, 0, :], 1.0 / D, None, ALU.mult))
            wait(V, m)
            m = self.v.did(V.tensor_tensor(z, z, spread(self.small[:, 0, :]), ALU.subtract))
            m = self.moment(z, [m], LN_EPS, 1)
            wait(V, m)
            return self.v.did(V.tensor_tensor(to, z, spread(self.small[:, 1, :]), ALU.mult))

    def spread(col, width=D):
        return col.unsqueeze(2).to_broadcast([P, col.shape[1], width])

    def tiles_of(row):
        return row.unsqueeze(1).to_broadcast([P, BLOCK, row.shape[1]])

    def vec_row(v):
        return v.rearrange("(a n) -> a n", a=1).to_broadcast([P, v.shape[0]])

    def vec_col(v):
        return v.rearrange("(n a) -> n a", a=1)

    def project0(queries):
        def weights(ctx, k):
            k.wqkv, k.bqkv = k.sb("w3", [P, 3 * D]), k.sb("b3", [P, 3 * D])
            pairs = []
            for n, name in enumerate(("k", "v", "q")):
                pairs.append((k.wqkv[:, n * D:(n + 1) * D], a[f"L0_gnn_W{name}"]))
                pairs.append((k.bqkv[:, n * D:(n + 1) * D], vec_row(a[f"L0_gnn_b{name}"])))
            return pairs

        def make(ctx, k):
            xin, xt, kv = k.sb("xin", [P, BLOCK, D]), k.sb("xt", [P, BLOCK, D]), k.sb("kv", [P, BLOCK, 2 * D])

            def body(b):
                own = ds(b * BLOCK, BLOCK)
                m = k.act.did(A.activation(xin[:], x[:, own, :], ACT.Copy))
                ready = k.transpose(xin, xt, [m], (0, 1))
                done = project3(k, xt, ready, k.wqkv, k.bqkv, kv, queries[:, own, :])
                wait(SP, *done)
                k.out.did(SP.dma_start(by_tile(kv_t)[:, own, :], kv[:]))
            return body
        node_phase("proj0", make, weights)

    def project3(k, xt, ready, w, bias, first, rest):
        wait(PE, *ready)
        done = []
        for j in range(BLOCK):
            b = 2 + j % 6
            if j >= 6:
                wait(PE, done[2 * (j - 6) + 1])
            m = k.pe.did(PE.matmul(bank[b][:, 0:3 * D], xt[:, j, :], w[:], start=True, stop=True))
            wait(V, m)
            done.append(k.v.did(V.tensor_tensor(first[:, j, :], bank[b][:, 0:2 * D], bias[:, 0:2 * D], ALU.add)))
            done.append(k.v.did(V.tensor_tensor(rest[:, j, :], bank[b][:, 2 * D:3 * D], bias[:, 2 * D:3 * D],
                                                ALU.add)))
        return done

    def after0(inv_root_deg):
        def make(ctx, k):
            z, t1 = k.sb("z", [P, BLOCK, D]), k.sb("t1", [P, BLOCK, D + 1])
            zs = k.sb("zs", [P, 2, BLOCK, HEADS0])

            def body(b):
                own = ds(b * BLOCK, BLOCK)
                m = k.v.did(V.tensor_scalar(zs[:, 0], acc[:, own, D:D + HEADS0], 1e-6, None, ALU.add))
                mb = k.v.did(V.tensor_scalar(k.small[:, 2, :], acc[:, own, D + HEADS0], 1.0, None, ALU.max))
                wait(A, mb)
                ma = k.act.did(A.activation(k.small[:, 3, :], k.small[:, 2, :], ACT.Sqrt))
                wait(V, m, ma)
                m = k.v.did(V.reciprocal(zs[:, 1], zs[:, 0]))
                mr = k.v.did(V.reciprocal(k.small[:, 2, :], k.small[:, 3, :]))
                wait(V, m, mr)
                mi = k.v.did(V.tensor_copy(inv_root_deg[:, own], k.small[:, 2, :]))
                for j in range(BLOCK):
                    m = k.v.did(V.tensor_tensor(
                        z[:, j, :].rearrange("p (h c) -> p h c", h=HEADS0),
                        acc[:, ds(b * BLOCK + j, 1), 0:D].rearrange("p a (h c) -> p (a h) c", h=HEADS0),
                        spread(zs[:, 1, j, :], HDIM0), ALU.mult))
                wait(V, m, mi)
                m = k.v.did(V.tensor_tensor(z[:], z[:], x[:, own, :], ALU.add))
                m = k.layernorm(z[:], x[:, own, :], [m])
                wait(V, m)
                k.v.did(V.tensor_tensor(t1[:, :, 0:D], x[:, own, :], spread(k.small[:, 2, :]), ALU.mult))
                m = k.v.did(V.tensor_copy(t1[:, :, D:D + 1], k.small[:, 2, :].unsqueeze(2)))
                wait(SP, m)
                k.out.did(SP.dma_start(by_tile(x1_t)[:, own, :], t1[:]))
            return body
        node_phase("after0", make)

    def after1(inv_root_deg):
        def weights(ctx, k):
            k.w2e, k.w1n, k.w2n, k.up = (k.sb(n, [P, D]) for n in ("w2e", "w1n", "w2n", "up"))
            k.b2e, k.b2n, k.rms = (k.sb(n, [P, D]) for n in ("b2e", "b2n", "rms"))
            k.b1n, k.eps = k.sb("b1n", [P, 1]), k.sb("eps", [P, 1])
            k.prepare(G, G.memset(k.up[:], 0.0))
            k.prepared()
            pairs = [(k.w2e[:], a["L1_gnn_W2e"]), (k.w1n[:], a["L1_gnn_W1n"]), (k.w2n[:], a["L1_gnn_W2n"]),
                     (k.b2e[:], vec_row(a["L1_gnn_b2e"])), (k.b2n[:], vec_row(a["L1_gnn_b2n"])),
                     (k.rms[:], vec_row(a["L1_gnn_rms_w"])), (k.b1n[:], vec_col(a["L1_gnn_b1n"])),
                     (k.eps[:], a["gin_eps"].to_broadcast([P, 1])),
                     (k.up[0:MUL, 0:MUL], a["L2_gnn_W_up0"])]
            pairs += [(k.up[MUL + c:P:3, MUL + MUL * c:2 * MUL + MUL * c], a["L2_gnn_W_up1"]) for c in range(3)]
            return pairs

        def make(ctx, k):
            k.prepare(V, V.tensor_scalar(k.up[:], k.up[:], MUL ** -0.5, None, ALU.mult))
            k.prepare(V, V.tensor_scalar(k.eps[:], k.eps[:], 1.0, None, ALU.add))
            k.prepared()
            h, ht, z, t2, x1 = (k.sb(n, [P, BLOCK, D]) for n in ("h", "ht", "z", "t2", "x1"))

            def body(b):
                own = ds(b * BLOCK, BLOCK)
                m = k.act.did(A.activation(h[:], acc[:, own, D + 1:W1], ACT.Copy))
                mx = k.act.did(A.activation(x1[:], x[:, own, :], ACT.Copy))
                mb = k.v.did(V.tensor_copy(k.small[:, 2, :], acc[:, own, D]))
                ready = k.transpose(h, ht, [m], (0, 1))
                wait(V, mb)
                for j in range(BLOCK):
                    m = k.v.did(V.tensor_scalar(z[:, j, :], k.b2e[:], k.small[:, 2, j:j + 1], None, ALU.mult))
                wait(V, m)
                m = k.v.did(V.tensor_tensor(z[:], z[:], acc[:, own, 0:D], ALU.add))
                for part, ps, done in k.project([(ht, k.w2e[:])], ready, (2, 3)):
                    wait(V, m, done)
                    ms = k.v.did(V.tensor_tensor(z[:, part, :], z[:, part, :], ps, ALU.add))
                wait(V, ms)
                m = k.v.did(V.tensor_tensor(z[:], z[:], spread(inv_root_deg[:, own]), ALU.mult))
                wait(V, m, mx)
                m = k.v.did(V.scalar_tensor_tensor(out=h[:], in0=x1[:], scalar=k.eps[:], in1=z[:],
                                                   op0=ALU.mult, op1=ALU.add))
                ready = k.transpose(h, ht, [m], (0, 1))
                wait(PE, *ready)
                hid = []
                for n, (lo, hi) in enumerate(((0, 4), (4, BLOCK))):
                    m = k.pe.did(PE.matmul(bank[4 + n][:, 0:(hi - lo) * P], k.w1n[:],
                                           ht[:, lo:hi, :].rearrange("p t d -> p (t d)"), start=True, stop=True))
                    wait(A, m)
                    hid.append(k.act.did(A.activation(h[:, lo:hi, :].rearrange("p t d -> p (t d)"),
                                                      bank[4 + n][:, 0:(hi - lo) * P], ACT.Relu, bias=k.b1n[:])))
                m = None
                for part, ps, done in k.project([(h, k.w2n[:])], hid, (2, 3)):
                    wait(V, done)
                    ms = k.v.did(V.tensor_tensor(z[:, part, :], ps, x1[:, part, :], ALU.add))
                wait(V, ms)
                m = k.v.did(V.tensor_tensor(z[:], z[:], tiles_of(k.b2n[:]), ALU.add))
                m = k.moment(z[:], [m], RMS_EPS, 2)
                wait(V, m)
                m = k.v.did(V.tensor_tensor(z[:], z[:], spread(k.small[:, 2, :]), ALU.mult))
                wait(V, m)
                m = k.v.did(V.tensor_tensor(z[:], z[:], tiles_of(k.rms[:]), ALU.mult))
                wait(V, m)
                m = k.v.did(V.tensor_tensor(z[:], z[:], x1[:], ALU.add))
                m = k.layernorm(z[:], h[:], [m])
                wait(A, m)
                carry(A, k.s_carry)
                mx = k.act.did(A.activation(x[:, own, :], h[:], ACT.Copy))
                ready = k.transpose(h, ht, [m], (0, 1))
                out = []
                for part, ps, done in k.project([(ht, k.up[:])], ready, (2, 3)):
                    wait(V, done)
                    out.append(k.v.did(V.tensor_copy(t2[:, part, :], ps)))
                wait(SP, *out)
                k.out.did(SP.dma_start(by_tile(up_t)[:, own, :], t2[:]))
            return body
        node_phase("after1", make, weights)

    def after2(at_dst):
        def weights(ctx, k):
            k.raw = k.sb("raw", [P, 2, MUL])
            k.wo = k.sb("wo", [P, 2, D])
            k.w3, k.b3 = k.sb("w3", [P, 3 * D]), k.sb("b3", [P, 3 * D])
            k.prepare(G, G.memset(k.wo[:], 0.0))
            k.prepare(G, G.memset(k.raw[:], 0.0))
            k.prepared()
            pairs = [(k.raw[0:2 * MUL, 0, :], a["L2_gnn_W_out0"]), (k.raw[2 * MUL:P, 0, :], a["L2_gnn_W_out1"]),
                     (k.raw[0:2 * MUL, 1, :], a["L2_gnn_W_out1"]), (k.raw[2 * MUL:P, 1, :], a["L2_gnn_W_out1"])]
            for n, name in enumerate(("src", "v", "dst")):
                pairs.append((k.w3[:, n * D:(n + 1) * D], a[f"W_{name}_t"]))
                pairs.append((k.b3[:, n * D:(n + 1) * D], vec_row(a[f"L3_gnn_b_{name}"])))
            return pairs

        def make(ctx, k):
            scale = (2 * MUL) ** -0.5 / AVG
            k.prepare(V, V.tensor_scalar(k.wo[0:2 * MUL, 0, 0:MUL], k.raw[0:2 * MUL, 0, :], scale, None, ALU.mult))
            for c, (lo, half) in enumerate(((2 * MUL, 0), (0, 1), (2 * MUL, 1))):
                for row, factor in ((lo, scale * SQ3), (lo + MUL, scale)):
                    k.prepare(V, V.tensor_scalar(k.wo[row:row + MUL, half, MUL + c:P:3],
                                                 k.raw[row:row + MUL, half, :], factor, None, ALU.mult))
            k.prepared()
            h, ht, ht2, z, xt = (k.sb(n, [P, BLOCK, D]) for n in ("h", "ht", "ht2", "z", "xt"))
            t3 = k.sb("t3", [P, BLOCK, 2 * D])

            def body(b):
                own = ds(b * BLOCK, BLOCK)
                m = k.act.did(A.activation(h[:], acc[:, own, 0:D], ACT.Copy))
                mb = k.act.did(A.activation(z[:], acc[:, own, D:2 * D], ACT.Copy))
                ready = k.transpose(h, ht, [m], (0, 1)) + k.transpose(z, ht2, [mb], (2, 3))
                for part, ps, done in k.project([(ht, k.wo[:, 0, :]), (ht2, k.wo[:, 1, :])], ready, (4, 5)):
                    wait(V, done)
                    m = k.v.did(V.tensor_tensor(z[:, part, :], ps, x[:, ds(b * BLOCK + part.start,
                                                                         part.stop - part.start), :], ALU.add))
                m = k.layernorm(z[:], h[:], [m])
                wait(A, m)
                carry(A, k.s_carry)
                k.act.did(A.activation(x[:, own, :], h[:], ACT.Copy))
                ready = k.transpose(h, xt, [m], (0, 1))
                done = project3(k, xt, ready, k.w3, k.b3, t3, at_dst[:, own, 0:D])
                wait(SP, *done)
                k.out.did(SP.dma_start(by_tile(fsv_t)[:, own, :], t3[:]))
                k.out.did(SP.dma_start(by_tile(fs_t)[:, own, :], t3[:, :, 0:D]))
            return body
        node_phase("after2", make, weights)

    def maxima(at_dst):
        def make(ctx, k):
            s, r = k.sb("s", [P, BLOCK, D]), k.sb("r", [P, BLOCK, D])

            def body(b):
                own = ds(b * BLOCK, BLOCK)
                m = k.v.did(V.tensor_tensor(s[:], acc[:, own, 0:D], at_dst[:, own, 0:D], ALU.add))
                wait(A, m)
                m = k.act.did(A.activation(r[:], s[:], ACT.Relu, scale=0.8))
                wait(V, m)
                k.v.did(V.scalar_tensor_tensor(out=at_dst[:, own, D:2 * D], in0=s[:], scalar=0.2, in1=r[:],
                                               op0=ALU.mult, op1=ALU.add))
            return body
        node_phase("maxima", make)

    def after3():
        def make(ctx, k):
            z, s, y = (k.sb(n, [P, BLOCK, D]) for n in ("z", "s", "y"))

            def body(b):
                own = ds(b * BLOCK, BLOCK)
                m = k.v.did(V.tensor_scalar(s[:], acc[:, own, D:2 * D], 1e-30, None, ALU.max))
                wait(V, m)
                m = k.v.did(V.reciprocal(z[:], s[:]))
                wait(V, m)
                m = k.v.did(V.tensor_tensor(z[:], z[:], acc[:, own, 0:D], ALU.mult))
                wait(V, m)
                m = k.v.did(V.tensor_tensor(z[:], z[:], x[:, own, :], ALU.add))
                m = k.layernorm(z[:], y[:], [m])
                wait(A, m)
                carry(A, k.s_carry)
                k.act.did(A.activation(x[:, own, :], y[:], ACT.Copy))
            return body
        node_phase("after3", make)
        with nc.semaphore("written") as written:
            SP.dma_start(a["out"][0:FULL_TILES * P, :].rearrange("(t p) d -> p t d", p=P),
                         x[:, 0:FULL_TILES, :]).then_inc(written, 16)
            SP.dma_start(a["out"][FULL_TILES * P:N_NODES, :], x[0:REST, FULL_TILES, :]).then_inc(written, 16)
            SP.wait_ge(written, 32)

    class EdgePass:

        def __init__(self, ctx, table, width, sums, local, fixed=()):
            self.ctx, self.sb, self.sem, self.table, self.sums = ctx, ctx.sb, ctx.sem, table, sums
            self.src = self.sb("src", [P, N_ITEMS], I32)
            self.local = self.sb("local", [P, N_ITEMS])
            self.index = self.sb("index", [P, SLOTS, GROUP], I32)
            self.rows = self.sb("rows", [P, SLOTS, GROUP, width])
            self.sel = self.sb("sel", [P, SLOTS, GROUP, P])
            self.s_index = [self.sem(f"index{u}") for u in range(SLOTS)]
            self.s_rows = [self.sem(f"rows{u}") for u in range(SLOTS)]
            self.s_sel = self.sem("sel")
            self.s_sums = self.sem("sums")
            self.s_added = self.sem("added")
            self.s_load = self.sem("load")
            self.s_carry = self.sem("carry")
            self.loads = 0
            self.zeroed = self.sem("zeroed")
            self.load([(self.src[:], src_d[:, 0:N_ITEMS]), (self.local[:], local[:, 0:N_ITEMS])] + list(fixed))
            G.memset(acc[:, :, 0:sums], 0.0).then_inc(self.zeroed, 1)
            V.wait_ge(self.zeroed, 1)

        def load(self, pairs):
            for to, of in pairs:
                SP.dma_start(to, of).then_inc(self.s_load, 16)
                self.loads += 16
            for e in ENGINES:
                e.wait_ge(self.s_load, self.loads)

        def gather(self, g, s_free, per=1):
            u = g.slot
            if g.old(SLOTS):
                SP.wait_ge(self.s_rows[u], g.i * 64)
            SP.dma_start(self.index[:, u, :], self.src[:, ds(g.n * GROUP, GROUP)]).then_inc(self.s_index[u], 16)
            G.wait_ge(self.s_index[u], (g.i + 1) * 16)
            if g.old(SLOTS):
                G.wait_ge(s_free, (g.n - (SLOTS - 1)) * per)
            carry(G, self.s_carry)
            for i in range(GROUP):
                G.indirect_dma_start(out=self.rows[:, u, i, :], out_offset=None, in_=self.table,
                                     in_offset=bass.IndirectOffsetOnAxis(ap=self.index[:, u, i:i + 1], axis=0)
                                     ).then_inc(self.s_rows[u], 16)

        def have_rows(self, engine, g):
            engine.wait_ge(self.s_rows[g.slot], (g.i + 1) * 64)

        def select(self, g):
            if g.old(SLOTS):
                V.wait_ge(self.s_sums, (g.n - (SLOTS - 1)) * GROUP)
            for i in range(GROUP):
                m = V.tensor_scalar(self.sel[:, g.slot, i, :], node_iota[:],
                                    self.local[:, ds(g.n * GROUP + i, 1)], None, ALU.is_equal)
            m.then_inc(self.s_sel, 1)

        def scatter(self, g, parts):
            for i in range(GROUP):
                if g.old(1):
                    PE.wait_ge(self.s_added, (g.n - 1) * GROUP + i + 1)
                for at, rows in parts(i):
                    m = PE.matmul(bank[i][:, at:at + rows.shape[1]], self.sel[:, g.slot, i, :], rows,
                                  start=True, stop=True)
                m.then_inc(self.s_sums, 1)

        def add(self, g):
            tiles = self.tiles(g, DVE_ENGINE)
            for i in range(GROUP):
                V.wait_ge(self.s_sums, g.n * GROUP + i + 1)
                if i or g.old(1):
                    V.wait_ge(self.s_added, g.n * GROUP + i)
                to = acc[:, ds(tiles[i], 1), 0:self.sums]
                V.tensor_tensor(to, to, bank[i][:, 0:self.sums].unsqueeze(1), ALU.add).then_inc(self.s_added, 1)

        def tiles(self, g, engine):
            _, tiles = nc.values_load_multi_w_load_instructions(
                tile_of[0:1, ds(g.n * GROUP, GROUP)], engines=(engine,), min_val=0, max_val=N_TILES - 1,
                skip_runtime_bounds_check_because=CLIPPED)
            return tiles

        def run(self, stages):
            pipeline(nc, stages)
            for e in ENGINES:
                e.wait_ge(self.s_added, N_ITEMS)
            self.ctx.end()

    class Turned:

        def __init__(self, ps, n_bank):
            self.ps, self.bank = ps, n_bank
            self.sel_t = ps.sb("sel_t", [P, 2, GROUP, P])
            self.s_t = ps.sem("t")
            self.s_copied = ps.sem("copied")

        def turn(self, g, s_used):
            PE.wait_ge(self.ps.s_sel, g.n + 1)
            if g.old(1):
                PE.wait_ge(self.s_copied, g.n)
            for i in range(GROUP):
                m = PE.transpose(bank[self.bank][:, i * P:(i + 1) * P], self.ps.sel[:, g.slot, i, :], ident[:])
            m.then_inc(self.s_t, 1)
            A.wait_ge(self.s_t, g.n + 1)
            if g.old(2):
                A.wait_ge(s_used, g.n - 1)
            A.activation(self.sel_t[:, g.r2].rearrange("p i e -> p (i e)"), bank[self.bank][:], ACT.Copy
                         ).then_inc(self.s_copied, 1)

    def quad(b, width=P):
        return bank[b][:, 0:GROUP * width].rearrange("p (i d) -> p i d", i=GROUP)

    def edges0(queries):
        with Phase(nc, "e0") as ctx:
            ps = EdgePass(ctx, kv_t, 2 * D, W0, local_d)
            turned = Turned(ps, 4)
            B_Q, B_S = 5, 6
            prod = ps.sb("prod", [P, GROUP, D])
            dots = ps.sb("dots", [P, GROUP * HEADS0])
            clip = ps.sb("clip", [P, GROUP * HEADS0])
            msg = ps.sb("msg", [P, 2, GROUP, W0])
            s_q, s_prod, s_dots, s_clip = (ps.sem(n) for n in ("q", "prod", "dots", "clip"))
            s_score, s_msg = ps.sem("score"), ps.sem("msg")
            score = bank[B_S][:, 0:GROUP * HEADS0]
            ones = ps.sem("ones")
            V.memset(msg[:, :, :, W0 - 1], 1.0).then_inc(ones, 1)
            PE.wait_ge(ones, 1)

            def gather(g):
                ps.gather(g, s_msg)

            def front(g):
                ps.select(g)
                turned.turn(g, s_q)

            def scores(g):
                tiles = ps.tiles(g, PE_ENGINE)
                PE.wait_ge(turned.s_copied, g.n + 1)
                if g.old(1):
                    PE.wait_ge(s_prod, g.n)
                for i in range(GROUP):
                    m = PE.matmul(bank[B_Q][:, i * P:(i + 1) * P], turned.sel_t[:, g.r2, i, :],
                                  queries[:, ds(tiles[i], 1), :].rearrange("p a d -> p (a d)"),
                                  start=True, stop=True)
                m.then_inc(s_q, 1)
                ps.have_rows(V, g)
                V.wait_ge(s_q, g.n + 1)
                if g.old(1):
                    V.wait_ge(s_dots, g.n)
                V.tensor_tensor(prod[:], ps.rows[:, g.slot, :, 0:D], quad(B_Q), ALU.mult).then_inc(s_prod, 1)
                V.wait_ge(s_prod, g.n + 1)
                if g.old(1):
                    V.wait_ge(s_clip, g.n)
                V.tensor_reduce(dots[:], prod[:].rearrange("p i (h c) -> p (i h) c", c=HDIM0), AX.X, ALU.add
                                ).then_inc(s_dots, 1)
                V.wait_ge(s_dots, g.n + 1)
                if g.old(1):
                    V.wait_ge(s_score, 2 * g.n)
                V.tensor_scalar(clip[:], dots[:], -20.0, 20.0, ALU.max, ALU.min).then_inc(s_clip, 1)
                A.wait_ge(s_clip, g.n + 1)
                if g.old(1):
                    A.wait_ge(s_msg, g.n)
                A.activation(score, clip[:], ACT.Exp, scale=0.25).then_inc(s_score, 1)
                if g.old(2):
                    A.wait_ge(ps.s_sums, (g.n - 1) * GROUP)
                A.activation(msg[:, g.r2, :, D:D + HEADS0], clip[:].rearrange("p (i h) -> p i h", i=GROUP),
                             ACT.Exp, scale=0.25).then_inc(s_score, 1)

            def sums(g):
                PE.wait_ge(s_msg, g.n + 1)
                ps.scatter(g, lambda i: [(0, msg[:, g.r2, i, :])])
                ps.add(g)

            def message(g):
                V.wait_ge(s_score, 2 * (g.n + 1))
                for i in range(GROUP):
                    m = V.tensor_tensor(msg[:, g.r2, i, 0:D].rearrange("p (h c) -> p h c", c=HDIM0),
                                        ps.rows[:, g.slot, i, D:2 * D].rearrange("p (h c) -> p h c", c=HDIM0),
                                        spread(score[:, i * HEADS0:(i + 1) * HEADS0], HDIM0), ALU.mult)
                m.then_inc(s_msg, 1)

            ps.run([(0, gather), (0, front), (1, scores), (2, sums), (1, message)])

    def edges1():
        with Phase(nc, "e1") as ctx:
            w1 = ctx.sb("w1", [ED + 1, D])
            chunk_of = ctx.sb("chunk", [1, ITEMS_PAD], I32)
            ps = EdgePass(ctx, x1_t, D + 1, W1, local_d,
                          [(w1[0:ED, :], a["L1_gnn_W1e"]),
                           (w1[ED:ED + 1, :], a["L1_gnn_b1e"].rearrange("(a n) -> a n", a=1)),
                           (chunk_of[:], item_rows[1:2, :])])
            attr = ps.sb("attr", [ED + 1, SLOTS, GROUP, P])
            hid = ps.sb("hid", [P, 2, GROUP, D])
            s_attr = [ps.sem(f"attr{u}") for u in range(SLOTS)]
            s_h, s_relu, ones = ps.sem("h"), ps.sem("relu"), ps.sem("ones")
            B_H = (4, 5)
            V.memset(attr[ED:ED + 1, :, :, :], 1.0).then_inc(ones, 1)
            PE.wait_ge(ones, 1)

            def gather(g):
                ps.gather(g, ps.s_sums, GROUP)
                u = g.slot
                _, chunks = nc.values_load_multi_w_load_instructions(
                    chunk_of[0:1, ds(g.n * GROUP, GROUP)], engines=(SP_ENGINE,), min_val=0, max_val=N_CHUNKS - 1,
                    skip_runtime_bounds_check_because=CLIPPED)
                if g.old(SLOTS):
                    SP.wait_ge(s_h, g.n - (SLOTS - 1))
                for i in range(GROUP):
                    SP.dma_start(attr[0:ED, u, i, :], a["attr_rows"][ds(chunks[i], 1), :, :]
                                 .rearrange("a k e -> (a k) e")).then_inc(s_attr[u], 16)

            def hidden(g):
                ps.select(g)
                PE.wait_ge(s_attr[g.slot], (g.i + 1) * 64)
                if g.old(2):
                    PE.wait_ge(s_relu, (g.n - 1) * GROUP)
                for i in range(GROUP):
                    m = PE.matmul(bank[B_H[g.r2]][:, i * P:(i + 1) * P], attr[:, g.slot, i, :], w1[:],
                                  start=True, stop=True)
                m.then_inc(s_h, 1)
                A.wait_ge(s_h, g.n + 1)
                ps.have_rows(A, g)
                if g.old(2):
                    A.wait_ge(ps.s_sums, (g.n - 1) * GROUP)
                for i in range(GROUP):
                    A.activation(hid[:, g.r2, i, :], bank[B_H[g.r2]][:, i * P:(i + 1) * P], ACT.Relu,
                                 scale=ps.rows[:, g.slot, i, D:D + 1]).then_inc(s_relu, 1)

            def sums(g):
                PE.wait_ge(s_relu, (g.n + 1) * GROUP)
                PE.wait_ge(ps.s_sel, g.n + 1)
                ps.have_rows(PE, g)
                ps.scatter(g, lambda i: [(0, ps.rows[:, g.slot, i, :]), (D + 1, hid[:, g.r2, i, :])])
                ps.add(g)

            ps.run([(0, gather), (0, hidden), (1, sums)])

    def edges2():
        with Phase(nc, "e2") as ctx:
            w0 = ctx.sb("w0", [2 * NB, 2 * RH])
            b0 = ctx.sb("b0", [2 * RH, 1])
            w1 = ctx.sb("w1", [2 * RH, 2, RH])
            b1 = ctx.sb("b1", [RH, 1])
            w2 = ctx.sb("w2", [RH + 1, D])
            rhat = ctx.sb("rhat", [P, N_ITEMS, 3])
            clear = ctx.sem("clear")
            G.memset(w0[:], 0.0).then_inc(clear, 1)
            G.memset(w1[:], 0.0).then_inc(clear, 1)
            SP.wait_ge(clear, 2)
            fixed = [(w0[h * NB:(h + 1) * NB, h * RH:(h + 1) * RH], a["L2_gnn_mlp_w0"]) for h in range(2)]
            fixed += [(b0[h * RH:(h + 1) * RH, :], vec_col(a["L2_gnn_mlp_b0"])) for h in range(2)]
            fixed += [(w1[h * RH:(h + 1) * RH, h, :], a["L2_gnn_mlp_w1"]) for h in range(2)]
            fixed += [(b1[:], vec_col(a["L2_gnn_mlp_b1"])), (w2[0:RH, :], a["L2_gnn_mlp_w2"]),
                      (w2[RH:RH + 1, :], a["L2_gnn_mlp_b2"].rearrange("(a n) -> a n", a=1)),
                      (rhat[:], rhat_d[:, 0:N_ITEMS, :])]
            ps = EdgePass(ctx, up_t, D, W2, local_d, fixed)
            emb = ps.sb("emb", [2 * NB, SLOTS, 2 * P])
            h1 = ps.sb("h1", [2 * RH, 2, 2 * P])
            h2 = ps.sb("h2", [RH + 1, 2, 4 * P])
            w1ss = ps.sb("w1ss", [P, GROUP, MUL])
            u_c = ps.sb("u_c", [P, GROUP, 3, MUL])
            u = ps.sb("u", [P, GROUP, MUL])
            msg = ps.sb("msg", [P, 2, GROUP, W2])
            s_emb = [ps.sem(f"emb{n}") for n in range(SLOTS)]
            s_h1, s_silu1, s_h2, s_silu2, s_w, s_dir = (ps.sem(n) for n in
                                                        ("h1", "silu1", "h2", "silu2", "w", "dir"))
            s_w1ss, s_u_c, s_u, s_msg, ones = (ps.sem(n) for n in ("w1ss", "u_c", "u", "msg", "ones"))
            B_H1, B_H2, B_W, B_DIR = 4, 5, 6, 7
            V.memset(h2[RH:RH + 1, :, :], 1.0).then_inc(ones, 1)
            PE.wait_ge(ones, 1)

            def gather(g):
                ps.gather(g, s_msg)
                if g.old(SLOTS):
                    SP.wait_ge(s_h1, g.n - (SLOTS - 1))
                SP.dma_start(emb[:, g.slot, :],
                             emb_d[ds(g.n * 2, 2), :, :, :].rearrange("a j b e -> (a j) (b e)")
                             ).then_inc(s_emb[g.slot], 16)

            def hidden1(g):
                PE.wait_ge(s_emb[g.slot], (g.i + 1) * 16)
                if g.old(1):
                    PE.wait_ge(s_silu1, g.n)
                PE.matmul(bank[B_H1][:, 0:2 * P], w0[:], emb[:, g.slot, :], start=True, stop=True
                          ).then_inc(s_h1, 1)
                A.wait_ge(s_h1, g.n + 1)
                if g.old(2):
                    A.wait_ge(s_h2, g.n - 1)
                A.activation(h1[:, g.r2, :], bank[B_H1][:, 0:2 * P], ACT.Silu, bias=b0[:]).then_inc(s_silu1, 1)

            def hidden2(g):
                PE.wait_ge(s_silu1, g.n + 1)
                if g.old(1):
                    PE.wait_ge(s_silu2, g.n)
                for h in range(2):
                    m = PE.matmul(bank[B_H2][0:RH, h * 2 * P:(h + 1) * 2 * P], w1[:, h, :], h1[:, g.r2, :], start=True, stop=True)
                m.then_inc(s_h2, 1)
                A.wait_ge(s_h2, g.n + 1)
                if g.old(2):
                    A.wait_ge(s_w, g.n - 1)
                A.activation(h2[0:RH, g.r2, :], bank[B_H2][0:RH, :], ACT.Silu, bias=b1[:]).then_inc(s_silu2, 1)

            def messages(g):
                ps.select(g)
                PE.wait_ge(s_silu2, g.n + 1)
                if g.old(1):
                    PE.wait_ge(s_msg, g.n)
                for i in range(GROUP):
                    m = PE.matmul(bank[B_W][:, i * P:(i + 1) * P], h2[:, g.r2, i * P:(i + 1) * P], w2[:],
                                  start=True, stop=True)
                m.then_inc(s_w, 1)
                w = quad(B_W)
                to = msg[:, g.r2]
                rows = ps.rows[:, g.slot]
                ss, vv = rows[:, :, 0:MUL], rows[:, :, MUL:].rearrange("p i (c k) -> p i c k", c=3)
                turned_to = to[:, :, 2 * MUL:].rearrange("p i (c s k) -> p i c s k", c=3, s=2)
                direction = bank[B_DIR][:, 0:GROUP * 3].rearrange("p (i c) -> p i c", c=3).unsqueeze(3) \
                    .to_broadcast([P, GROUP, 3, MUL])

                def thrice(t):
                    return t.unsqueeze(2).to_broadcast([P, GROUP, 3, MUL])

                if g.old(1):
                    V.wait_ge(s_msg, g.n)
                V.tensor_scalar(bank[B_DIR][:, 0:GROUP * 3], rhat[:, ds(g.n * GROUP, GROUP), :]
                                .rearrange("p i c -> p (i c)"), 1.0, None, ALU.mult).then_inc(s_dir, 1)
                ps.have_rows(V, g)
                V.wait_ge(s_w, g.n + 1)
                V.wait_ge(s_dir, g.n + 1)
                if g.old(2):
                    V.wait_ge(ps.s_sums, (g.n - 1) * GROUP)
                V.tensor_tensor(w1ss[:], w[:, :, MUL:2 * MUL], ss, ALU.mult).then_inc(s_w1ss, 1)
                V.tensor_tensor(u_c[:], vv, direction, ALU.mult).then_inc(s_u_c, 1)
                V.tensor_tensor(to[:, :, 0:MUL], w[:, :, 0:MUL], ss, ALU.mult)
                V.wait_ge(s_u_c, g.n + 1)
                V.tensor_reduce(u[:], u_c[:].rearrange("p i c k -> p i k c"), AX.X, ALU.add).then_inc(s_u, 1)
                V.wait_ge(s_w1ss, g.n + 1)
                V.tensor_tensor(turned_to[:, :, :, 0, :], thrice(w1ss[:]), direction, ALU.mult)
                V.tensor_tensor(turned_to[:, :, :, 1, :], thrice(w[:, :, 2 * MUL:3 * MUL]), vv, ALU.mult)
                V.wait_ge(s_u, g.n + 1)
                V.tensor_tensor(to[:, :, MUL:2 * MUL], w[:, :, 3 * MUL:], u[:], ALU.mult).then_inc(s_msg, 1)

            def sums(g):
                PE.wait_ge(s_msg, g.n + 1)
                PE.wait_ge(ps.s_sel, g.n + 1)
                ps.scatter(g, lambda i: [(0, msg[:, g.r2, i, :])])
                ps.add(g)

            ps.run([(0, gather), (3, sums), (0, hidden1), (1, hidden2), (2, messages)])

    def edges3_max():
        with Phase(nc, "e3m") as ctx:
            ps = EdgePass(ctx, fs_t, D, D, local_last_d)
            reset = ps.sb("reset", [P, SLOTS, GROUP * P])
            run = ps.sb("run", [P, 2, GROUP * P])
            back = ps.sb("back", [P, 2, GROUP, P])
            s_reset = [ps.sem(f"reset{u}") for u in range(SLOTS)]
            s_f, s_run, s_b, s_back, start = (ps.sem(n) for n in ("f", "run", "b", "back", "start"))
            B_F, B_B = (4, 5), (6, 7)
            V.memset(run[:], LOW).then_inc(start, 1)
            V.wait_ge(start, 1)

            def gather(g):
                ps.gather(g, s_f)
                if g.old(SLOTS):
                    SP.wait_ge(s_run, g.n - (SLOTS - 1))
                SP.dma_start(reset[:, g.slot, :], reset_d[ds(g.n, 1), :].to_broadcast([P, GROUP * P])
                             ).then_inc(s_reset[g.slot], 16)

            def forward(g):
                ps.have_rows(PE, g)
                if g.old(2):
                    PE.wait_ge(s_run, g.n - 1)
                for i in range(GROUP):
                    m = PE.transpose(bank[B_F[g.r2]][:, i * P:(i + 1) * P], ps.rows[:, g.slot, i, :], ident[:])
                m.then_inc(s_f, 1)
                ps.select(g)
                V.wait_ge(s_f, g.n + 1)
                V.wait_ge(s_reset[g.slot], (g.i + 1) * 16)
                if g.old(1):
                    V.wait_ge(s_run, g.n)
                if g.old(2):
                    V.wait_ge(s_b, g.n - 1)
                V.tensor_tensor_scan(run[:, g.r2, :], reset[:, g.slot, :], bank[B_F[g.r2]][:],
                                     run[:, 1 - g.r2, GROUP * P - 1:GROUP * P], ALU.add, ALU.max
                                     ).then_inc(s_run, 1)

            def backward(g):
                PE.wait_ge(s_run, g.n + 1)
                if g.old(2):
                    PE.wait_ge(s_back, g.n - 1)
                for i in range(GROUP):
                    m = PE.transpose(bank[B_B[g.r2]][:, i * P:(i + 1) * P], run[:, g.r2, i * P:(i + 1) * P],
                                     ident[:])
                m.then_inc(s_b, 1)
                A.wait_ge(s_b, g.n + 1)
                if g.old(2):
                    A.wait_ge(ps.s_sums, (g.n - 1) * GROUP)
                A.activation(back[:, g.r2].rearrange("p i d -> p (i d)"), bank[B_B[g.r2]][:], ACT.Copy
                             ).then_inc(s_back, 1)

            def sums(g):
                PE.wait_ge(s_back, g.n + 1)
                PE.wait_ge(ps.s_sel, g.n + 1)
                ps.scatter(g, lambda i: [(0, back[:, g.r2, i, :])])
                ps.add(g)

            ps.run([(0, gather), (0, forward), (1, backward), (2, sums)])

    def edges3(at_dst):
        with Phase(nc, "e3") as ctx:
            ps = EdgePass(ctx, fsv_t, 2 * D, W3, local_d)
            turned = Turned(ps, 4)
            B_A, B_M, B_E = 5, 6, 7
            relu = ps.sb("relu", [P, GROUP, D])
            diff = ps.sb("diff", [P, GROUP, D])
            msg = ps.sb("msg", [P, 2, GROUP, W3])
            s_a, s_relu, s_e, s_diff, s_exp, s_msg = (ps.sem(n) for n in
                                                      ("a", "relu", "e", "diff", "exp", "msg"))

            def gather(g):
                if g.old(SLOTS):
                    G.wait_ge(s_a, g.n - (SLOTS - 1))
                ps.gather(g, s_msg)

            def front(g):
                ps.select(g)
                turned.turn(g, s_a)

            def scores(g):
                tiles = ps.tiles(g, PE_ENGINE)
                PE.wait_ge(turned.s_copied, g.n + 1)
                ps.have_rows(PE, g)
                if g.old(1):
                    PE.wait_ge(s_diff, g.n)
                for i in range(GROUP):
                    dst_rows = at_dst[:, ds(tiles[i], 1), :].rearrange("p a d -> p (a d)")
                    cols = slice(i * P, (i + 1) * P)
                    PE.matmul(bank[B_A][:, cols], ident[:], ps.rows[:, g.slot, i, 0:D], start=True, stop=False)
                    PE.matmul(bank[B_A][:, cols], turned.sel_t[:, g.r2, i, :], dst_rows[:, 0:D],
                              start=False, stop=True)
                    m = PE.matmul(bank[B_M][:, cols], turned.sel_t[:, g.r2, i, :], dst_rows[:, D:2 * D],
                                  start=True, stop=True)
                m.then_inc(s_a, 1)
                A.wait_ge(s_a, g.n + 1)
                if g.old(1):
                    A.wait_ge(s_e, g.n)
                A.activation(relu[:], quad(B_A), ACT.Relu, scale=0.8).then_inc(s_relu, 1)
                V.wait_ge(s_relu, g.n + 1)
                if g.old(1):
                    V.wait_ge(s_exp, 2 * g.n)
                V.scalar_tensor_tensor(out=diff[:], in0=quad(B_A), scalar=0.2, in1=relu[:],
                                       op0=ALU.mult, op1=ALU.add).then_inc(s_e, 1)
                V.wait_ge(s_e, g.n + 1)
                V.tensor_tensor(diff[:], diff[:], quad(B_M), ALU.subtract).then_inc(s_diff, 1)
                A.wait_ge(s_diff, g.n + 1)
                if g.old(1):
                    A.wait_ge(s_msg, g.n)
                A.activation(quad(B_E), diff[:], ACT.Exp).then_inc(s_exp, 1)
                if g.old(2):
                    A.wait_ge(ps.s_sums, (g.n - 1) * GROUP)
                A.activation(msg[:, g.r2, :, D:2 * D], diff[:], ACT.Exp).then_inc(s_exp, 1)

            def sums(g):
                PE.wait_ge(s_msg, g.n + 1)
                ps.scatter(g, lambda i: [(0, msg[:, g.r2, i, :])])
                ps.add(g)

            def message(g):
                V.wait_ge(s_exp, 2 * (g.n + 1))
                V.tensor_tensor(msg[:, g.r2, :, 0:D], ps.rows[:, g.slot, :, D:2 * D], quad(B_E), ALU.mult
                                ).then_inc(s_msg, 1)

            ps.run([(0, gather), (0, front), (1, scores), (2, sums), (1, message)])

    with root:
        setup()
        with nc.sbuf_tensor("queries", [P, N_TILES, D], F32) as queries:
            project0(queries)
            edges0(queries)
        with nc.sbuf_tensor("inv_root_deg", [P, N_TILES], F32) as inv_root_deg:
            after0(inv_root_deg)
            edges1()
            after1(inv_root_deg)
        edges2()
        with nc.sbuf_tensor("at_dst", [P, N_TILES, 2 * D], F32) as at_dst:
            after2(at_dst)
            edges3_max()
            maxima(at_dst)
            edges3(at_dst)
        after3()


_WEIGHTS = ["L0_gnn_Wq", "L0_gnn_bq", "L0_gnn_Wk", "L0_gnn_bk", "L0_gnn_Wv", "L0_gnn_bv",
            "L1_gnn_W1n", "L1_gnn_b1n", "L1_gnn_W2n", "L1_gnn_b2n", "L1_gnn_W1e", "L1_gnn_b1e",
            "L1_gnn_W2e", "L1_gnn_b2e", "L1_gnn_rms_w", "L2_gnn_W_up0", "L2_gnn_W_up1",
            "L2_gnn_mlp_w0", "L2_gnn_mlp_b0", "L2_gnn_mlp_w1", "L2_gnn_mlp_b1", "L2_gnn_mlp_w2",
            "L2_gnn_mlp_b2", "L2_gnn_W_out0", "L2_gnn_W_out1", "L3_gnn_b_src", "L3_gnn_b_dst", "L3_gnn_b_v"]


def kernel(**inputs):
    import numpy as np
    import concourse.bacc as bacc
    from concourse import mybir as _mybir
    from concourse.bass_utils import run_bass_kernel_spmd as run

    get = lambda name: np.asarray(inputs[name])
    pad = N_CHUNKS * P - N_EDGES

    def chunks(v, fill):
        v = np.concatenate([v, np.full((pad,) + v.shape[1:], fill, v.dtype)])
        return v.reshape((N_CHUNKS, P) + v.shape[1:])

    dst = get("dst")
    ends = np.concatenate([np.full((1,), -1, dst.dtype), dst, np.full((pad + 1,), FAR, dst.dtype)])
    arrays = {
        "x": get("x"),
        "dst_rows": np.ascontiguousarray(np.stack([ends[c * P:c * P + P + 2] for c in range(N_CHUNKS)])),
        "src_rows": chunks(get("src"), 0),
        "vec_rows": np.ascontiguousarray(chunks(get("edge_attr_3"), 0).transpose(0, 2, 1)).reshape(N_CHUNKS, 3 * P),
        "length_rows": chunks(get("edge_weight"), 0),
        "attr_rows": np.ascontiguousarray(chunks(get("edge_attr_64"), 0).transpose(0, 2, 1)),
        "gin_eps": get("L1_gnn_gin_eps").reshape(1, 1),
        "W_src_t": np.ascontiguousarray(get("L3_gnn_W_src").T),
        "W_dst_t": np.ascontiguousarray(get("L3_gnn_W_dst").T),
        "W_v_t": np.ascontiguousarray(get("L3_gnn_W_v").T),
    }
    arrays.update({name: get(name) for name in _WEIGHTS})

    nc = bacc.Bacc("TRN2", target_bir_lowering=False, num_devices=1)
    aps = {name: nc.dram_tensor(f"in_{name}", v.shape, _mybir.dt.from_np(v.dtype), kind="ExternalInput").ap()
           for name, v in arrays.items()}
    aps["out"] = nc.dram_tensor("out_x", (N_NODES, D), F32, kind="ExternalOutput").ap()
    build(nc, aps)
    r = run(nc, [{f"in_{name}": np.ascontiguousarray(v) for name, v in arrays.items()}], core_ids=[0])
    return r.results[0]["out_x"]
```

```python
from contextlib import ExitStack

import concourse.bass as bass
from concourse import mybir

P = 128
N_NODES = 6250
N_EDGES = 106250
D = 128
N_TILES = -(-N_NODES // P)
N_CHUNKS = -(-N_EDGES // P)
GROUP = 4
SLOTS = 4
N_GROUPS = -(-(N_CHUNKS + N_TILES - 1) // (GROUP * SLOTS)) * SLOTS
N_ITEMS = GROUP * N_GROUPS
ITEM_TILES = -(-N_ITEMS // P)
ITEMS_PAD = ITEM_TILES * P
BLOCK = 7
N_BLOCKS = N_TILES // BLOCK
assert N_BLOCKS * BLOCK == N_TILES
FULL_TILES = N_NODES // P
REST = N_NODES - FULL_TILES * P
HEADS0, HDIM0 = 8, 16
ED = 64
MUL, NB, RH = 32, 8, 64
SQ3 = 3.0 ** 0.5
AVG = 16.0
FAR = 1 << 20
LOW = -3.0e38
LN_EPS = 1e-5
RMS_EPS = 1.1920929e-07

F32 = mybir.dt.float32
I32 = mybir.dt.int32
ALU = mybir.AluOpType
ACT = mybir.ActivationFunctionType
AX = mybir.AxisListType
DVE_ENGINE = mybir.EngineType.DVE
PE_ENGINE = mybir.EngineType.PE
SP_ENGINE = mybir.EngineType.SP
ds = bass.ds
CLIPPED = "the setup clips tiles and chunks to their tables"

W0 = 128 + HEADS0 + 1
W1 = 2 * D + 1
W2 = 256
W3 = 256
ACC_W = max(W0, W1, W2, W3)


class Counter:

    def __init__(self, sem, by=1):
        self.sem, self.by, self.at, self.per, self.round = sem, by, 0, 0, 0

    def did(self, instruction):
        instruction.then_inc(self.sem, self.by)
        self.at += self.by
        return self, self.at


def wait(engine, *marks):
    last = {}
    for counter, at in marks:
        last[counter] = max(at, last.get(counter, 0))
    for counter, at in last.items():
        engine.wait_ge(counter.sem, counter.round * counter.per + at)


def rounds(nc, counters, engines, n, body, ready):
    for c in counters:
        c.at = c.per = c.round = 0
    body(0)
    for c in counters:
        c.per = c.at
    with nc.Fori(1, n) as b:
        for c in counters:
            c.round, c.at = b, 0
        for e in engines:
            for c in counters:
                if c.per:
                    e.wait_ge(c.sem, b * c.per)
            e.wait_ge(ready, 1)
        body(b)
    for c in counters:
        assert c.at == c.per


class Phase(ExitStack):

    def __init__(self, nc, tag):
        super().__init__()
        self.nc, self.tag, self.sems = nc, tag, []

    def sb(self, name, shape, dt=F32):
        return self.enter_context(self.nc.sbuf_tensor(f"{self.tag}_{name}", shape, dt))

    def sem(self, name):
        self.sems.append(self.nc.alloc_semaphore(f"{self.tag}_{name}"))
        return self.sems[-1]

    def end(self):
        self.nc.all_engine_barrier()
        self.nc.clear_and_free_semaphores(self.sems)
        self.nc.all_engine_barrier()


class Group:

    def __init__(self, i, u):
        self.i, self.u, self.n = i, u, i * SLOTS + u
        self.round = i + u // SLOTS
        self.slot, self.r2 = u % SLOTS, u % 2
        self.old = lambda k: not isinstance(self.n, int) or self.n >= k

    def upto(self, k):
        return self.i * SLOTS + (self.u + k + 1)


def pipeline(nc, stages):
    depth = max(lag for lag, _ in stages)
    assert depth <= SLOTS

    def step(i, v):
        for lag, fn in stages:
            g = Group(i, v - lag)
            if isinstance(g.n, int) and not 0 <= g.n < N_GROUPS:
                continue
            fn(g)

    for s in range(2 * SLOTS):
        step(s // SLOTS, s % SLOTS)
    with nc.Fori(2, N_GROUPS // SLOTS) as i:
        for v in range(SLOTS):
            step(i, v)
    for s in range(N_GROUPS, N_GROUPS + depth):
        step(s // SLOTS, s % SLOTS)


def build(nc, a):
    PE, V, A, G, SP = nc.tensor, nc.vector, nc.scalar, nc.gpsimd, nc.sync
    ENGINES = (PE, V, A, G, SP)
    root = ExitStack()

    def dram(name, shape, dt=F32):
        return nc.dram_tensor(name, shape, dt).ap()

    first_col = dram("dst_heads", [2, ITEMS_PAD], I32)
    item_rows = dram("item_rows", [2, ITEMS_PAD], I32)
    local_d = dram("local_d", [P, ITEMS_PAD])
    local_last_d = dram("local_last_d", [P, ITEMS_PAD])
    src_d = dram("src_d", [P, ITEMS_PAD], I32)
    rhat_d = dram("rhat_d", [P, ITEMS_PAD, 3])
    reset_d = dram("reset_d", [ITEMS_PAD // GROUP, GROUP * P])
    emb_d = dram("emb_d", [ITEMS_PAD // 2, NB, 2, P])
    kv_t = dram("kv_t", [N_TILES * P, 2 * D])
    x1_t = dram("x1_t", [N_TILES * P, D + 1])
    up_t = dram("up_t", [N_TILES * P, D])
    fs_t = dram("fs_t", [N_TILES * P, D])
    fsv_t = dram("fsv_t", [N_TILES * P, 2 * D])

    def by_tile(table):
        return table.rearrange("(t p) d -> p t d", p=P)

    def carry(engine, sem):
        engine.sem_inc(sem, 1)

    def sb(ctx, name, shape, dt=F32):
        return ctx.enter_context(nc.sbuf_tensor(name, shape, dt))

    x = sb(root, "x", [P, N_TILES, D])
    acc = sb(root, "acc", [P, N_TILES, ACC_W])
    ident = sb(root, "ident", [P, P])
    node_iota = sb(root, "node_iota", [P, P])
    ones_row = sb(root, "ones_row", [1, P])
    tile_of = sb(root, "tile_of", [1, ITEMS_PAD], I32)
    banks = root.enter_context(nc.psum_tensor("banks", [P, 8, 512], F32))
    bank = [banks[:, i, :] for i in range(8)]

    def counters(ctx):
        return lambda name, by=1: Counter(ctx.sem(name), by)

    def setup():
        with Phase(nc, "set") as ctx:
            make = counters(ctx)
            pe, v, act, g = make("pe"), make("v"), make("act"), make("g")
            dma = lambda name: make(name, 16)
            d_x, d_head, d_items, d_out = dma("d_x"), dma("d_head"), dma("d_items"), dma("d_out")
            d_rows, d_tile = dma("d_rows"), dma("d_tile")

            m = g.did(G.memset(x[:, FULL_TILES, :], 0.0))
            wait(SP, m)
            d_x.did(SP.dma_start(x[:, 0:FULL_TILES, :],
                                 a["x"][0:FULL_TILES * P, :].rearrange("(t p) d -> p t d", p=P)))
            x_in = d_x.did(SP.dma_start(x[0:REST, FULL_TILES, :], a["x"][FULL_TILES * P:N_NODES, :]))

            heads = sb(ctx, "heads", [1, 2, N_CHUNKS], I32)
            with nc.allow_non_contiguous_dma(reason="first and last destination of each chunk"):
                d_head.did(SP.dma_start(heads[:, 0, :], a["dst_rows"][:, 1:2].rearrange("c a -> a c")))
                heads_in = d_head.did(SP.dma_start(heads[:, 1, :],
                                                   a["dst_rows"][:, P:P + 1].rearrange("c a -> a c")))

            iota_i = sb(ctx, "iota_i", [P, P], I32)
            item_i = sb(ctx, "item_i", [P, ITEM_TILES], I32)
            m1 = g.did(G.iota(iota_i[:], pattern=[[1, P]], base=0, channel_multiplier=0))
            m2 = g.did(G.iota(item_i[:], pattern=[[P, ITEM_TILES]], base=0, channel_multiplier=1))
            g.did(G.memset(ident[:], 0.0))
            m3 = g.did(G.memset(ones_row[:], 1.0))
            wait(G, m3)
            ident_ready = g.did(G.affine_select(out=ident[:], in_=ident[:], compare_op=ALU.not_equal, fill=1.0,
                                                base=0, pattern=[[-1, P]], channel_multiplier=1))
            item_no = sb(ctx, "item_no", [P, ITEM_TILES])
            wait(V, m1, m2)
            v.did(V.tensor_copy(node_iota[:], iota_i[:]))
            v.did(V.tensor_copy(item_no[:], item_i[:]))

            tiles_i = sb(ctx, "tiles_i", [1, 2, N_CHUNKS], I32)
            tiles = sb(ctx, "tiles", [1, 2, N_CHUNKS])
            row = sb(ctx, "row", [1, 4, N_CHUNKS])
            wait(V, heads_in)
            m = v.did(V.tensor_scalar(tiles_i[:], heads[:], 7, None, ALU.arith_shift_right))
            wait(V, m)
            m = v.did(V.tensor_copy(tiles[:], tiles_i[:]))
            wait(V, m)
            m = v.did(V.tensor_scalar(row[:, 0, :], tiles[:, 1, :], float(N_TILES - 1), 1.0, ALU.min, ALU.add))
            wait(V, m)
            m = v.did(V.tensor_tensor(row[:, 0, :], row[:, 0, :], tiles[:, 0, :], ALU.subtract))
            m0 = v.did(V.memset(row[:, 1, :], 0.0))
            wait(V, m, m0)
            m = v.did(V.tensor_tensor_scan(row[:, 2, :], row[:, 1, :], row[:, 0, :], 0.0, ALU.add, ALU.add))
            wait(V, m)
            m = v.did(V.tensor_tensor(row[:, 1, :], row[:, 2, :], row[:, 0, :], ALU.subtract))
            wait(V, m)
            m = v.did(V.tensor_tensor(row[:, 2, :], tiles[:, 0, :], row[:, 1, :], ALU.subtract))
            wait(V, m)
            m0 = v.did(V.tensor_copy(row[:, 3, 0:1], row[:, 2, 0:1]))
            m = v.did(V.tensor_tensor(row[:, 3, 1:], row[:, 2, 1:], row[:, 2, 0:N_CHUNKS - 1], ALU.subtract))

            before = sb(ctx, "before", [P, N_CHUNKS])
            jump = sb(ctx, "jump", [P, N_CHUNKS])
            wait(PE, ident_ready, m0, m)
            for k, (r, lo) in enumerate([(1, 0), (1, 512), (3, 0), (3, 512)]):
                hi = min(lo + 512, N_CHUNKS)
                m = pe.did(PE.matmul(bank[k][:, 0:hi - lo], ones_row[:], row[:, r, lo:hi], start=True, stop=True))
                wait(V, m)
                to = before if r == 1 else jump
                m_rows = v.did(V.tensor_copy(to[:, lo:hi], bank[k][:, 0:hi - lo]))
            hit = sb(ctx, "hit", [P, 2, N_CHUNKS])
            found = sb(ctx, "found", [P, 2, ITEM_TILES])
            for q in range(ITEM_TILES):
                wait(V, m_rows)
                ma = v.did(V.tensor_scalar(hit[:, 0, :], before[:], item_no[:, q:q + 1], None, ALU.is_le))
                mb = v.did(V.scalar_tensor_tensor(out=hit[:, 1, :], in0=before[:], scalar=item_no[:, q:q + 1],
                                                  in1=jump[:], op0=ALU.is_le, op1=ALU.mult))
                wait(V, ma, mb)
                m_rows = v.did(V.tensor_reduce(found[:, :, q:q + 1], hit[:], AX.X, ALU.add))
            chunk = sb(ctx, "chunk", [P, ITEM_TILES])
            tile = sb(ctx, "tile", [P, ITEM_TILES])
            item_tab = sb(ctx, "item_tab", [P, 2, ITEM_TILES], I32)
            wait(V, m_rows)
            ma = v.did(V.tensor_scalar(chunk[:], found[:, 0, :], -1.0, None, ALU.add))
            mb = v.did(V.tensor_tensor(tile[:], found[:, 1, :], item_no[:], ALU.add))
            wait(V, ma, mb)
            v.did(V.tensor_copy(item_tab[:, 1, :], chunk[:]))
            v.did(V.tensor_scalar(item_tab[:, 0, :], tile[:], float(N_TILES - 1), None, ALU.min))
            tile_base = sb(ctx, "tile_base", [P, ITEM_TILES])
            m_tab = v.did(V.tensor_scalar(tile_base[:], tile[:], float(P), None, ALU.mult))
            wait(SP, m_tab)
            with nc.allow_non_contiguous_dma(reason="a small table, once"):
                d_tile.did(SP.dma_start(item_rows[0, :].rearrange("(q p) -> p q", p=P), item_tab[:, 0, :]))
                m = d_tile.did(SP.dma_start(item_rows[1, :].rearrange("(q p) -> p q", p=P), item_tab[:, 1, :]))
            wait(SP, m)
            tile_in = d_rows.did(SP.dma_start(tile_of[:], item_rows[0:1, :]))

            dst_i = sb(ctx, "dst_i", [P, ITEM_TILES, P + 2], I32)
            src_i = sb(ctx, "src_i", [P, ITEM_TILES, P], I32)
            vec = sb(ctx, "vec", [P, ITEM_TILES, 3 * P])
            length = sb(ctx, "length", [P, ITEM_TILES, P])
            wait(G, m_tab)
            for q in range(ITEM_TILES):
                at = bass.IndirectOffsetOnAxis(ap=item_tab[:, 1, q:q + 1], axis=0)
                for to, table in ((dst_i, a["dst_rows"]), (src_i, a["src_rows"]), (vec, a["vec_rows"]),
                                  (length, a["length_rows"])):
                    rows_in = d_items.did(G.indirect_dma_start(out=to[:, q, :], out_offset=None, in_=table,
                                                               in_offset=at))
            dst = sb(ctx, "dst", [P, ITEM_TILES, P + 2])
            spare = acc[:].rearrange("p t d -> p (t d)")
            by_item = spare[:, 0:6 * ITEMS_PAD].rearrange("p (k q e) -> p k q e", k=6, q=ITEM_TILES)
            assert (6 + NB) * ITEMS_PAD <= N_TILES * ACC_W
            reset = sb(ctx, "reset", [P, ITEM_TILES, P])
            tmp = sb(ctx, "tmp", [P, 2, ITEM_TILES, P])
            wait(V, rows_in)
            v.did(V.tensor_copy(by_item[:, 2], src_i[:]))
            m = v.did(V.tensor_copy(dst[:], dst_i[:]))
            wait(V, m)
            for q in range(ITEM_TILES):
                m = v.did(V.tensor_scalar(by_item[:, 0, q, :], dst[:, q, 1:P + 1], tile_base[:, q:q + 1], None,
                                          ALU.subtract))
            mb = v.did(V.tensor_tensor(reset[:], dst[:, :, 1:P + 1], dst[:, :, 0:P], ALU.not_equal))
            mc = v.did(V.tensor_tensor(tmp[:, 0], dst[:, :, 1:P + 1], dst[:, :, 2:P + 2], ALU.not_equal))
            wait(V, m, mb, mc)
            m_reset = v.did(V.tensor_scalar(reset[:], reset[:], LOW, None, ALU.mult))
            m = v.did(V.scalar_tensor_tensor(out=tmp[:, 1], in0=by_item[:, 0], scalar=1.0, in1=tmp[:, 0],
                                             op0=ALU.add, op1=ALU.mult))
            wait(V, m)
            m = v.did(V.tensor_scalar(by_item[:, 1], tmp[:, 1], -1.0, None, ALU.add))
            part = vec[:].rearrange("p q (c e) -> p q c e", c=3)
            wait(V, m)
            m = v.did(V.tensor_tensor(tmp[:, 0], part[:, :, 0, :], part[:, :, 0, :], ALU.mult))
            for c in (1, 2):
                mb = v.did(V.tensor_tensor(tmp[:, 1], part[:, :, c, :], part[:, :, c, :], ALU.mult))
                wait(V, m, mb)
                m = v.did(V.tensor_tensor(tmp[:, 0], tmp[:, 0], tmp[:, 1], ALU.add))
                wait(V, m)
            wait(A, m)
            m = act.did(A.activation(tmp[:, 1], tmp[:, 0], ACT.Sqrt))
            wait(V, m)
            m = v.did(V.tensor_scalar(tmp[:, 0], tmp[:, 1], 1e-12, None, ALU.add))
            wait(V, m)
            m = v.did(V.reciprocal(tmp[:, 1], tmp[:, 0]))
            wait(V, m)
            for c in range(3):
                m = v.did(V.tensor_tensor(by_item[:, 3 + c], part[:, :, c, :], tmp[:, 1], ALU.mult))

            wait(SP, m_reset)
            d_out.did(SP.dma_start(reset_d.rearrange("g (i e) -> (g i) e", i=GROUP)
                                   .rearrange("(q p) e -> p q e", p=P), reset[:]))

            table_f = [sb(ctx, f"table{k}", [P, ITEMS_PAD]) for k in range(2)]
            table_src = sb(ctx, "table_src", [P, ITEMS_PAD], I32)
            table_r = sb(ctx, "table_r", [P, ITEMS_PAD, 3])
            wait(PE, m)
            copies = []
            for n in range(6 * ITEM_TILES):
                k, q = n // ITEM_TILES, n % ITEM_TILES
                if n >= 8:
                    wait(PE, copies[n - 8])
                m = pe.did(PE.transpose(bank[n % 8][:, 0:P], by_item[:, k, q, :], ident[:]))
                to = (table_f + [table_src])[k][:, q * P:(q + 1) * P] if k < 3 else \
                    table_r[:, q * P:(q + 1) * P, k - 3]
                e, c = ((A, act), (V, v))[n % 2]
                wait(e, m)
                copies.append(c.did(e.tensor_copy(to, bank[n % 8][:, 0:P]) if e is V
                                    else e.activation(to, bank[n % 8][:, 0:P], ACT.Copy)))
            wait(SP, *copies)
            for to, of in ((local_d, table_f[0]), (local_last_d, table_f[1]), (src_d, table_src),
                           (rhat_d, table_r)):
                d_out.did(SP.dma_start(to, of[:]))

            clipped = sb(ctx, "clipped", [P, ITEM_TILES, P])
            inside = sb(ctx, "inside", [P, ITEM_TILES, P])
            emb = spare[:, 6 * ITEMS_PAD:(6 + NB) * ITEMS_PAD].rearrange("p (q j e) -> p q j e", q=ITEM_TILES, j=NB)
            mb = v.did(V.tensor_scalar(clipped[:], length[:], 0.0, 1.0, ALU.max, ALU.min))
            m = v.did(V.tensor_scalar(inside[:], length[:], 1.0, NB ** 0.5, ALU.is_le, ALU.mult))
            wait(V, mb, m)
            for j in range(NB):
                m = v.did(V.tensor_scalar(tmp[:, 0], clipped[:], float(NB - 1), float(-j), ALU.mult, ALU.add))
                wait(A, m)
                m = act.did(A.activation(tmp[:, 1], tmp[:, 0], ACT.Square))
                wait(A, m)
                m = act.did(A.activation(tmp[:, 1], tmp[:, 1], ACT.Exp, scale=-0.5))
                wait(V, m)
                m = v.did(V.tensor_tensor(emb[:, :, j, :], tmp[:, 1], inside[:], ALU.mult))
                wait(V, m)
            wait(SP, m)
            half = P // 2
            for q in range(ITEM_TILES):
                for b in range(2):
                    d_out.did(SP.dma_start(emb_d[q * half:(q + 1) * half, :, b, :], emb[b::2, q, :, :]))
            last = (d_out, d_out.at)
            for e in ENGINES:
                wait(e, last, x_in, tile_in)
            ctx.end()

    def node_phase(tag, body, weights=()):
        with Phase(nc, tag) as ctx:
            k = NodePhase(ctx)
            k.load(weights(ctx, k) if weights else [])
            body_fn = body(ctx, k)
            V.memset(k.small[:], 0.0).then_inc(k.ready, 1)
            V.wait_ge(k.ready, 1)
            rounds(nc, k.all, (PE, V, A), N_BLOCKS, body_fn, k.ready)
            for e in ENGINES:
                for c in k.all:
                    e.wait_ge(c.sem, c.per * N_BLOCKS)
            ctx.end()

    class NodePhase:

        def __init__(self, ctx):
            self.ctx, self.sb, self.ready = ctx, ctx.sb, ctx.sem("ready")
            self.s_carry = ctx.sem("carry")
            make = counters(ctx)
            self.pe, self.v, self.act = make("pe"), make("v"), make("act")
            self.out = make("out", 16)
            self.w = make("w", 16)
            self.prep = make("prep")
            self.all = [self.pe, self.v, self.act, self.out]
            self.small = ctx.sb("small", [P, 4, BLOCK])
            self.square = ctx.sb("square", [P, BLOCK, D])

        def load(self, pairs):
            for to, of in pairs:
                self.w.did(SP.dma_start(to, of))
            if pairs:
                for e in ENGINES:
                    wait(e, (self.w, self.w.at))

        def prepare(self, engine, instruction):
            wait(engine, self.prep.did(instruction))

        def prepared(self):
            for e in ENGINES:
                wait(e, (self.prep, self.prep.at))


        def transpose(self, of, to, ready, banks):
            wait(PE, *ready)
            done = []
            for n, (lo, hi) in enumerate(((0, 4), (4, BLOCK))):
                for j in range(lo, hi):
                    m = PE.transpose(bank[banks[n]][:, (j - lo) * P:(j - lo + 1) * P], of[:, j, :], ident[:])
                m = self.pe.did(m)
                wait(A, m)
                done.append(self.act.did(A.activation(
                    to[:, lo:hi, :], bank[banks[n]][:, 0:(hi - lo) * P].rearrange("p (t d) -> p t d", d=P),
                    ACT.Copy)))
            return done

        def project(self, pairs, ready, banks):
            wait(PE, *ready)
            out = []
            for n, (lo, hi) in enumerate(((0, 4), (4, BLOCK))):
                for j in range(lo, hi):
                    for k, (xt, w) in enumerate(pairs):
                        m = PE.matmul(bank[banks[n]][:, (j - lo) * P:(j - lo + 1) * P], xt[:, j, :], w,
                                      start=(k == 0), stop=(k == len(pairs) - 1))
                out.append((slice(lo, hi), bank[banks[n]][:, 0:(hi - lo) * P].rearrange("p (t d) -> p t d", d=P),
                            self.pe.did(m)))
            return out

        def moment(self, of, ready, eps, col):
            wait(A, *ready)
            m = self.act.did(A.activation(self.square[:], of, ACT.Square))
            wait(V, m)
            m = self.v.did(V.tensor_reduce(self.small[:, col, :], self.square[:], AX.X, ALU.add))
            wait(V, m)
            m = self.v.did(V.tensor_scalar(self.small[:, col, :], self.small[:, col, :], 1.0 / D, eps,
                                           ALU.mult, ALU.add))
            wait(A, m)
            m = self.act.did(A.activation(self.small[:, 3, :], self.small[:, col, :], ACT.Sqrt))
            wait(V, m)
            m = self.v.did(V.reciprocal(self.small[:, col, :], self.small[:, 3, :]))
            return m

        def layernorm(self, z, to, ready):
            wait(V, *ready)
            m = self.v.did(V.tensor_reduce(self.small[:, 0, :], z, AX.X, ALU.add))
            wait(V, m)
            m = self.v.did(V.tensor_scalar(self.small[:, 0, :], self.small[:, 0, :], 1.0 / D, None, ALU.mult))
            wait(V, m)
            m = self.v.did(V.tensor_tensor(z, z, spread(self.small[:, 0, :]), ALU.subtract))
            m = self.moment(z, [m], LN_EPS, 1)
            wait(V, m)
            return self.v.did(V.tensor_tensor(to, z, spread(self.small[:, 1, :]), ALU.mult))

    def spread(col, width=D):
        return col.unsqueeze(2).to_broadcast([P, col.shape[1], width])

    def tiles_of(row):
        return row.unsqueeze(1).to_broadcast([P, BLOCK, row.shape[1]])

    def vec_row(v):
        return v.rearrange("(a n) -> a n", a=1).to_broadcast([P, v.shape[0]])

    def vec_col(v):
        return v.rearrange("(n a) -> n a", a=1)

    def project0(queries):
        def weights(ctx, k):
            k.wqkv, k.bqkv = k.sb("w3", [P, 3 * D]), k.sb("b3", [P, 3 * D])
            pairs = []
            for n, name in enumerate(("k", "v", "q")):
                pairs.append((k.wqkv[:, n * D:(n + 1) * D], a[f"L0_gnn_W{name}"]))
                pairs.append((k.bqkv[:, n * D:(n + 1) * D], vec_row(a[f"L0_gnn_b{name}"])))
            return pairs

        def make(ctx, k):
            xin, xt, kv = k.sb("xin", [P, BLOCK, D]), k.sb("xt", [P, BLOCK, D]), k.sb("kv", [P, BLOCK, 2 * D])

            def body(b):
                own = ds(b * BLOCK, BLOCK)
                m = k.act.did(A.activation(xin[:], x[:, own, :], ACT.Copy))
                ready = k.transpose(xin, xt, [m], (0, 1))
                done = project3(k, xt, ready, k.wqkv, k.bqkv, kv, queries[:, own, :])
                wait(SP, *done)
                k.out.did(SP.dma_start(by_tile(kv_t)[:, own, :], kv[:]))
            return body
        node_phase("proj0", make, weights)

    def project3(k, xt, ready, w, bias, first, rest):
        wait(PE, *ready)
        done = []
        for j in range(BLOCK):
            b = 2 + j % 6
            if j >= 6:
                wait(PE, done[2 * (j - 6) + 1])
            m = k.pe.did(PE.matmul(bank[b][:, 0:3 * D], xt[:, j, :], w[:], start=True, stop=True))
            wait(V, m)
            done.append(k.v.did(V.tensor_tensor(first[:, j, :], bank[b][:, 0:2 * D], bias[:, 0:2 * D], ALU.add)))
            done.append(k.v.did(V.tensor_tensor(rest[:, j, :], bank[b][:, 2 * D:3 * D], bias[:, 2 * D:3 * D],
                                                ALU.add)))
        return done

    def after0(inv_root_deg):
        def make(ctx, k):
            z, t1 = k.sb("z", [P, BLOCK, D]), k.sb("t1", [P, BLOCK, D + 1])
            zs = k.sb("zs", [P, 2, BLOCK, HEADS0])

            def body(b):
                own = ds(b * BLOCK, BLOCK)
                m = k.v.did(V.tensor_scalar(zs[:, 0], acc[:, own, D:D + HEADS0], 1e-6, None, ALU.add))
                mb = k.v.did(V.tensor_scalar(k.small[:, 2, :], acc[:, own, D + HEADS0], 1.0, None, ALU.max))
                wait(A, mb)
                ma = k.act.did(A.activation(k.small[:, 3, :], k.small[:, 2, :], ACT.Sqrt))
                wait(V, m, ma)
                m = k.v.did(V.reciprocal(zs[:, 1], zs[:, 0]))
                mr = k.v.did(V.reciprocal(k.small[:, 2, :], k.small[:, 3, :]))
                wait(V, m, mr)
                mi = k.v.did(V.tensor_copy(inv_root_deg[:, own], k.small[:, 2, :]))
                for j in range(BLOCK):
                    m = k.v.did(V.tensor_tensor(
                        z[:, j, :].rearrange("p (h c) -> p h c", h=HEADS0),
                        acc[:, ds(b * BLOCK + j, 1), 0:D].rearrange("p a (h c) -> p (a h) c", h=HEADS0),
                        spread(zs[:, 1, j, :], HDIM0), ALU.mult))
                wait(V, m, mi)
                m = k.v.did(V.tensor_tensor(z[:], z[:], x[:, own, :], ALU.add))
                m = k.layernorm(z[:], x[:, own, :], [m])
                wait(V, m)
                k.v.did(V.tensor_tensor(t1[:, :, 0:D], x[:, own, :], spread(k.small[:, 2, :]), ALU.mult))
                m = k.v.did(V.tensor_copy(t1[:, :, D:D + 1], k.small[:, 2, :].unsqueeze(2)))
                wait(SP, m)
                k.out.did(SP.dma_start(by_tile(x1_t)[:, own, :], t1[:]))
            return body
        node_phase("after0", make)

    def after1(inv_root_deg):
        def weights(ctx, k):
            k.w2e, k.w1n, k.w2n, k.up = (k.sb(n, [P, D]) for n in ("w2e", "w1n", "w2n", "up"))
            k.b2e, k.b2n, k.rms = (k.sb(n, [P, D]) for n in ("b2e", "b2n", "rms"))
            k.b1n, k.eps = k.sb("b1n", [P, 1]), k.sb("eps", [P, 1])
            k.prepare(G, G.memset(k.up[:], 0.0))
            k.prepared()
            pairs = [(k.w2e[:], a["L1_gnn_W2e"]), (k.w1n[:], a["L1_gnn_W1n"]), (k.w2n[:], a["L1_gnn_W2n"]),
                     (k.b2e[:], vec_row(a["L1_gnn_b2e"])), (k.b2n[:], vec_row(a["L1_gnn_b2n"])),
                     (k.rms[:], vec_row(a["L1_gnn_rms_w"])), (k.b1n[:], vec_col(a["L1_gnn_b1n"])),
                     (k.eps[:], a["gin_eps"].to_broadcast([P, 1])),
                     (k.up[0:MUL, 0:MUL], a["L2_gnn_W_up0"])]
            pairs += [(k.up[MUL + c:P:3, MUL + MUL * c:2 * MUL + MUL * c], a["L2_gnn_W_up1"]) for c in range(3)]
            return pairs

        def make(ctx, k):
            k.prepare(V, V.tensor_scalar(k.up[:], k.up[:], MUL ** -0.5, None, ALU.mult))
            k.prepare(V, V.tensor_scalar(k.eps[:], k.eps[:], 1.0, None, ALU.add))
            k.prepared()
            h, ht, z, t2, x1 = (k.sb(n, [P, BLOCK, D]) for n in ("h", "ht", "z", "t2", "x1"))

            def body(b):
                own = ds(b * BLOCK, BLOCK)
                m = k.act.did(A.activation(h[:], acc[:, own, D + 1:W1], ACT.Copy))
                mx = k.act.did(A.activation(x1[:], x[:, own, :], ACT.Copy))
                mb = k.v.did(V.tensor_copy(k.small[:, 2, :], acc[:, own, D]))
                ready = k.transpose(h, ht, [m], (0, 1))
                wait(V, mb)
                for j in range(BLOCK):
                    m = k.v.did(V.tensor_scalar(z[:, j, :], k.b2e[:], k.small[:, 2, j:j + 1], None, ALU.mult))
                wait(V, m)
                m = k.v.did(V.tensor_tensor(z[:], z[:], acc[:, own, 0:D], ALU.add))
                for part, ps, done in k.project([(ht, k.w2e[:])], ready, (2, 3)):
                    wait(V, m, done)
                    ms = k.v.did(V.tensor_tensor(z[:, part, :], z[:, part, :], ps, ALU.add))
                wait(V, ms)
                m = k.v.did(V.tensor_tensor(z[:], z[:], spread(inv_root_deg[:, own]), ALU.mult))
                wait(V, m, mx)
                m = k.v.did(V.scalar_tensor_tensor(out=h[:], in0=x1[:], scalar=k.eps[:], in1=z[:],
                                                   op0=ALU.mult, op1=ALU.add))
                ready = k.transpose(h, ht, [m], (0, 1))
                wait(PE, *ready)
                hid = []
                for n, (lo, hi) in enumerate(((0, 4), (4, BLOCK))):
                    m = k.pe.did(PE.matmul(bank[4 + n][:, 0:(hi - lo) * P], k.w1n[:],
                                           ht[:, lo:hi, :].rearrange("p t d -> p (t d)"), start=True, stop=True))
                    wait(A, m)
                    hid.append(k.act.did(A.activation(h[:, lo:hi, :].rearrange("p t d -> p (t d)"),
                                                      bank[4 + n][:, 0:(hi - lo) * P], ACT.Relu, bias=k.b1n[:])))
                m = None
                for part, ps, done in k.project([(h, k.w2n[:])], hid, (2, 3)):
                    wait(V, done)
                    ms = k.v.did(V.tensor_tensor(z[:, part, :], ps, x1[:, part, :], ALU.add))
                wait(V, ms)
                m = k.v.did(V.tensor_tensor(z[:], z[:], tiles_of(k.b2n[:]), ALU.add))
                m = k.moment(z[:], [m], RMS_EPS, 2)
                wait(V, m)
                m = k.v.did(V.tensor_tensor(z[:], z[:], spread(k.small[:, 2, :]), ALU.mult))
                wait(V, m)
                m = k.v.did(V.tensor_tensor(z[:], z[:], tiles_of(k.rms[:]), ALU.mult))
                wait(V, m)
                m = k.v.did(V.tensor_tensor(z[:], z[:], x1[:], ALU.add))
                m = k.layernorm(z[:], h[:], [m])
                wait(A, m)
                carry(A, k.s_carry)
                mx = k.act.did(A.activation(x[:, own, :], h[:], ACT.Copy))
                ready = k.transpose(h, ht, [m], (0, 1))
                out = []
                for part, ps, done in k.project([(ht, k.up[:])], ready, (2, 3)):
                    wait(V, done)
                    out.append(k.v.did(V.tensor_copy(t2[:, part, :], ps)))
                wait(SP, *out)
                k.out.did(SP.dma_start(by_tile(up_t)[:, own, :], t2[:]))
            return body
        node_phase("after1", make, weights)

    def after2(at_dst):
        def weights(ctx, k):
            k.raw = k.sb("raw", [P, 2, MUL])
            k.wo = k.sb("wo", [P, 2, D])
            k.w3, k.b3 = k.sb("w3", [P, 3 * D]), k.sb("b3", [P, 3 * D])
            k.prepare(G, G.memset(k.wo[:], 0.0))
            k.prepare(G, G.memset(k.raw[:], 0.0))
            k.prepared()
            pairs = [(k.raw[0:2 * MUL, 0, :], a["L2_gnn_W_out0"]), (k.raw[2 * MUL:P, 0, :], a["L2_gnn_W_out1"]),
                     (k.raw[0:2 * MUL, 1, :], a["L2_gnn_W_out1"]), (k.raw[2 * MUL:P, 1, :], a["L2_gnn_W_out1"])]
            for n, name in enumerate(("src", "v", "dst")):
                pairs.append((k.w3[:, n * D:(n + 1) * D], a[f"W_{name}_t"]))
                pairs.append((k.b3[:, n * D:(n + 1) * D], vec_row(a[f"L3_gnn_b_{name}"])))
            return pairs

        def make(ctx, k):
            scale = (2 * MUL) ** -0.5 / AVG
            k.prepare(V, V.tensor_scalar(k.wo[0:2 * MUL, 0, 0:MUL], k.raw[0:2 * MUL, 0, :], scale, None, ALU.mult))
            for c, (lo, half) in enumerate(((2 * MUL, 0), (0, 1), (2 * MUL, 1))):
                for row, factor in ((lo, scale * SQ3), (lo + MUL, scale)):
                    k.prepare(V, V.tensor_scalar(k.wo[row:row + MUL, half, MUL + c:P:3],
                                                 k.raw[row:row + MUL, half, :], factor, None, ALU.mult))
            k.prepared()
            h, ht, ht2, z, xt = (k.sb(n, [P, BLOCK, D]) for n in ("h", "ht", "ht2", "z", "xt"))
            t3 = k.sb("t3", [P, BLOCK, 2 * D])

            def body(b):
                own = ds(b * BLOCK, BLOCK)
                m = k.act.did(A.activation(h[:], acc[:, own, 0:D], ACT.Copy))
                mb = k.act.did(A.activation(z[:], acc[:, own, D:2 * D], ACT.Copy))
                ready = k.transpose(h, ht, [m], (0, 1)) + k.transpose(z, ht2, [mb], (2, 3))
                for part, ps, done in k.project([(ht, k.wo[:, 0, :]), (ht2, k.wo[:, 1, :])], ready, (4, 5)):
                    wait(V, done)
                    m = k.v.did(V.tensor_tensor(z[:, part, :], ps, x[:, ds(b * BLOCK + part.start,
                                                                         part.stop - part.start), :], ALU.add))
                m = k.layernorm(z[:], h[:], [m])
                wait(A, m)
                carry(A, k.s_carry)
                k.act.did(A.activation(x[:, own, :], h[:], ACT.Copy))
                ready = k.transpose(h, xt, [m], (0, 1))
                done = project3(k, xt, ready, k.w3, k.b3, t3, at_dst[:, own, 0:D])
                wait(SP, *done)
                k.out.did(SP.dma_start(by_tile(fsv_t)[:, own, :], t3[:]))
                k.out.did(SP.dma_start(by_tile(fs_t)[:, own, :], t3[:, :, 0:D]))
            return body
        node_phase("after2", make, weights)

    def maxima(at_dst):
        def make(ctx, k):
            s, r = k.sb("s", [P, BLOCK, D]), k.sb("r", [P, BLOCK, D])

            def body(b):
                own = ds(b * BLOCK, BLOCK)
                m = k.v.did(V.tensor_tensor(s[:], acc[:, own, 0:D], at_dst[:, own, 0:D], ALU.add))
                wait(A, m)
                m = k.act.did(A.activation(r[:], s[:], ACT.Relu, scale=0.8))
                wait(V, m)
                k.v.did(V.scalar_tensor_tensor(out=at_dst[:, own, D:2 * D], in0=s[:], scalar=0.2, in1=r[:],
                                               op0=ALU.mult, op1=ALU.add))
            return body
        node_phase("maxima", make)

    def after3():
        def make(ctx, k):
            z, s, y = (k.sb(n, [P, BLOCK, D]) for n in ("z", "s", "y"))

            def body(b):
                own = ds(b * BLOCK, BLOCK)
                m = k.v.did(V.tensor_scalar(s[:], acc[:, own, D:2 * D], 1e-30, None, ALU.max))
                wait(V, m)
                m = k.v.did(V.reciprocal(z[:], s[:]))
                wait(V, m)
                m = k.v.did(V.tensor_tensor(z[:], z[:], acc[:, own, 0:D], ALU.mult))
                wait(V, m)
                m = k.v.did(V.tensor_tensor(z[:], z[:], x[:, own, :], ALU.add))
                m = k.layernorm(z[:], y[:], [m])
                wait(A, m)
                carry(A, k.s_carry)
                k.act.did(A.activation(x[:, own, :], y[:], ACT.Copy))
            return body
        node_phase("after3", make)
        with nc.semaphore("written") as written:
            SP.dma_start(a["out"][0:FULL_TILES * P, :].rearrange("(t p) d -> p t d", p=P),
                         x[:, 0:FULL_TILES, :]).then_inc(written, 16)
            SP.dma_start(a["out"][FULL_TILES * P:N_NODES, :], x[0:REST, FULL_TILES, :]).then_inc(written, 16)
            SP.wait_ge(written, 32)

    class EdgePass:

        def __init__(self, ctx, table, width, sums, local, fixed=()):
            self.ctx, self.sb, self.sem, self.table, self.sums = ctx, ctx.sb, ctx.sem, table, sums
            self.src = self.sb("src", [P, N_ITEMS], I32)
            self.local = self.sb("local", [P, N_ITEMS])
            self.index = self.sb("index", [P, SLOTS, GROUP], I32)
            self.rows = self.sb("rows", [P, SLOTS, GROUP, width])
            self.sel = self.sb("sel", [P, SLOTS, GROUP, P])
            self.per_bank = 2 if 2 * sums <= 512 else 1
            self.s_index = [self.sem(f"index{u}") for u in range(SLOTS)]
            self.s_rows = [self.sem(f"rows{u}") for u in range(SLOTS)]
            self.s_sel = self.sem("sel")
            self.s_sums = [self.sem(f"sums{k}") for k in range(GROUP // self.per_bank)]
            self.s_added = [self.sem(f"added{i}") for i in range(GROUP)]
            self.s_load = self.sem("load")
            self.s_carry = self.sem("carry")
            self.loads = 0
            self.zeroed = self.sem("zeroed")
            self.load([(self.src[:], src_d[:, 0:N_ITEMS]), (self.local[:], local[:, 0:N_ITEMS])] + list(fixed))
            G.memset(acc[:, :, 0:sums], 0.0).then_inc(self.zeroed, 1)
            V.wait_ge(self.zeroed, 1)

        def load(self, pairs):
            for to, of in pairs:
                SP.dma_start(to, of).then_inc(self.s_load, 16)
                self.loads += 16
            for e in ENGINES:
                e.wait_ge(self.s_load, self.loads)

        def gather(self, g, s_free):
            u = g.slot
            if g.old(SLOTS):
                SP.wait_ge(self.s_rows[u], g.round * 64)
            SP.dma_start(self.index[:, u, :], self.src[:, ds(g.n * GROUP, GROUP)]).then_inc(self.s_index[u], 16)
            G.wait_ge(self.s_index[u], (g.round + 1) * 16)
            if g.old(SLOTS):
                G.wait_ge(s_free, g.upto(-SLOTS))
            carry(G, self.s_carry)
            for i in range(GROUP):
                G.indirect_dma_start(out=self.rows[:, u, i, :], out_offset=None, in_=self.table,
                                     in_offset=bass.IndirectOffsetOnAxis(ap=self.index[:, u, i:i + 1], axis=0)
                                     ).then_inc(self.s_rows[u], 16)

        def have_rows(self, engine, g):
            engine.wait_ge(self.s_rows[g.slot], (g.round + 1) * 64)

        def summed(self, engine, g, k):
            engine.wait_ge(self.s_sums[-1], g.upto(k))

        def select(self, g):
            if g.old(SLOTS):
                self.summed(V, g, -SLOTS)
            V.tensor_tensor(self.sel[:, g.slot],
                            node_iota[:].unsqueeze(1).to_broadcast([P, GROUP, P]),
                            self.local[:, ds(g.n * GROUP, GROUP)].unsqueeze(2).to_broadcast([P, GROUP, P]),
                            ALU.is_equal).then_inc(self.s_sel, 1)

        def place(self, g, i):
            if self.per_bank == 1:
                return i, 0
            return 2 * g.r2 + i // 2, i % 2 * self.sums

        def scatter(self, g, parts):
            for i in range(GROUP):
                n_bank, col = self.place(g, i)
                if i % self.per_bank == 0 and g.old(self.per_bank):
                    PE.wait_ge(self.s_added[i + self.per_bank - 1], g.upto(-self.per_bank))
                for at, rows in parts(i):
                    m = PE.matmul(bank[n_bank][:, col + at:col + at + rows.shape[1]], self.sel[:, g.slot, i, :],
                                  rows, start=True, stop=True)
                if (i + 1) % self.per_bank == 0:
                    m.then_inc(self.s_sums[i // self.per_bank], 1)

        def add(self, i):
            def stage(g):
                if i == 0:
                    self.tiles_to = self.tiles(g, DVE_ENGINE)
                n_bank, col = self.place(g, i)
                if i % self.per_bank == 0:
                    V.wait_ge(self.s_sums[i // self.per_bank], g.upto(0))
                if i:
                    V.wait_ge(self.s_added[i - 1], g.upto(0))
                elif g.old(1):
                    V.wait_ge(self.s_added[GROUP - 1], g.upto(-1))
                to = acc[:, ds(self.tiles_to[i], 1), 0:self.sums]
                V.tensor_tensor(to, to, bank[n_bank][:, col:col + self.sums].unsqueeze(1), ALU.add
                                ).then_inc(self.s_added[i], 1)
            return stage

        def tiles(self, g, engine):
            _, tiles = nc.values_load_multi_w_load_instructions(
                tile_of[0:1, ds(g.n * GROUP, GROUP)], engines=(engine,), min_val=0, max_val=N_TILES - 1,
                skip_runtime_bounds_check_because=CLIPPED)
            return tiles

        def run(self, stages):
            pipeline(nc, stages)
            for e in ENGINES:
                e.wait_ge(self.s_added[GROUP - 1], N_GROUPS)
            self.ctx.end()

    class Turned:

        def __init__(self, ps, n_bank, s_used):
            self.ps, self.bank, self.s_used = ps, n_bank, s_used
            self.sel_t = ps.sb("sel_t", [P, 2, GROUP, P])
            self.s_t = ps.sem("t")
            self.s_copied = ps.sem("copied")

        def turn(self, g):
            PE.wait_ge(self.ps.s_sel, g.upto(0))
            if g.old(1):
                PE.wait_ge(self.s_copied, g.upto(-1))
            for i in range(GROUP):
                m = PE.transpose(bank[self.bank][:, i * P:(i + 1) * P], self.ps.sel[:, g.slot, i, :], ident[:])
            m.then_inc(self.s_t, 1)
            A.wait_ge(self.s_t, g.upto(0))
            if g.old(2):
                A.wait_ge(self.s_used, g.upto(-2))
            A.activation(self.sel_t[:, g.r2].rearrange("p i e -> p (i e)"), bank[self.bank], ACT.Copy
                         ).then_inc(self.s_copied, 1)

    def quad(b, width=P):
        return bank[b][:, 0:GROUP * width].rearrange("p (i d) -> p i d", i=GROUP)

    def edges0(queries):
        with Phase(nc, "e0") as ctx:
            ps = EdgePass(ctx, kv_t, 2 * D, W0, local_d)
            B_T, B_Q = 4, (5, 6)
            prod = ps.sb("prod", [P, GROUP, D])
            dots = ps.sb("dots", [P, GROUP * HEADS0])
            clip = ps.sb("clip", [P, 2, GROUP * HEADS0])
            msg = ps.sb("msg", [P, 2, GROUP, W0])
            s_q, s_prod, s_dots, s_clip, s_score, s_msg, ones = (
                ps.sem(n) for n in ("q", "prod", "dots", "clip", "score", "msg", "ones"))
            turned = Turned(ps, B_T, s_q)
            V.memset(msg[:, :, :, W0 - 1], 1.0).then_inc(ones, 1)
            PE.wait_ge(ones, 1)

            def gather(g):
                ps.gather(g, s_msg)

            def queries_to_edges(g):
                tiles = ps.tiles(g, PE_ENGINE)
                PE.wait_ge(turned.s_copied, g.upto(0))
                if g.old(2):
                    PE.wait_ge(s_prod, g.upto(-2))
                for i in range(GROUP):
                    m = PE.matmul(bank[B_Q[g.r2]][:, i * P:(i + 1) * P], turned.sel_t[:, g.r2, i, :],
                                  queries[:, ds(tiles[i], 1), :].rearrange("p a d -> p (a d)"),
                                  start=True, stop=True)
                m.then_inc(s_q, 1)

            def products(g):
                ps.have_rows(V, g)
                V.wait_ge(s_q, g.upto(0))
                if g.old(1):
                    V.wait_ge(s_dots, g.upto(-1))
                V.tensor_tensor(prod[:], ps.rows[:, g.slot, :, 0:D], quad(B_Q[g.r2]), ALU.mult
                                ).then_inc(s_prod, 1)

            def dot(g):
                V.wait_ge(s_prod, g.upto(0))
                if g.old(1):
                    V.wait_ge(s_clip, g.upto(-1))
                V.tensor_reduce(dots[:], prod[:].rearrange("p i (h c) -> p (i h) c", c=HDIM0), AX.X, ALU.add
                                ).then_inc(s_dots, 1)

            def score(g):
                V.wait_ge(s_dots, g.upto(0))
                if g.old(2):
                    V.wait_ge(s_score, g.upto(-2))
                V.tensor_scalar(clip[:, g.r2, :], dots[:], -20.0, 20.0, ALU.max, ALU.min).then_inc(s_clip, 1)
                A.wait_ge(s_clip, g.upto(0))
                if g.old(2):
                    ps.summed(A, g, -2)
                A.activation(msg[:, g.r2, :, D:D + HEADS0], clip[:, g.r2, :].rearrange("p (i h) -> p i h", i=GROUP),
                             ACT.Exp, scale=0.25).then_inc(s_score, 1)

            def message(g):
                V.wait_ge(s_score, g.upto(0))
                V.tensor_tensor(msg[:, g.r2, :, 0:D].rearrange("p i (h c) -> p i h c", c=HDIM0),
                                ps.rows[:, g.slot, :, D:2 * D].rearrange("p i (h c) -> p i h c", c=HDIM0),
                                msg[:, g.r2, :, D:D + HEADS0].unsqueeze(3).to_broadcast([P, GROUP, HEADS0, HDIM0]),
                                ALU.mult).then_inc(s_msg, 1)

            def sums(g):
                PE.wait_ge(s_msg, g.upto(0))
                ps.scatter(g, lambda i: [(0, msg[:, g.r2, i, :])])

            ps.run([(0, gather), (2, queries_to_edges), (1, turned.turn), (4, ps.add(0)), (3, message),
                    (4, ps.add(1)), (2, products), (4, ps.add(2)), (2, dot), (4, ps.add(3)), (2, score),
                    (0, ps.select), (3, sums)])

    def edges1():
        with Phase(nc, "e1") as ctx:
            w1 = ctx.sb("w1", [ED + 1, D])
            chunk_of = ctx.sb("chunk", [1, ITEMS_PAD], I32)
            ps = EdgePass(ctx, x1_t, D + 1, W1, local_d,
                          [(w1[0:ED, :], a["L1_gnn_W1e"]),
                           (w1[ED:ED + 1, :], a["L1_gnn_b1e"].rearrange("(a n) -> a n", a=1)),
                           (chunk_of[:], item_rows[1:2, :])])
            attr = ps.sb("attr", [ED + 1, SLOTS, GROUP, P])
            hid = ps.sb("hid", [P, 2, GROUP, D])
            s_attr = [ps.sem(f"attr{u}") for u in range(SLOTS)]
            s_h, s_relu, ones = ps.sem("h"), ps.sem("relu"), ps.sem("ones")
            B_H = (4, 5)
            V.memset(attr[ED:ED + 1, :, :, :], 1.0).then_inc(ones, 1)
            PE.wait_ge(ones, 1)

            def gather(g):
                ps.gather(g, ps.s_sums[-1])
                u = g.slot
                _, chunks = nc.values_load_multi_w_load_instructions(
                    chunk_of[0:1, ds(g.n * GROUP, GROUP)], engines=(SP_ENGINE,), min_val=0, max_val=N_CHUNKS - 1,
                    skip_runtime_bounds_check_because=CLIPPED)
                if g.old(SLOTS):
                    SP.wait_ge(s_h, g.upto(-SLOTS))
                for i in range(GROUP):
                    SP.dma_start(attr[0:ED, u, i, :], a["attr_rows"][ds(chunks[i], 1), :, :]
                                 .rearrange("a k e -> (a k) e")).then_inc(s_attr[u], 16)

            def hidden(g):
                PE.wait_ge(s_attr[g.slot], (g.round + 1) * 64)
                if g.old(2):
                    PE.wait_ge(s_relu, g.upto(-2))
                for i in range(GROUP):
                    m = PE.matmul(bank[B_H[g.r2]][:, i * P:(i + 1) * P], attr[:, g.slot, i, :], w1[:],
                                  start=True, stop=True)
                m.then_inc(s_h, 1)
                A.wait_ge(s_h, g.upto(0))
                ps.have_rows(A, g)
                if g.old(2):
                    ps.summed(A, g, -2)
                for i in range(GROUP):
                    m = A.activation(hid[:, g.r2, i, :], bank[B_H[g.r2]][:, i * P:(i + 1) * P], ACT.Relu,
                                     scale=ps.rows[:, g.slot, i, D:D + 1])
                m.then_inc(s_relu, 1)

            def sums(g):
                PE.wait_ge(s_relu, g.upto(0))
                PE.wait_ge(ps.s_sel, g.upto(0))
                ps.have_rows(PE, g)
                ps.scatter(g, lambda i: [(0, ps.rows[:, g.slot, i, :]), (D + 1, hid[:, g.r2, i, :])])

            ps.run([(0, gather), (0, ps.select), (0, hidden), (1, sums), (1, ps.add(0)), (1, ps.add(1)),
                    (1, ps.add(2)), (1, ps.add(3))])

    def edges2():
        with Phase(nc, "e2") as ctx:
            w0 = ctx.sb("w0", [2 * NB, 2 * RH])
            b0 = ctx.sb("b0", [2 * RH, 1])
            w1 = ctx.sb("w1", [2 * RH, 2, RH])
            b1 = ctx.sb("b1", [RH, 1])
            w2 = ctx.sb("w2", [RH + 1, D])
            rhat = ctx.sb("rhat", [P, N_ITEMS, 3])
            clear = ctx.sem("clear")
            G.memset(w0[:], 0.0).then_inc(clear, 1)
            G.memset(w1[:], 0.0).then_inc(clear, 1)
            SP.wait_ge(clear, 2)
            fixed = [(w0[h * NB:(h + 1) * NB, h * RH:(h + 1) * RH], a["L2_gnn_mlp_w0"]) for h in range(2)]
            fixed += [(b0[h * RH:(h + 1) * RH, :], vec_col(a["L2_gnn_mlp_b0"])) for h in range(2)]
            fixed += [(w1[h * RH:(h + 1) * RH, h, :], a["L2_gnn_mlp_w1"]) for h in range(2)]
            fixed += [(b1[:], vec_col(a["L2_gnn_mlp_b1"])), (w2[0:RH, :], a["L2_gnn_mlp_w2"]),
                      (w2[RH:RH + 1, :], a["L2_gnn_mlp_b2"].rearrange("(a n) -> a n", a=1)),
                      (rhat[:], rhat_d[:, 0:N_ITEMS, :])]
            ps = EdgePass(ctx, up_t, D, W2, local_d, fixed)
            emb = ps.sb("emb", [2 * NB, SLOTS, 2 * P])
            h1 = ps.sb("h1", [2 * RH, 2, 2 * P])
            h2 = ps.sb("h2", [RH + 1, 2, 4 * P])
            u_c = ps.sb("u_c", [P, GROUP, 3, MUL])
            u = ps.sb("u", [P, GROUP, MUL])
            msg = ps.sb("msg", [P, 2, GROUP, W2 + MUL])
            s_emb = [ps.sem(f"emb{n}") for n in range(SLOTS)]
            s_h1, s_silu1, s_h2, s_silu2, s_w = (ps.sem(n) for n in ("h1", "silu1", "h2", "silu2", "w"))
            s_by_s, s_u_c, s_u, s_msg, ones = (ps.sem(n) for n in ("by_s", "u_c", "u", "msg", "ones"))
            B_H1, B_H2, B_W = 4, 5, (6, 7)
            V.memset(h2[RH:RH + 1, :, :], 1.0).then_inc(ones, 1)
            PE.wait_ge(ones, 1)

            def gather(g):
                ps.gather(g, s_msg)
                if g.old(SLOTS):
                    SP.wait_ge(s_h1, g.upto(-SLOTS))
                SP.dma_start(emb[:, g.slot, :],
                             emb_d[ds(g.n * 2, 2), :, :, :].rearrange("a j b e -> (a j) (b e)")
                             ).then_inc(s_emb[g.slot], 16)

            def hidden1(g):
                PE.wait_ge(s_emb[g.slot], (g.round + 1) * 16)
                if g.old(1):
                    PE.wait_ge(s_silu1, g.upto(-1))
                PE.matmul(bank[B_H1][:, 0:2 * P], w0[:], emb[:, g.slot, :], start=True, stop=True
                          ).then_inc(s_h1, 1)
                A.wait_ge(s_h1, g.upto(0))
                if g.old(2):
                    A.wait_ge(s_h2, g.upto(-2))
                A.activation(h1[:, g.r2, :], bank[B_H1][:, 0:2 * P], ACT.Silu, bias=b0[:]).then_inc(s_silu1, 1)

            def hidden2(g):
                PE.wait_ge(s_silu1, g.upto(0))
                if g.old(1):
                    PE.wait_ge(s_silu2, g.upto(-1))
                for h in range(2):
                    m = PE.matmul(bank[B_H2][0:RH, h * 2 * P:(h + 1) * 2 * P], w1[:, h, :], h1[:, g.r2, :],
                                  start=True, stop=True)
                m.then_inc(s_h2, 1)
                A.wait_ge(s_h2, g.upto(0))
                if g.old(2):
                    A.wait_ge(s_w, g.upto(-2))
                A.activation(h2[0:RH, g.r2, :], bank[B_H2][0:RH, :], ACT.Silu, bias=b1[:]).then_inc(s_silu2, 1)

            def weights(g):
                PE.wait_ge(s_silu2, g.upto(0))
                if g.old(2):
                    PE.wait_ge(s_msg, g.upto(-2))
                for i in range(GROUP):
                    m = PE.matmul(bank[B_W[g.r2]][:, i * P:(i + 1) * P], h2[:, g.r2, i * P:(i + 1) * P], w2[:],
                                  start=True, stop=True)
                m.then_inc(s_w, 1)

            def scalars(g):
                return ps.rows[:, g.slot, :, 0:MUL]

            def vectors(g):
                return ps.rows[:, g.slot, :, MUL:].rearrange("p i (c k) -> p i c k", c=3)

            def direction(g):
                return rhat[:, ds(g.n * GROUP, GROUP), :].unsqueeze(3).to_broadcast([P, GROUP, 3, MUL])

            def three(t):
                return t.unsqueeze(2).to_broadcast([P, GROUP, 3, MUL])

            def by_direction(g):
                ps.have_rows(V, g)
                if g.old(1):
                    V.wait_ge(s_u, g.upto(-1))
                V.tensor_tensor(u_c[:], vectors(g), direction(g), ALU.mult).then_inc(s_u_c, 1)

            def by_scalars(g):
                V.wait_ge(s_w, g.upto(0))
                if g.old(2):
                    ps.summed(V, g, -2)
                    V.wait_ge(s_msg, g.upto(-2))
                V.tensor_tensor(msg[:, g.r2, :, 0:MUL], quad(B_W[g.r2])[:, :, 0:MUL], scalars(g), ALU.mult)
                V.tensor_tensor(msg[:, g.r2, :, W2:], quad(B_W[g.r2])[:, :, MUL:2 * MUL], scalars(g), ALU.mult
                                ).then_inc(s_by_s, 1)

            def dot(g):
                V.wait_ge(s_u_c, g.upto(0))
                if g.old(1):
                    V.wait_ge(s_msg, g.upto(-1))
                V.tensor_reduce(u[:], u_c[:].rearrange("p i c k -> p i k c"), AX.X, ALU.add).then_inc(s_u, 1)

            def by_c(g):
                return msg[:, g.r2, :, 2 * MUL:W2].rearrange("p i (c s k) -> p i c s k", c=3, s=2)

            def m1(g):
                V.wait_ge(s_by_s, g.upto(0))
                V.tensor_tensor(by_c(g)[:, :, :, 0, :], three(msg[:, g.r2, :, W2:]), direction(g), ALU.mult)

            def m2(g):
                V.tensor_tensor(by_c(g)[:, :, :, 1, :], three(quad(B_W[g.r2])[:, :, 2 * MUL:3 * MUL]), vectors(g),
                                ALU.mult)

            def m3(g):
                V.wait_ge(s_u, g.upto(0))
                V.tensor_tensor(msg[:, g.r2, :, MUL:2 * MUL], quad(B_W[g.r2])[:, :, 3 * MUL:], u[:], ALU.mult
                                ).then_inc(s_msg, 1)

            def sums(g):
                PE.wait_ge(s_msg, g.upto(0))
                PE.wait_ge(ps.s_sel, g.upto(0))
                ps.scatter(g, lambda i: [(0, msg[:, g.r2, i, 0:W2])])

            ps.run([(0, gather), (3, weights), (4, sums), (2, hidden2), (1, hidden1),
                    (3, by_direction), (3, ps.select), (3, by_scalars), (3, dot), (4, ps.add(0)), (3, m1),
                    (4, ps.add(1)), (3, m2), (4, ps.add(2)), (3, m3), (4, ps.add(3))])

    def edges3_max():
        with Phase(nc, "e3m") as ctx:
            ps = EdgePass(ctx, fs_t, D, D, local_last_d)
            reset = ps.sb("reset", [P, SLOTS, GROUP * P])
            run = ps.sb("run", [P, 2, GROUP * P])
            back = ps.sb("back", [P, 2, GROUP, P])
            s_reset = [ps.sem(f"reset{u}") for u in range(SLOTS)]
            s_f, s_run, s_b, s_back, start = (ps.sem(n) for n in ("f", "run", "b", "back", "start"))
            B_F, B_B = (4, 5), (6, 7)
            V.memset(run[:], LOW).then_inc(start, 1)
            V.wait_ge(start, 1)

            def gather(g):
                ps.gather(g, s_f)
                if g.old(SLOTS):
                    SP.wait_ge(s_run, g.upto(-SLOTS))
                SP.dma_start(reset[:, g.slot, :], reset_d[ds(g.n, 1), :].to_broadcast([P, GROUP * P])
                             ).then_inc(s_reset[g.slot], 16)

            def forward(g):
                ps.have_rows(PE, g)
                if g.old(2):
                    PE.wait_ge(s_run, g.upto(-2))
                for i in range(GROUP):
                    m = PE.transpose(bank[B_F[g.r2]][:, i * P:(i + 1) * P], ps.rows[:, g.slot, i, :], ident[:])
                m.then_inc(s_f, 1)
                ps.select(g)
                V.wait_ge(s_f, g.upto(0))
                V.wait_ge(s_reset[g.slot], (g.round + 1) * 16)
                if g.old(1):
                    V.wait_ge(s_run, g.upto(-1))
                if g.old(2):
                    V.wait_ge(s_b, g.upto(-2))
                V.tensor_tensor_scan(run[:, g.r2, :], reset[:, g.slot, :], bank[B_F[g.r2]],
                                     run[:, 1 - g.r2, GROUP * P - 1:GROUP * P], ALU.add, ALU.max
                                     ).then_inc(s_run, 1)

            def backward(g):
                PE.wait_ge(s_run, g.upto(0))
                if g.old(2):
                    PE.wait_ge(s_back, g.upto(-2))
                for i in range(GROUP):
                    m = PE.transpose(bank[B_B[g.r2]][:, i * P:(i + 1) * P], run[:, g.r2, i * P:(i + 1) * P],
                                     ident[:])
                m.then_inc(s_b, 1)
                A.wait_ge(s_b, g.upto(0))
                if g.old(2):
                    ps.summed(A, g, -2)
                A.activation(back[:, g.r2].rearrange("p i d -> p (i d)"), bank[B_B[g.r2]], ACT.Copy
                             ).then_inc(s_back, 1)

            def sums(g):
                PE.wait_ge(s_back, g.upto(0))
                PE.wait_ge(ps.s_sel, g.upto(0))
                ps.scatter(g, lambda i: [(0, back[:, g.r2, i, :])])

            ps.run([(0, gather), (0, forward), (1, backward), (2, sums), (2, ps.add(0)), (2, ps.add(1)),
                    (2, ps.add(2)), (2, ps.add(3))])

    def edges3(at_dst):
        with Phase(nc, "e3") as ctx:
            ps = EdgePass(ctx, fsv_t, 2 * D, W3, local_d)
            B_T, B_AM = 4, 5
            relu = ps.sb("relu", [P, GROUP, D])
            diff = ps.sb("diff", [P, 2, GROUP, D])
            msg = ps.sb("msg", [P, 2, GROUP, W3])
            s_a, s_relu, s_e, s_diff, s_exp, s_msg = (ps.sem(n) for n in
                                                      ("a", "relu", "e", "diff", "exp", "msg"))
            turned = Turned(ps, B_T, s_a)
            both = banks[:, B_AM:B_AM + 2, :].rearrange("p b (i d) -> p (b i) d", i=2)
            at_edge, max_edge = both[:, :, 0:D], both[:, :, D:2 * D]

            def gather(g):
                if g.old(SLOTS):
                    G.wait_ge(s_a, g.upto(-SLOTS))
                ps.gather(g, s_msg)

            def to_edges(g):
                tiles = ps.tiles(g, PE_ENGINE)
                PE.wait_ge(turned.s_copied, g.upto(0))
                ps.have_rows(PE, g)
                if g.old(1):
                    PE.wait_ge(s_diff, g.upto(-1))
                for i in range(GROUP):
                    b = bank[B_AM + i // 2][:, i % 2 * 2 * D:(i % 2 + 1) * 2 * D]
                    PE.matmul(b, turned.sel_t[:, g.r2, i, :],
                              at_dst[:, ds(tiles[i], 1), :].rearrange("p a d -> p (a d)"), start=True, stop=False)
                    m = PE.matmul(b[:, 0:D], ident[:], ps.rows[:, g.slot, i, 0:D], start=False, stop=True)
                m.then_inc(s_a, 1)
                A.wait_ge(s_a, g.upto(0))
                if g.old(1):
                    A.wait_ge(s_e, g.upto(-1))
                A.activation(relu[:], at_edge, ACT.Relu, scale=0.8).then_inc(s_relu, 1)

            def leaky(g):
                V.wait_ge(s_relu, g.upto(0))
                if g.old(2):
                    V.wait_ge(s_exp, g.upto(-2))
                V.scalar_tensor_tensor(out=diff[:, g.r2], in0=at_edge, scalar=0.2, in1=relu[:],
                                       op0=ALU.mult, op1=ALU.add).then_inc(s_e, 1)

            def exps(g):
                V.wait_ge(s_e, g.upto(0))
                V.tensor_tensor(diff[:, g.r2], diff[:, g.r2], max_edge, ALU.subtract).then_inc(s_diff, 1)
                A.wait_ge(s_diff, g.upto(0))
                if g.old(2):
                    ps.summed(A, g, -2)
                A.activation(msg[:, g.r2, :, D:2 * D], diff[:, g.r2], ACT.Exp).then_inc(s_exp, 1)

            def message(g):
                V.wait_ge(s_exp, g.upto(0))
                V.tensor_tensor(msg[:, g.r2, :, 0:D], ps.rows[:, g.slot, :, D:2 * D], msg[:, g.r2, :, D:2 * D],
                                ALU.mult).then_inc(s_msg, 1)

            def sums(g):
                PE.wait_ge(s_msg, g.upto(0))
                ps.scatter(g, lambda i: [(0, msg[:, g.r2, i, :])])

            ps.run([(0, gather), (2, to_edges), (1, turned.turn), (4, ps.add(0)), (3, message), (4, ps.add(1)),
                    (2, leaky), (4, ps.add(2)), (2, exps), (4, ps.add(3)), (0, ps.select), (3, sums)])

    with root:
        setup()
        with nc.sbuf_tensor("queries", [P, N_TILES, D], F32) as queries:
            project0(queries)
            edges0(queries)
        with nc.sbuf_tensor("inv_root_deg", [P, N_TILES], F32) as inv_root_deg:
            after0(inv_root_deg)
            edges1()
            after1(inv_root_deg)
        edges2()
        with nc.sbuf_tensor("at_dst", [P, N_TILES, 2 * D], F32) as at_dst:
            after2(at_dst)
            edges3_max()
            maxima(at_dst)
            edges3(at_dst)
        after3()


_WEIGHTS = ["L0_gnn_Wq", "L0_gnn_bq", "L0_gnn_Wk", "L0_gnn_bk", "L0_gnn_Wv", "L0_gnn_bv",
            "L1_gnn_W1n", "L1_gnn_b1n", "L1_gnn_W2n", "L1_gnn_b2n", "L1_gnn_W1e", "L1_gnn_b1e",
            "L1_gnn_W2e", "L1_gnn_b2e", "L1_gnn_rms_w", "L2_gnn_W_up0", "L2_gnn_W_up1",
            "L2_gnn_mlp_w0", "L2_gnn_mlp_b0", "L2_gnn_mlp_w1", "L2_gnn_mlp_b1", "L2_gnn_mlp_w2",
            "L2_gnn_mlp_b2", "L2_gnn_W_out0", "L2_gnn_W_out1", "L3_gnn_b_src", "L3_gnn_b_dst", "L3_gnn_b_v"]


def kernel(**inputs):
    import numpy as np
    import concourse.bacc as bacc
    from concourse import mybir as _mybir
    from concourse.bass_utils import run_bass_kernel_spmd as run

    get = lambda name: np.asarray(inputs[name])
    pad = N_CHUNKS * P - N_EDGES

    def chunks(v, fill):
        v = np.concatenate([v, np.full((pad,) + v.shape[1:], fill, v.dtype)])
        return v.reshape((N_CHUNKS, P) + v.shape[1:])

    dst = get("dst")
    ends = np.concatenate([np.full((1,), -1, dst.dtype), dst, np.full((pad + 1,), FAR, dst.dtype)])
    arrays = {
        "x": get("x"),
        "dst_rows": np.ascontiguousarray(np.stack([ends[c * P:c * P + P + 2] for c in range(N_CHUNKS)])),
        "src_rows": chunks(get("src"), 0),
        "vec_rows": np.ascontiguousarray(chunks(get("edge_attr_3"), 0).transpose(0, 2, 1)).reshape(N_CHUNKS, 3 * P),
        "length_rows": chunks(get("edge_weight"), 0),
        "attr_rows": np.ascontiguousarray(chunks(get("edge_attr_64"), 0).transpose(0, 2, 1)),
        "gin_eps": get("L1_gnn_gin_eps").reshape(1, 1),
        "W_src_t": np.ascontiguousarray(get("L3_gnn_W_src").T),
        "W_dst_t": np.ascontiguousarray(get("L3_gnn_W_dst").T),
        "W_v_t": np.ascontiguousarray(get("L3_gnn_W_v").T),
    }
    arrays.update({name: get(name) for name in _WEIGHTS})

    nc = bacc.Bacc("TRN2", target_bir_lowering=False, num_devices=1)
    aps = {name: nc.dram_tensor(f"in_{name}", v.shape, _mybir.dt.from_np(v.dtype), kind="ExternalInput").ap()
           for name, v in arrays.items()}
    aps["out"] = nc.dram_tensor("out_x", (N_NODES, D), F32, kind="ExternalOutput").ap()
    build(nc, aps)
    r = run(nc, [{f"in_{name}": np.ascontiguousarray(v) for name, v in arrays.items()}], core_ids=[0])
    return r.results[0]["out_x"]
```

```python
from contextlib import ExitStack

import concourse.bass as bass
from concourse import mybir

P = 128
N_NODES = 6250
N_EDGES = 106250
D = 128
BLOCK = 5
HALF = 3
STREAMS = 2
N_TILES = -(-N_NODES // (P * BLOCK * STREAMS)) * BLOCK * STREAMS
N_CHUNKS = -(-N_EDGES // P)
GROUP = 4
SLOTS = 4
N_GROUPS = -(-(N_CHUNKS + N_TILES - 1) // (GROUP * SLOTS)) * SLOTS
N_ITEMS = GROUP * N_GROUPS
ITEM_TILES = -(-N_ITEMS // P)
ITEMS_PAD = ITEM_TILES * P
N_BLOCKS = N_TILES // BLOCK
FULL_TILES = N_NODES // P
REST = N_NODES - FULL_TILES * P
HEADS0, HDIM0 = 8, 16
ED = 64
MUL, NB, RH = 32, 8, 64
SQ3 = 3.0 ** 0.5
AVG = 16.0
FAR = 1 << 20
LOW = -3.0e38
LN_EPS = 1e-5
RMS_EPS = 1.1920929e-07

F32 = mybir.dt.float32
I32 = mybir.dt.int32
ALU = mybir.AluOpType
ACT = mybir.ActivationFunctionType
AX = mybir.AxisListType
DVE_ENGINE = mybir.EngineType.DVE
PE_ENGINE = mybir.EngineType.PE
SP_ENGINE = mybir.EngineType.SP
ds = bass.ds
MIDDLE = "middle"
CLIPPED = "the setup clips tiles and chunks to their tables"

W0 = 128 + HEADS0 + 1
W1 = 2 * D + 1
W2 = 256
W3 = 256
ACC_W = max(W0, W1, W2, W3)


class Counter:

    def __init__(self, sem, by=1, base=0):
        self.sem, self.by, self.base, self.at, self.per, self.round = sem, by, base, 0, 0, 0

    def did(self, instruction):
        instruction.then_inc(self.sem, self.by)
        self.at += self.by
        return self, self.at


def wait(engine, *marks):
    last = {}
    for counter, at in marks:
        last[counter] = max(at, last.get(counter, 0))
    for counter, at in last.items():
        engine.wait_ge(counter.sem, counter.round * counter.per + (counter.base + at))


class Phase(ExitStack):

    def __init__(self, nc, tag):
        super().__init__()
        self.nc, self.tag, self.sems = nc, tag, []

    def sb(self, name, shape, dt=F32):
        return self.enter_context(self.nc.sbuf_tensor(f"{self.tag}_{name}", shape, dt))

    def sem(self, name):
        self.sems.append(self.nc.alloc_semaphore(f"{self.tag}_{name}"))
        return self.sems[-1]

    def end(self):
        self.nc.all_engine_barrier()
        self.nc.clear_and_free_semaphores(self.sems)
        self.nc.all_engine_barrier()


class Group:

    def __init__(self, i, u):
        self.i, self.u, self.n = i, u, i * SLOTS + u
        self.round = i + u // SLOTS
        self.slot, self.r2 = u % SLOTS, u % 2
        self.old = lambda k: not isinstance(self.n, int) or self.n >= k

    def upto(self, k):
        return self.i * SLOTS + (self.u + k + 1)


def pipeline(nc, stages):
    depth = max(lag for lag, _ in stages)
    assert depth <= SLOTS

    def step(i, v):
        for lag, fn in stages:
            g = Group(i, v - lag)
            if isinstance(g.n, int) and not 0 <= g.n < N_GROUPS:
                continue
            fn(g)

    for s in range(2 * SLOTS):
        step(s // SLOTS, s % SLOTS)
    with nc.Fori(2, N_GROUPS // SLOTS) as i:
        for v in range(SLOTS):
            step(i, v)
    for s in range(N_GROUPS, N_GROUPS + depth):
        step(s // SLOTS, s % SLOTS)


def build(nc, a):
    PE, V, A, G, SP = nc.tensor, nc.vector, nc.scalar, nc.gpsimd, nc.sync
    ENGINES = (PE, V, A, G, SP)
    root = ExitStack()

    def dram(name, shape, dt=F32):
        return nc.dram_tensor(name, shape, dt).ap()

    item_rows = dram("item_rows", [2, ITEMS_PAD], I32)
    local_d = dram("local_d", [P, ITEMS_PAD])
    local_last_d = dram("local_last_d", [P, ITEMS_PAD])
    src_d = dram("src_d", [P, ITEMS_PAD], I32)
    rhat_d = dram("rhat_d", [P, ITEMS_PAD, 3])
    reset_d = dram("reset_d", [ITEMS_PAD // GROUP, GROUP * P])
    emb_d = dram("emb_d", [ITEMS_PAD // 2, NB, 2, P])
    kv_t = dram("kv_t", [N_TILES * P, 2 * D])
    x1_t = dram("x1_t", [N_TILES * P, D + 1])
    up_t = dram("up_t", [N_TILES * P, D])
    fs_t = dram("fs_t", [N_TILES * P, D])
    fsv_t = dram("fsv_t", [N_TILES * P, 2 * D])

    def by_tile(table):
        return table.rearrange("(t p) d -> p t d", p=P)

    def carry(engine, sem):
        engine.sem_inc(sem, 1)

    def sb(ctx, name, shape, dt=F32):
        return ctx.enter_context(nc.sbuf_tensor(name, shape, dt))

    x = sb(root, "x", [P, N_TILES, D])
    acc = sb(root, "acc", [P, N_TILES, ACC_W])
    ident = sb(root, "ident", [P, P])
    node_iota = sb(root, "node_iota", [P, P])
    ones_row = sb(root, "ones_row", [1, P])
    ones_col = sb(root, "ones_col", [P, 1])
    tile_of = sb(root, "tile_of", [1, ITEMS_PAD], I32)
    banks = root.enter_context(nc.psum_tensor("banks", [P, 8, 512], F32))
    bank = [banks[:, i, :] for i in range(8)]

    def counters(ctx):
        return lambda name, by=1: Counter(ctx.sem(name), by)

    def setup():
        with Phase(nc, "set") as ctx:
            make = counters(ctx)
            pe, v, act, g = make("pe"), make("v"), make("act"), make("g")
            dma = lambda name: make(name, 16)
            d_x, d_head, d_out = dma("d_x"), dma("d_head"), dma("d_out")
            d_rows, d_tile, d_floats, d_ints = dma("d_rows"), dma("d_tile"), dma("d_floats"), dma("d_ints")

            m = g.did(G.memset(x[:, FULL_TILES:, :], 0.0))
            wait(SP, m)
            d_x.did(SP.dma_start(x[:, 0:FULL_TILES, :],
                                 a["x"][0:FULL_TILES * P, :].rearrange("(t p) d -> p t d", p=P)))
            x_in = d_x.did(SP.dma_start(x[0:REST, FULL_TILES, :], a["x"][FULL_TILES * P:N_NODES, :]))

            heads = sb(ctx, "heads", [1, 2, N_CHUNKS], I32)
            with nc.allow_non_contiguous_dma(reason="first and last destination of each chunk"):
                d_head.did(SP.dma_start(heads[:, 0, :], a["int_rows"][:, 1:2].rearrange("c a -> a c")))
                heads_in = d_head.did(SP.dma_start(heads[:, 1, :],
                                                   a["int_rows"][:, P:P + 1].rearrange("c a -> a c")))

            iota_i = sb(ctx, "iota_i", [P, P], I32)
            item_i = sb(ctx, "item_i", [P, ITEM_TILES], I32)
            m1 = g.did(G.iota(iota_i[:], pattern=[[1, P]], base=0, channel_multiplier=0))
            m2 = g.did(G.iota(item_i[:], pattern=[[P, ITEM_TILES]], base=0, channel_multiplier=1))
            g.did(G.memset(ident[:], 0.0))
            g.did(G.memset(ones_col[:], 1.0))
            m3 = g.did(G.memset(ones_row[:], 1.0))
            wait(G, m3)
            ident_ready = g.did(G.affine_select(out=ident[:], in_=ident[:], compare_op=ALU.not_equal, fill=1.0,
                                                base=0, pattern=[[-1, P]], channel_multiplier=1))
            item_no = sb(ctx, "item_no", [P, ITEM_TILES])
            wait(V, m1, m2)
            v.did(V.tensor_copy(node_iota[:], iota_i[:]))
            v.did(V.tensor_copy(item_no[:], item_i[:]))

            tiles_i = sb(ctx, "tiles_i", [1, 2, N_CHUNKS], I32)
            tiles = sb(ctx, "tiles", [1, 2, N_CHUNKS])
            row = sb(ctx, "row", [1, 4, N_CHUNKS])
            wait(V, heads_in)
            m = v.did(V.tensor_scalar(tiles_i[:], heads[:], 7, None, ALU.arith_shift_right))
            wait(V, m)
            m = v.did(V.tensor_copy(tiles[:], tiles_i[:]))
            wait(V, m)
            m = v.did(V.tensor_scalar(row[:, 0, :], tiles[:, 1, :], float(N_TILES - 1), 1.0, ALU.min, ALU.add))
            wait(V, m)
            m = v.did(V.tensor_tensor(row[:, 0, :], row[:, 0, :], tiles[:, 0, :], ALU.subtract))
            m0 = v.did(V.memset(row[:, 1, :], 0.0))
            wait(V, m, m0)
            m = v.did(V.tensor_tensor_scan(row[:, 2, :], row[:, 1, :], row[:, 0, :], 0.0, ALU.add, ALU.add))
            wait(V, m)
            m = v.did(V.tensor_tensor(row[:, 1, :], row[:, 2, :], row[:, 0, :], ALU.subtract))
            wait(V, m)
            m = v.did(V.tensor_tensor(row[:, 2, :], tiles[:, 0, :], row[:, 1, :], ALU.subtract))
            wait(V, m)
            m0 = v.did(V.tensor_copy(row[:, 3, 0:1], row[:, 2, 0:1]))
            m = v.did(V.tensor_tensor(row[:, 3, 1:], row[:, 2, 1:], row[:, 2, 0:N_CHUNKS - 1], ALU.subtract))

            before = sb(ctx, "before", [P, N_CHUNKS])
            jump = sb(ctx, "jump", [P, N_CHUNKS])
            wait(PE, ident_ready, m0, m)
            for k, (r, lo) in enumerate([(1, 0), (1, 512), (3, 0), (3, 512)]):
                hi = min(lo + 512, N_CHUNKS)
                m = pe.did(PE.matmul(bank[k][:, 0:hi - lo], ones_row[:], row[:, r, lo:hi], start=True, stop=True))
                wait(V, m)
                to = before if r == 1 else jump
                m_rows = v.did(V.tensor_copy(to[:, lo:hi], bank[k][:, 0:hi - lo]))
            hit = sb(ctx, "hit", [P, 2, N_CHUNKS])
            found = sb(ctx, "found", [P, 2, ITEM_TILES])
            for q in range(ITEM_TILES):
                wait(V, m_rows)
                ma = v.did(V.tensor_scalar(hit[:, 0, :], before[:], item_no[:, q:q + 1], None, ALU.is_le))
                mb = v.did(V.scalar_tensor_tensor(out=hit[:, 1, :], in0=before[:], scalar=item_no[:, q:q + 1],
                                                  in1=jump[:], op0=ALU.is_le, op1=ALU.mult))
                wait(V, ma, mb)
                m_rows = v.did(V.tensor_reduce(found[:, :, q:q + 1], hit[:], AX.X, ALU.add))
            chunk = sb(ctx, "chunk", [P, ITEM_TILES])
            tile = sb(ctx, "tile", [P, ITEM_TILES])
            item_tab = sb(ctx, "item_tab", [P, 2, ITEM_TILES], I32)
            wait(V, m_rows)
            ma = v.did(V.tensor_scalar(chunk[:], found[:, 0, :], -1.0, None, ALU.add))
            mb = v.did(V.tensor_tensor(tile[:], found[:, 1, :], item_no[:], ALU.add))
            wait(V, ma, mb)
            v.did(V.tensor_copy(item_tab[:, 1, :], chunk[:]))
            v.did(V.tensor_scalar(item_tab[:, 0, :], tile[:], float(N_TILES - 1), None, ALU.min))
            tile_base = sb(ctx, "tile_base", [P, ITEM_TILES])
            m_tab = v.did(V.tensor_scalar(tile_base[:], tile[:], float(P), None, ALU.mult))
            wait(SP, m_tab)
            with nc.allow_non_contiguous_dma(reason="a small table, once"):
                d_tile.did(SP.dma_start(item_rows[0, :].rearrange("(q p) -> p q", p=P), item_tab[:, 0, :]))
                m = d_tile.did(SP.dma_start(item_rows[1, :].rearrange("(q p) -> p q", p=P), item_tab[:, 1, :]))
            wait(SP, m)
            tile_in = d_rows.did(SP.dma_start(tile_of[:], item_rows[0:1, :]))

            floats = sb(ctx, "floats", [P, ITEM_TILES, 4 * P])
            ints = sb(ctx, "ints", [P, ITEM_TILES, 2 * P + 2], I32)
            wait(G, m_tab)
            for to, table, counter in ((floats, a["float_rows"], d_floats), (ints, a["int_rows"], d_ints)):
                for q in range(ITEM_TILES):
                    counter.did(G.indirect_dma_start(
                        out=to[:, q, :], out_offset=None, in_=table,
                        in_offset=bass.IndirectOffsetOnAxis(ap=item_tab[:, 1, q:q + 1], axis=0)))
            floats_in, ints_in = (d_floats, d_floats.at), (d_ints, d_ints.at)
            part = floats[:, :, 0:3 * P].rearrange("p q (c e) -> p q c e", c=3)
            length = floats[:, :, 3 * P:]
            dst = sb(ctx, "dst", [P, ITEM_TILES, P + 2])
            spare = acc[:].rearrange("p t d -> p (t d)")
            by_item = spare[:, 0:6 * ITEMS_PAD].rearrange("p (k q e) -> p k q e", k=6, q=ITEM_TILES)
            emb = spare[:, 6 * ITEMS_PAD:(6 + NB) * ITEMS_PAD].rearrange("p (q j e) -> p q j e", q=ITEM_TILES, j=NB)
            assert (6 + NB) * ITEMS_PAD <= N_TILES * ACC_W
            reset = sb(ctx, "reset", [P, ITEM_TILES, P])
            clipped = sb(ctx, "clipped", [P, ITEM_TILES, P])
            inside = sb(ctx, "inside", [P, ITEM_TILES, P])
            tmp = sb(ctx, "tmp", [P, 2, ITEM_TILES, P])

            wait(V, floats_in)
            m_clipped = v.did(V.tensor_scalar(clipped[:], length, 0.0, 1.0, ALU.max, ALU.min))
            m_inside = v.did(V.tensor_scalar(inside[:], length, 1.0, NB ** 0.5, ALU.is_le, ALU.mult))
            m = v.did(V.tensor_tensor(tmp[:, 0], part[:, :, 0, :], part[:, :, 0, :], ALU.mult))
            for c in (1, 2):
                mb = v.did(V.tensor_tensor(tmp[:, 1], part[:, :, c, :], part[:, :, c, :], ALU.mult))
                wait(V, m, mb)
                m = v.did(V.tensor_tensor(tmp[:, 0], tmp[:, 0], tmp[:, 1], ALU.add))
                wait(V, m)
            wait(A, m)
            m = act.did(A.activation(tmp[:, 1], tmp[:, 0], ACT.Sqrt))
            wait(V, m)
            m = v.did(V.tensor_scalar(tmp[:, 0], tmp[:, 1], 1e-12, None, ALU.add))
            wait(V, m)
            m = v.did(V.reciprocal(tmp[:, 1], tmp[:, 0]))
            wait(V, m)
            for c in range(3):
                m = v.did(V.tensor_tensor(by_item[:, 3 + c], part[:, :, c, :], tmp[:, 1], ALU.mult))

            wait(A, m_clipped)
            for j in range(NB):
                mj = act.did(A.activation(emb[:, :, j, :], clipped[:], ACT.Square, scale=float(1 - NB),
                                          bias=node_iota[:, j:j + 1]))
            wait(A, mj)
            exps = [act.did(A.activation(emb[:, :, j, :], emb[:, :, j, :], ACT.Exp, scale=-0.5)) for j in range(NB)]

            wait(V, ints_in)
            v.did(V.tensor_copy(by_item[:, 2], ints[:, :, P + 2:]))
            mb = v.did(V.tensor_copy(dst[:], ints[:, :, 0:P + 2]))
            wait(V, m, mb)
            for q in range(ITEM_TILES):
                m = v.did(V.tensor_scalar(by_item[:, 0, q, :], dst[:, q, 1:P + 1], tile_base[:, q:q + 1], None,
                                          ALU.subtract))
            mb = v.did(V.tensor_tensor(reset[:], dst[:, :, 1:P + 1], dst[:, :, 0:P], ALU.not_equal))
            mc = v.did(V.tensor_tensor(tmp[:, 0], dst[:, :, 1:P + 1], dst[:, :, 2:P + 2], ALU.not_equal))
            wait(V, m, mb, mc)
            m_reset = v.did(V.tensor_scalar(reset[:], reset[:], LOW, None, ALU.mult))
            m = v.did(V.scalar_tensor_tensor(out=tmp[:, 1], in0=by_item[:, 0], scalar=1.0, in1=tmp[:, 0],
                                             op0=ALU.add, op1=ALU.mult))
            wait(V, m)
            m_items = v.did(V.tensor_scalar(by_item[:, 1], tmp[:, 1], -1.0, None, ALU.add))
            wait(V, m_inside)
            for j in range(NB):
                wait(V, exps[j])
                m_emb = v.did(V.tensor_tensor(emb[:, :, j, :], emb[:, :, j, :], inside[:], ALU.mult))

            wait(SP, m_reset)
            d_out.did(SP.dma_start(reset_d.rearrange("g (i e) -> (g i) e", i=GROUP)
                                   .rearrange("(q p) e -> p q e", p=P), reset[:]))

            table_f = [sb(ctx, f"table{k}", [P, ITEMS_PAD]) for k in range(2)]
            table_src = sb(ctx, "table_src", [P, ITEMS_PAD], I32)
            table_r = sb(ctx, "table_r", [P, ITEMS_PAD, 3])
            wait(PE, m_items)
            copies = []
            for n in range(6 * ITEM_TILES):
                k, q = n // ITEM_TILES, n % ITEM_TILES
                if n >= 8:
                    wait(PE, copies[n - 8])
                m = pe.did(PE.transpose(bank[n % 8][:, 0:P], by_item[:, k, q, :], ident[:]))
                to = (table_f + [table_src])[k][:, q * P:(q + 1) * P] if k < 3 else \
                    table_r[:, q * P:(q + 1) * P, k - 3]
                e, c = ((A, act), (V, v))[n % 2]
                wait(e, m)
                copies.append(c.did(e.tensor_copy(to, bank[n % 8][:, 0:P]) if e is V
                                    else e.activation(to, bank[n % 8][:, 0:P], ACT.Copy)))
            wait(SP, m_emb)
            half = P // 2
            for q in range(ITEM_TILES):
                for b in range(2):
                    d_out.did(SP.dma_start(emb_d[q * half:(q + 1) * half, :, b, :], emb[b::2, q, :, :]))
            wait(SP, *copies)
            for to, of in ((local_d, table_f[0]), (local_last_d, table_f[1]), (src_d, table_src),
                           (rhat_d, table_r)):
                d_out.did(SP.dma_start(to, of[:]))

            last = (d_out, d_out.at)
            for e in ENGINES:
                wait(e, last, x_in, tile_in)
            ctx.end()

    class NodePhase:

        def __init__(self, ctx):
            self.ctx, self.sb = ctx, ctx.sb
            self.ready = ctx.sem("ready")
            self.w, self.prep = Counter(ctx.sem("w"), 16), Counter(ctx.sem("prep"))

        def load(self, pairs):
            for to, of in pairs:
                self.w.did(SP.dma_start(to, of))
            for e in ENGINES:
                wait(e, (self.w, self.w.at))

        def prepare(self, engine, instruction):
            wait(engine, self.prep.did(instruction))

        def prepared(self):
            for e in ENGINES:
                wait(e, (self.prep, self.prep.at))

    class Stream:

        def __init__(self, phase, number):
            self.ctx, self.phase, self.number = phase.ctx, phase, number
            self.make_counter = lambda name, by=1: Counter(self.ctx.sem(f"{name}{number}"), by)
            self.pe, self.v, self.act, self.g = (self.make_counter(n) for n in ("pe", "v", "act", "g"))
            self.out = Counter(self.ctx.sem(f"out{number}"), 16, 16)
            SP.sem_inc(self.out.sem, 16)
            self.carried = self.ctx.sem(f"carry{number}")
            self.inner = [self.pe, self.v, self.act, self.g]
            self.all = self.inner + [self.out]
            self.small = self.sb("small", [P, 4, BLOCK])
            self.square = self.sb("square", [P, BLOCK, D])
            self.stats = self.sb("stats", [P, BLOCK, 6])
            self.mean_var = self.sb("mean_var", [P, BLOCK, 2])
            self.bank = bank[number * 4:number * 4 + 4]

        def sb(self, name, shape, dt=F32):
            return self.ctx.sb(f"{name}{self.number}", shape, dt)

        def set_round(self, r):
            self.block = r * STREAMS + self.number
            for c in self.all:
                c.round = r

        def start(self, r):
            self.set_round(r)
            for c in self.all:
                c.at = 0
            for e in (PE, V, A, G):
                for c in self.inner:
                    if c.per:
                        e.wait_ge(c.sem, r * c.per)
                e.wait_ge(self.phase.ready, 1)

        def rows_are_out(self, engine):
            wait(engine, (self.out, 0))

        @property
        def own(self):
            return ds(self.block * BLOCK, BLOCK)

        def tile(self, j):
            return ds(self.block * BLOCK + j, 1)

        def halves(self, n):
            for k, (lo, hi) in enumerate(((0, HALF), (HALF, BLOCK))):
                yield lo, hi, self.bank[n + k][:, 0:(hi - lo) * P]

        def transpose(self, of, to, ready, n):
            yield wait(PE, *ready)
            made, done = [], []
            for lo, hi, ps in self.halves(n):
                for j in range(lo, hi):
                    m = PE.transpose(ps[:, (j - lo) * P:(j - lo + 1) * P], of[:, j, :], ident[:])
                made.append((lo, hi, ps, self.pe.did(m)))
            for lo, hi, ps, m in made:
                yield wait(A, m)
                done.append(self.act.did(A.activation(to[:, lo:hi, :], ps.rearrange("p (t d) -> p t d", d=P),
                                                      ACT.Copy)))
            return done

        def project(self, pairs, ready, n):
            out = []
            for half, (lo, hi, ps) in enumerate(self.halves(n)):
                yield wait(PE, *ready[half::2])
                for j in range(lo, hi):
                    for k, (xt, w) in enumerate(pairs):
                        m = PE.matmul(ps[:, (j - lo) * P:(j - lo + 1) * P], xt[:, j, :], w,
                                      start=(k == 0), stop=(k == len(pairs) - 1))
                out.append((slice(lo, hi), ps.rearrange("p (t d) -> p t d", d=P), self.pe.did(m)))
            return out

        def inverse_root(self, col, of, factor, eps, ready):
            yield wait(V, *ready)
            m = self.v.did(V.tensor_scalar(self.small[:, col, :], of, factor, eps, ALU.mult, ALU.add))
            yield wait(A, m)
            m = self.act.did(A.activation(self.small[:, 3, :], self.small[:, col, :], ACT.Sqrt))
            yield wait(V, m)
            return self.v.did(V.reciprocal(self.small[:, col, :], self.small[:, 3, :]))

        def root_mean_square(self, of, ready, eps, col):
            yield wait(A, *ready)
            m = self.act.did(A.activation(self.square[:], of, ACT.Square))
            yield wait(V, m)
            m = self.v.did(V.tensor_reduce(self.small[:, col, :], self.square[:], AX.X, ALU.add))
            return (yield from self.inverse_root(col, self.small[:, col, :], 1.0 / D, eps, [m]))

        def layernorm(self, z, to, ready):
            yield wait(V, *ready)
            for j in range(BLOCK):
                m = self.v.did(V.bn_stats(self.stats[:, j, :], z[:, j, :]))
            yield wait(V, m)
            carry(V, self.carried)
            for j in range(BLOCK):
                m = self.v.did(V.bn_aggr(self.mean_var[:, j, :], self.stats[:, j, :]))
            m = yield from self.inverse_root(1, self.mean_var[:, :, 1], 1.0, LN_EPS, [m])
            yield wait(V, m)
            carry(V, self.carried)
            for j in range(BLOCK):
                m = self.v.did(V.tensor_scalar(to(j), z[:, j, :], self.mean_var[:, j, 0:1], self.small[:, 1, j:j + 1],
                                               ALU.subtract, ALU.mult))
            return m

        def project3(self, xt, ready, w, bias, first, rest):
            done = []
            for j in range(BLOCK):
                ps = self.bank[(0, 2, 3, 1)[j % 4]]
                if j in (0, HALF):
                    yield wait(PE, ready[j // HALF])
                if j >= 4:
                    wait(PE, done[2 * (j - 4) + 1])
                m = self.pe.did(PE.matmul(ps[:, 0:3 * D], xt[:, j, :], w[:], start=True, stop=True))
                yield wait(V, m)
                done.append(self.v.did(V.tensor_tensor(first[:, j, :], ps[:, 0:2 * D], bias[:, 0:2 * D], ALU.add)))
                done.append(self.v.did(V.tensor_tensor(rest[:, j, :], ps[:, 2 * D:3 * D], bias[:, 2 * D:3 * D],
                                                       ALU.add)))
            return done

    def node_phase(tag, make, weights=None):
        with Phase(nc, tag) as ctx:
            phase = NodePhase(ctx)
            if weights:
                weights(phase)
            V.memset(ctx.sb("start", [P, 1])[:], 0.0).then_inc(phase.ready, 1)
            V.wait_ge(phase.ready, 1)
            first, second = streams = [Stream(phase, s) for s in range(STREAMS)]
            steps_first, steps_second = (make(s, phase) for s in streams)
            n_rounds = N_BLOCKS // STREAMS

            def run(*halves):
                running = list(halves)
                while running:
                    for steps in list(running):
                        if next(steps, MIDDLE) == MIDDLE:
                            running.remove(steps)

            first.set_round(0)
            second.set_round(0)
            a_block, b_block = steps_first(), steps_second()
            run(a_block)
            run(a_block, b_block)
            for c, c2 in zip(first.all, second.all):
                c.per = c2.per = c.at
            with nc.Fori(1, n_rounds) as r:
                first.start(r)
                second.set_round(r - 1)
                a_block = steps_first()
                run(a_block, b_block)
                second.start(r)
                b_block = steps_second()
                run(a_block, b_block)
            second.set_round(n_rounds - 1)
            run(b_block)
            for c in first.all + second.all:
                assert c.at == c.per
                for e in ENGINES:
                    e.wait_ge(c.sem, c.base + c.per * n_rounds)
            ctx.end()

    def spread(col, width=D):
        return col.unsqueeze(2).to_broadcast([P, col.shape[1], width])

    def tiles_of(row):
        return row.unsqueeze(1).to_broadcast([P, BLOCK, row.shape[1]])

    def vec_row(v):
        return v.rearrange("(a n) -> a n", a=1).to_broadcast([P, v.shape[0]])

    def vec_col(v):
        return v.rearrange("(n a) -> n a", a=1)

    def project0(queries):
        def weights(w):
            w.wqkv, w.bqkv = w.sb("w3", [P, 3 * D]), w.sb("b3", [P, 3 * D])
            pairs = []
            for n, name in enumerate(("k", "v", "q")):
                pairs.append((w.wqkv[:, n * D:(n + 1) * D], a[f"L0_gnn_W{name}"]))
                pairs.append((w.bqkv[:, n * D:(n + 1) * D], vec_row(a[f"L0_gnn_b{name}"])))
            w.load(pairs)

        def make(k, w):
            xin, xt, kv = k.sb("xin", [P, BLOCK, D]), k.sb("xt", [P, BLOCK, D]), k.sb("kv", [P, BLOCK, 2 * D])

            def steps():
                m = k.act.did(A.activation(xin[:], x[:, k.own, :], ACT.Copy))
                ready = yield from k.transpose(xin, xt, [m], 0)
                yield MIDDLE
                k.rows_are_out(V)
                done = yield from k.project3(xt, ready, w.wqkv, w.bqkv, kv, queries[:, k.own, :])
                yield wait(SP, *done)
                k.out.did(SP.dma_start(by_tile(kv_t)[:, k.own, :], kv[:]))
            return steps
        node_phase("proj0", make, weights)

    def after0(inv_root_deg):
        def make(k, w):
            z, t1 = k.sb("z", [P, BLOCK, D]), k.sb("t1", [P, BLOCK, D + 1])
            zs = k.sb("zs", [P, 2, BLOCK, HEADS0])

            def by_head(t):
                return t.rearrange("p t (h c) -> p t h c", h=HEADS0)

            def steps():
                m = k.v.did(V.tensor_scalar(zs[:, 0], acc[:, k.own, D:D + HEADS0], 1e-6, None, ALU.add))
                mb = k.v.did(V.tensor_scalar(k.small[:, 2, :], acc[:, k.own, D + HEADS0], 1.0, None, ALU.max))
                yield wait(V, m)
                m = k.v.did(V.reciprocal(zs[:, 1], zs[:, 0]))
                yield wait(A, mb)
                ma = k.act.did(A.activation(k.small[:, 3, :], k.small[:, 2, :], ACT.Sqrt))
                yield wait(V, m, ma)
                mr = k.v.did(V.reciprocal(k.small[:, 2, :], k.small[:, 3, :]))
                m = k.v.did(V.tensor_tensor(by_head(z[:]), by_head(acc[:, k.own, 0:D]),
                                            zs[:, 1].unsqueeze(3).to_broadcast([P, BLOCK, HEADS0, HDIM0]), ALU.mult))
                yield wait(V, m, mr)
                m = k.v.did(V.tensor_tensor(z[:], z[:], x[:, k.own, :], ALU.add))
                mi = k.v.did(V.tensor_copy(inv_root_deg[:, k.own], k.small[:, 2, :]))
                yield MIDDLE
                m = yield from k.layernorm(z, lambda j: x[:, k.tile(j), :].rearrange("p a d -> p (a d)"),
                                           [m, mi])
                yield wait(V, m)
                k.rows_are_out(V)
                k.v.did(V.tensor_tensor(t1[:, :, 0:D], x[:, k.own, :], spread(k.small[:, 2, :]), ALU.mult))
                m = k.v.did(V.tensor_copy(t1[:, :, D:D + 1], k.small[:, 2, :].unsqueeze(2)))
                yield wait(SP, m)
                k.out.did(SP.dma_start(by_tile(x1_t)[:, k.own, :], t1[:]))
            return steps
        node_phase("after0", make)

    def after1(inv_root_deg):
        def weights(w):
            w.w2e, w.w1n, w.w2n, w.up = (w.sb(n, [P, D]) for n in ("w2e", "w1n", "w2n", "up"))
            w.b2e, w.b2n, w.rms = (w.sb(n, [P, D]) for n in ("b2e", "b2n", "rms"))
            w.b1n, w.eps = w.sb("b1n", [P, 1]), w.sb("eps", [P, 1])
            w.prepare(G, G.memset(w.up[:], 0.0))
            w.prepared()
            pairs = [(w.w2e[:], a["L1_gnn_W2e"]), (w.w1n[:], a["L1_gnn_W1n"]), (w.w2n[:], a["L1_gnn_W2n"]),
                     (w.b2e[:], vec_row(a["L1_gnn_b2e"])), (w.b2n[:], vec_row(a["L1_gnn_b2n"])), (w.rms[:], vec_row(a["L1_gnn_rms_w"])),
                     (w.b1n[:], vec_col(a["L1_gnn_b1n"])), (w.eps[:], a["gin_eps"].to_broadcast([P, 1])),
                     (w.up[0:MUL, 0:MUL], a["L2_gnn_W_up0"])]
            pairs += [(w.up[MUL + c:P:3, MUL + MUL * c:2 * MUL + MUL * c], a["L2_gnn_W_up1"]) for c in range(3)]
            w.load(pairs)
            w.prepare(V, V.tensor_scalar(w.up[:], w.up[:], MUL ** -0.5, None, ALU.mult))
            w.prepare(V, V.tensor_scalar(w.eps[:], w.eps[:], 1.0, None, ALU.add))
            w.prepared()

        def make(k, w):
            h, ht, z, t2, x1, xb = (k.sb(n, [P, BLOCK, D]) for n in ("h", "ht", "z", "t2", "x1", "xb"))

            def steps():
                m = k.act.did(A.activation(h[:], acc[:, k.own, D + 1:W1], ACT.Copy))
                mb = k.v.did(V.tensor_copy(k.small[:, 2, :], acc[:, k.own, D]))
                mx = k.act.did(A.activation(x1[:], x[:, k.own, :], ACT.Copy))
                wait(G, mx)
                mxb = k.g.did(G.tensor_tensor(xb[:], x1[:], tiles_of(w.b2n[:]), ALU.add))
                ready = yield from k.transpose(h, ht, [m], 0)
                yield wait(V, mb)
                carry(V, k.carried)
                for j in range(BLOCK):
                    m = k.v.did(V.scalar_tensor_tensor(
                        out=z[:, j, :], in0=w.b2e[:], scalar=k.small[:, 2, j:j + 1],
                        in1=acc[:, k.tile(j), 0:D].rearrange("p a d -> p (a d)"),
                        op0=ALU.mult, op1=ALU.add))
                for part, ps, done in (yield from k.project([(ht, w.w2e[:])], ready, 2)):
                    yield wait(V, m, done)
                    ms = k.v.did(V.tensor_tensor(z[:, part, :], z[:, part, :], ps, ALU.add))
                yield wait(V, ms)
                m = k.v.did(V.tensor_tensor(z[:], z[:], spread(inv_root_deg[:, k.own]), ALU.mult))
                yield wait(V, m, mx)
                m = k.v.did(V.scalar_tensor_tensor(out=h[:], in0=x1[:], scalar=w.eps[:], in1=z[:],
                                                   op0=ALU.mult, op1=ALU.add))
                ready = yield from k.transpose(h, ht, [m], 0)
                hid, made = [], []
                for half, (lo, hi, ps) in enumerate(k.halves(0)):
                    yield wait(PE, ready[half])
                    m = k.pe.did(PE.matmul(ps, w.w1n[:], ht[:, lo:hi, :].rearrange("p t d -> p (t d)"),
                                           start=True, stop=True))
                    made.append((lo, hi, ps, m))
                for lo, hi, ps, m in made:
                    yield wait(A, m)
                    hid.append(k.act.did(A.activation(h[:, lo:hi, :].rearrange("p t d -> p (t d)"), ps,
                                                      ACT.Relu, bias=w.b1n[:])))
                for part, ps, done in (yield from k.project([(h, w.w2n[:])], hid, 2)):
                    yield wait(V, done, mxb)
                    ms = k.v.did(V.tensor_tensor(z[:, part, :], ps, xb[:, part, :], ALU.add))
                m = yield from k.root_mean_square(z[:], [ms], RMS_EPS, 2)
                yield wait(V, m)
                for j in range(BLOCK):
                    m = k.v.did(V.scalar_tensor_tensor(out=z[:, j, :], in0=z[:, j, :], scalar=k.small[:, 2, j:j + 1],
                                                       in1=w.rms[:], op0=ALU.mult, op1=ALU.mult))
                yield MIDDLE
                yield wait(V, m)
                m = k.v.did(V.tensor_tensor(z[:], z[:], x1[:], ALU.add))
                m = yield from k.layernorm(z, lambda j: h[:, j, :], [m])
                yield wait(A, m)
                carry(A, k.carried)
                k.act.did(A.activation(x[:, k.own, :], h[:], ACT.Copy))
                ready = yield from k.transpose(h, ht, [m], 0)
                out = []
                k.rows_are_out(A)
                for part, ps, done in (yield from k.project([(ht, w.up[:])], ready, 2)):
                    yield wait(A, done)
                    out.append(k.act.did(A.activation(t2[:, part, :], ps, ACT.Copy)))
                yield wait(SP, *out)
                k.out.did(SP.dma_start(by_tile(up_t)[:, k.own, :], t2[:]))
            return steps
        node_phase("after1", make, weights)

    def after2(at_dst):
        def weights(w):
            raw = w.sb("raw", [P, 2, MUL])
            w.wo = w.sb("wo", [P, 2, D])
            w.w3, w.b3 = w.sb("w3", [P, 3 * D]), w.sb("b3", [P, 3 * D])
            w.prepare(G, G.memset(w.wo[:], 0.0))
            w.prepare(G, G.memset(raw[:], 0.0))
            w.prepared()
            pairs = [(raw[0:2 * MUL, 0, :], a["L2_gnn_W_out0"]), (raw[2 * MUL:P, 0, :], a["L2_gnn_W_out1"]),
                     (raw[0:2 * MUL, 1, :], a["L2_gnn_W_out1"]), (raw[2 * MUL:P, 1, :], a["L2_gnn_W_out1"])]
            for n, name in enumerate(("src", "v", "dst")):
                pairs.append((w.w3[:, n * D:(n + 1) * D], a[f"W_{name}_t"]))
                pairs.append((w.b3[:, n * D:(n + 1) * D], vec_row(a[f"L3_gnn_b_{name}"])))
            w.load(pairs)
            scale = (2 * MUL) ** -0.5 / AVG
            w.prepare(V, V.tensor_scalar(w.wo[0:2 * MUL, 0, 0:MUL], raw[0:2 * MUL, 0, :], scale, None, ALU.mult))
            for c, (lo, half) in enumerate(((2 * MUL, 0), (0, 1), (2 * MUL, 1))):
                for row, factor in ((lo, scale * SQ3), (lo + MUL, scale)):
                    w.prepare(V, V.tensor_scalar(w.wo[row:row + MUL, half, MUL + c:P:3],
                                                 raw[row:row + MUL, half, :], factor, None, ALU.mult))
            w.prepared()

        def make(k, w):
            h, ht, ht2, z, xt = (k.sb(n, [P, BLOCK, D]) for n in ("h", "ht", "ht2", "z", "xt"))
            t3 = k.sb("t3", [P, BLOCK, 2 * D])

            def steps():
                m = k.act.did(A.activation(h[:], acc[:, k.own, 0:D], ACT.Copy))
                mb = k.act.did(A.activation(z[:], acc[:, k.own, D:2 * D], ACT.Copy))
                ready = yield from k.transpose(h, ht, [m], 0)
                ready += yield from k.transpose(z, ht2, [mb], 2)
                for part, ps, done in (yield from k.project([(ht, w.wo[:, 0, :]), (ht2, w.wo[:, 1, :])], ready, 0)):
                    yield wait(V, done)
                    m = k.v.did(V.tensor_tensor(z[:, part, :], ps, x[:, ds(k.block * BLOCK + part.start,
                                                                         part.stop - part.start), :], ALU.add))
                yield MIDDLE
                m = yield from k.layernorm(z, lambda j: h[:, j, :], [m])
                yield
                wait(A, m)
                carry(A, k.carried)
                k.act.did(A.activation(x[:, k.own, :], h[:], ACT.Copy))
                ready = yield from k.transpose(h, xt, [m], 0)
                k.rows_are_out(V)
                done = yield from k.project3(xt, ready, w.w3, w.b3, t3, at_dst[:, k.own, 0:D])
                yield wait(SP, *done)
                k.out.did(SP.dma_start(by_tile(fsv_t)[:, k.own, :], t3[:]))
                k.out.did(SP.dma_start(by_tile(fs_t)[:, k.own, :], t3[:, :, 0:D]))
            return steps
        node_phase("after2", make, weights)

    def maxima(at_dst):
        def make(k, w):
            s, r = k.sb("s", [P, BLOCK, D]), k.sb("r", [P, BLOCK, D])

            def steps():
                m = k.v.did(V.tensor_tensor(s[:], acc[:, k.own, 0:D], at_dst[:, k.own, 0:D], ALU.add))
                yield MIDDLE
                yield wait(A, m)
                m = k.act.did(A.activation(r[:], s[:], ACT.Relu, scale=0.8))
                yield wait(V, m)
                k.v.did(V.scalar_tensor_tensor(out=at_dst[:, k.own, D:2 * D], in0=s[:], scalar=0.2, in1=r[:],
                                               op0=ALU.mult, op1=ALU.add))
            return steps
        node_phase("maxima", make)

    def after3():
        def make(k, w):
            z, s = (k.sb(n, [P, BLOCK, D]) for n in ("z", "s"))

            def steps():
                m = k.v.did(V.tensor_scalar(s[:], acc[:, k.own, D:2 * D], 1e-30, None, ALU.max))
                yield wait(V, m)
                m = k.v.did(V.reciprocal(z[:], s[:]))
                yield MIDDLE
                yield wait(G, m)
                carry(G, k.carried)
                m = k.g.did(G.tensor_tensor(z[:], z[:], acc[:, k.own, 0:D], ALU.mult))
                yield
                wait(G, m)
                carry(G, k.carried)
                m = k.g.did(G.tensor_tensor(z[:], z[:], x[:, k.own, :], ALU.add))
                yield
                yield from k.layernorm(z, lambda j: x[:, k.tile(j), :].rearrange("p a d -> p (a d)"), [m])
            return steps
        node_phase("after3", make)
        with nc.semaphore("written") as written:
            SP.dma_start(a["out"][0:FULL_TILES * P, :].rearrange("(t p) d -> p t d", p=P),
                         x[:, 0:FULL_TILES, :]).then_inc(written, 16)
            SP.dma_start(a["out"][FULL_TILES * P:N_NODES, :], x[0:REST, FULL_TILES, :]).then_inc(written, 16)
            SP.wait_ge(written, 32)

    class EdgePass:

        def __init__(self, ctx, table, width, sums, local, fixed=()):
            self.ctx, self.sb, self.sem, self.table, self.sums = ctx, ctx.sb, ctx.sem, table, sums
            self.src = self.sb("src", [P, N_ITEMS], I32)
            self.local = self.sb("local", [P, N_ITEMS])
            self.index = self.sb("index", [P, SLOTS, GROUP], I32)
            self.rows = self.sb("rows", [P, SLOTS, GROUP, width])
            self.sel = self.sb("sel", [P, SLOTS, GROUP, P])
            self.per_bank = 2 if 2 * sums <= 512 else 1
            self.s_index = [self.sem(f"index{u}") for u in range(SLOTS)]
            self.s_rows = [self.sem(f"rows{u}") for u in range(SLOTS)]
            self.s_sel = self.sem("sel")
            self.s_sums = [self.sem(f"sums{k}") for k in range(GROUP // self.per_bank)]
            self.s_added = [self.sem(f"added{i}") for i in range(GROUP)]
            self.s_load = self.sem("load")
            self.s_carry = self.sem("carry")
            self.zeroed = self.sem("zeroed")
            s_src = self.sem("src_in")
            SP.dma_start(self.src[:], src_d[:, 0:N_ITEMS]).then_inc(s_src, 16)
            fixed = [(self.local[:], local[:, 0:N_ITEMS])] + list(fixed)
            for to, of in fixed:
                SP.dma_start(to, of).then_inc(self.s_load, 16)
            self.loads = 16 * len(fixed)
            V.memset(acc[:, :, 0:sums], 0.0).then_inc(self.zeroed, 1)
            V.wait_ge(self.zeroed, 1)
            for e in (PE, V, A):
                e.wait_ge(self.s_load, self.loads)
            SP.wait_ge(s_src, 16)

        def gather(self, g, s_free):
            u = g.slot
            if g.old(SLOTS):
                SP.wait_ge(self.s_rows[u], g.round * 64)
            SP.dma_start(self.index[:, u, :], self.src[:, ds(g.n * GROUP, GROUP)]).then_inc(self.s_index[u], 16)
            G.wait_ge(self.s_index[u], (g.round + 1) * 16)
            if g.old(SLOTS):
                G.wait_ge(s_free, g.upto(-SLOTS))
            carry(G, self.s_carry)
            for i in range(GROUP):
                G.indirect_dma_start(out=self.rows[:, u, i, :], out_offset=None, in_=self.table,
                                     in_offset=bass.IndirectOffsetOnAxis(ap=self.index[:, u, i:i + 1], axis=0)
                                     ).then_inc(self.s_rows[u], 16)

        def have_rows(self, engine, g):
            engine.wait_ge(self.s_rows[g.slot], (g.round + 1) * 64)

        def summed(self, engine, g, k):
            engine.wait_ge(self.s_sums[-1], g.upto(k))

        def select(self, g):
            if g.old(SLOTS):
                self.summed(V, g, -SLOTS)
            V.tensor_tensor(self.sel[:, g.slot],
                            node_iota[:].unsqueeze(1).to_broadcast([P, GROUP, P]),
                            self.local[:, ds(g.n * GROUP, GROUP)].unsqueeze(2).to_broadcast([P, GROUP, P]),
                            ALU.is_equal).then_inc(self.s_sel, 1)

        def selector(self):
            away = self.sb("away", [P, GROUP, P])
            s_away = self.sem("away")

            def distance(g):
                if g.old(1):
                    A.wait_ge(self.s_sel, g.upto(-1))
                    carry(A, self.s_carry)
                for i in range(GROUP):
                    m = A.activation(away[:, i, :], node_iota[:], ACT.Abs,
                                     bias=self.local[:, ds(g.n * GROUP + i, 1)], scale=-1.0)
                m.then_inc(s_away, 1)

            def at_zero(g):
                A.wait_ge(s_away, g.upto(0))
                if g.old(SLOTS):
                    self.summed(A, g, -SLOTS)
                A.activation(self.sel[:, g.slot], away[:], ACT.Relu, bias=ones_col[:], scale=-1.0
                             ).then_inc(self.s_sel, 1)
            return distance, at_zero

        def place(self, g, i):
            if self.per_bank == 1:
                return i, 0
            return 2 * g.r2 + i // 2, i % 2 * self.sums

        def scatter(self, g, parts):
            for i in range(GROUP):
                n_bank, col = self.place(g, i)
                if i % self.per_bank == 0 and g.old(self.per_bank):
                    PE.wait_ge(self.s_added[i + self.per_bank - 1], g.upto(-self.per_bank))
                for at, rows in parts(i):
                    m = PE.matmul(bank[n_bank][:, col + at:col + at + rows.shape[1]], self.sel[:, g.slot, i, :],
                                  rows, start=True, stop=True)
                if (i + 1) % self.per_bank == 0:
                    m.then_inc(self.s_sums[i // self.per_bank], 1)

        def add(self, i):
            def stage(g):
                if i == 0:
                    self.tiles_to = self.tiles(g, DVE_ENGINE)
                n_bank, col = self.place(g, i)
                if i % self.per_bank == 0:
                    V.wait_ge(self.s_sums[i // self.per_bank], g.upto(0))
                if i:
                    V.wait_ge(self.s_added[i - 1], g.upto(0))
                elif g.old(1):
                    V.wait_ge(self.s_added[GROUP - 1], g.upto(-1))
                to = acc[:, ds(self.tiles_to[i], 1), 0:self.sums]
                V.tensor_tensor(to, to, bank[n_bank][:, col:col + self.sums].unsqueeze(1), ALU.add
                                ).then_inc(self.s_added[i], 1)
            return stage

        def tiles(self, g, engine):
            _, tiles = nc.values_load_multi_w_load_instructions(
                tile_of[0:1, ds(g.n * GROUP, GROUP)], engines=(engine,), min_val=0, max_val=N_TILES - 1,
                skip_runtime_bounds_check_because=CLIPPED)
            return tiles

        def run(self, stages):
            pipeline(nc, stages)
            for e in ENGINES:
                e.wait_ge(self.s_added[GROUP - 1], N_GROUPS)
            self.ctx.end()

    class Turned:

        def __init__(self, ps, n_bank, s_used):
            self.ps, self.bank, self.s_used = ps, n_bank, s_used
            self.sel_t = ps.sb("sel_t", [P, 2, GROUP, P])
            self.s_t = ps.sem("t")
            self.s_copied = ps.sem("copied")

        def turn(self, g):
            PE.wait_ge(self.ps.s_sel, g.upto(0))
            if g.old(1):
                PE.wait_ge(self.s_copied, g.upto(-1))
            for i in range(GROUP):
                m = PE.transpose(bank[self.bank][:, i * P:(i + 1) * P], self.ps.sel[:, g.slot, i, :], ident[:])
            m.then_inc(self.s_t, 1)
            A.wait_ge(self.s_t, g.upto(0))
            if g.old(2):
                A.wait_ge(self.s_used, g.upto(-2))
            A.activation(self.sel_t[:, g.r2].rearrange("p i e -> p (i e)"), bank[self.bank], ACT.Copy
                         ).then_inc(self.s_copied, 1)

    def quad(b, width=P):
        return bank[b][:, 0:GROUP * width].rearrange("p (i d) -> p i d", i=GROUP)

    def edges0(queries):
        with Phase(nc, "e0") as ctx:
            ps = EdgePass(ctx, kv_t, 2 * D, W0, local_d)
            B_T, B_Q = 4, (5, 6)
            prod = ps.sb("prod", [P, GROUP, D])
            dots = ps.sb("dots", [P, GROUP * HEADS0])
            clip = ps.sb("clip", [P, 2, GROUP * HEADS0])
            msg = ps.sb("msg", [P, 2, GROUP, W0])
            s_q, s_prod, s_dots, s_clip, s_score, s_msg, ones = (
                ps.sem(n) for n in ("q", "prod", "dots", "clip", "score", "msg", "ones"))
            turned = Turned(ps, B_T, s_q)
            V.memset(msg[:, :, :, W0 - 1], 1.0).then_inc(ones, 1)
            PE.wait_ge(ones, 1)

            def gather(g):
                ps.gather(g, s_msg)

            def queries_to_edges(g):
                tiles = ps.tiles(g, PE_ENGINE)
                PE.wait_ge(turned.s_copied, g.upto(0))
                if g.old(2):
                    PE.wait_ge(s_prod, g.upto(-2))
                for i in range(GROUP):
                    m = PE.matmul(bank[B_Q[g.r2]][:, i * P:(i + 1) * P], turned.sel_t[:, g.r2, i, :],
                                  queries[:, ds(tiles[i], 1), :].rearrange("p a d -> p (a d)"),
                                  start=True, stop=True)
                m.then_inc(s_q, 1)

            def products(g):
                ps.have_rows(V, g)
                V.wait_ge(s_q, g.upto(0))
                if g.old(1):
                    V.wait_ge(s_dots, g.upto(-1))
                V.tensor_tensor(prod[:], ps.rows[:, g.slot, :, 0:D], quad(B_Q[g.r2]), ALU.mult
                                ).then_inc(s_prod, 1)

            def dot(g):
                V.wait_ge(s_prod, g.upto(0))
                if g.old(1):
                    V.wait_ge(s_clip, g.upto(-1))
                V.tensor_reduce(dots[:], prod[:].rearrange("p i (h c) -> p (i h) c", c=HDIM0), AX.X, ALU.add
                                ).then_inc(s_dots, 1)

            def score(g):
                V.wait_ge(s_dots, g.upto(0))
                if g.old(2):
                    V.wait_ge(s_score, g.upto(-2))
                V.tensor_scalar(clip[:, g.r2, :], dots[:], -20.0, 20.0, ALU.max, ALU.min).then_inc(s_clip, 1)
                A.wait_ge(s_clip, g.upto(0))
                if g.old(2):
                    ps.summed(A, g, -2)
                A.activation(msg[:, g.r2, :, D:D + HEADS0], clip[:, g.r2, :].rearrange("p (i h) -> p i h", i=GROUP),
                             ACT.Exp, scale=0.25).then_inc(s_score, 1)

            def message(g):
                V.wait_ge(s_score, g.upto(0))
                V.tensor_tensor(msg[:, g.r2, :, 0:D].rearrange("p i (h c) -> p i h c", c=HDIM0),
                                ps.rows[:, g.slot, :, D:2 * D].rearrange("p i (h c) -> p i h c", c=HDIM0),
                                msg[:, g.r2, :, D:D + HEADS0].unsqueeze(3).to_broadcast([P, GROUP, HEADS0, HDIM0]),
                                ALU.mult).then_inc(s_msg, 1)

            def sums(g):
                PE.wait_ge(s_msg, g.upto(0))
                ps.scatter(g, lambda i: [(0, msg[:, g.r2, i, :])])

            ps.run([(0, gather), (2, queries_to_edges), (1, turned.turn), (4, ps.add(0)), (3, message),
                    (4, ps.add(1)), (2, products), (4, ps.add(2)), (2, dot), (4, ps.add(3)), (2, score),
                    (0, ps.select), (3, sums)])

    def edges1():
        with Phase(nc, "e1") as ctx:
            w1 = ctx.sb("w1", [ED + 1, D])
            chunk_of = ctx.sb("chunk", [1, ITEMS_PAD], I32)
            ps = EdgePass(ctx, x1_t, D + 1, W1, local_d,
                          [(w1[0:ED, :], a["L1_gnn_W1e"]),
                           (w1[ED:ED + 1, :], a["L1_gnn_b1e"].rearrange("(a n) -> a n", a=1)),
                           (chunk_of[:], item_rows[1:2, :])])
            SP.wait_ge(ps.s_load, ps.loads)
            attr = ps.sb("attr", [ED + 1, SLOTS, GROUP, P])
            hid = ps.sb("hid", [P, 2, GROUP, D])
            s_attr = [ps.sem(f"attr{u}") for u in range(SLOTS)]
            s_h, s_relu, ones = ps.sem("h"), ps.sem("relu"), ps.sem("ones")
            B_H = (4, 5)
            V.memset(attr[ED:ED + 1, :, :, :], 1.0).then_inc(ones, 1)
            PE.wait_ge(ones, 1)

            def gather(g):
                ps.gather(g, ps.s_sums[-1])
                u = g.slot
                _, chunks = nc.values_load_multi_w_load_instructions(
                    chunk_of[0:1, ds(g.n * GROUP, GROUP)], engines=(SP_ENGINE,), min_val=0, max_val=N_CHUNKS - 1,
                    skip_runtime_bounds_check_because=CLIPPED)
                if g.old(SLOTS):
                    SP.wait_ge(s_h, g.upto(-SLOTS))
                for i in range(GROUP):
                    SP.dma_start(attr[0:ED, u, i, :], a["attr_rows"][ds(chunks[i], 1), :, :]
                                 .rearrange("a k e -> (a k) e")).then_inc(s_attr[u], 16)

            def hidden(g):
                PE.wait_ge(s_attr[g.slot], (g.round + 1) * 64)
                if g.old(2):
                    PE.wait_ge(s_relu, g.upto(-2))
                for i in range(GROUP):
                    m = PE.matmul(bank[B_H[g.r2]][:, i * P:(i + 1) * P], attr[:, g.slot, i, :], w1[:],
                                  start=True, stop=True)
                m.then_inc(s_h, 1)
                A.wait_ge(s_h, g.upto(0))
                ps.have_rows(A, g)
                if g.old(2):
                    ps.summed(A, g, -2)
                for i in range(GROUP):
                    m = A.activation(hid[:, g.r2, i, :], bank[B_H[g.r2]][:, i * P:(i + 1) * P], ACT.Relu,
                                     scale=ps.rows[:, g.slot, i, D:D + 1])
                m.then_inc(s_relu, 1)

            def sums(g):
                PE.wait_ge(s_relu, g.upto(0))
                PE.wait_ge(ps.s_sel, g.upto(0))
                ps.have_rows(PE, g)
                ps.scatter(g, lambda i: [(0, ps.rows[:, g.slot, i, :]), (D + 1, hid[:, g.r2, i, :])])

            ps.run([(0, gather), (0, ps.select), (0, hidden), (1, sums), (1, ps.add(0)), (1, ps.add(1)),
                    (1, ps.add(2)), (1, ps.add(3))])

    def edges2():
        with Phase(nc, "e2") as ctx:
            w0 = ctx.sb("w0", [2 * NB, 2 * RH])
            b0 = ctx.sb("b0", [2 * RH, 1])
            w1 = ctx.sb("w1", [2 * RH, 2, RH])
            b1 = ctx.sb("b1", [RH, 1])
            w2 = ctx.sb("w2", [RH + 1, D])
            rhat = ctx.sb("rhat", [P, N_ITEMS, 3])
            clear = ctx.sem("clear")
            G.memset(w0[:], 0.0).then_inc(clear, 1)
            G.memset(w1[:], 0.0).then_inc(clear, 1)
            SP.wait_ge(clear, 2)
            fixed = [(w0[h * NB:(h + 1) * NB, h * RH:(h + 1) * RH], a["L2_gnn_mlp_w0"]) for h in range(2)]
            fixed += [(b0[h * RH:(h + 1) * RH, :], vec_col(a["L2_gnn_mlp_b0"])) for h in range(2)]
            fixed += [(w1[h * RH:(h + 1) * RH, h, :], a["L2_gnn_mlp_w1"]) for h in range(2)]
            fixed += [(b1[:], vec_col(a["L2_gnn_mlp_b1"])), (w2[0:RH, :], a["L2_gnn_mlp_w2"]),
                      (w2[RH:RH + 1, :], a["L2_gnn_mlp_b2"].rearrange("(a n) -> a n", a=1)),
                      (rhat[:], rhat_d[:, 0:N_ITEMS, :])]
            ps = EdgePass(ctx, up_t, D, W2, local_d, fixed)
            emb = ps.sb("emb", [2 * NB, SLOTS, 2 * P])
            h1 = ps.sb("h1", [2 * RH, 2, 2 * P])
            h2 = ps.sb("h2", [RH + 1, 2, 4 * P])
            u_c = ps.sb("u_c", [P, GROUP, 3, MUL])
            u = ps.sb("u", [P, GROUP, MUL])
            msg = ps.sb("msg", [P, 2, GROUP, W2 + MUL])
            s_emb = [ps.sem(f"emb{n}") for n in range(SLOTS)]
            s_h1, s_silu1, s_h2, s_silu2, s_w = (ps.sem(n) for n in ("h1", "silu1", "h2", "silu2", "w"))
            s_by_s, s_u_c, s_u, s_msg, ones = (ps.sem(n) for n in ("by_s", "u_c", "u", "msg", "ones"))
            B_H1, B_H2, B_W = 4, 5, (6, 7)
            distance, at_zero = ps.selector()
            V.memset(h2[RH:RH + 1, :, :], 1.0).then_inc(ones, 1)
            PE.wait_ge(ones, 1)

            def gather(g):
                ps.gather(g, s_msg)
                if g.old(SLOTS):
                    SP.wait_ge(s_h1, g.upto(-SLOTS))
                SP.dma_start(emb[:, g.slot, :],
                             emb_d[ds(g.n * 2, 2), :, :, :].rearrange("a j b e -> (a j) (b e)")
                             ).then_inc(s_emb[g.slot], 16)

            def hidden1(g):
                PE.wait_ge(s_emb[g.slot], (g.round + 1) * 16)
                if g.old(1):
                    PE.wait_ge(s_silu1, g.upto(-1))
                PE.matmul(bank[B_H1][:, 0:2 * P], w0[:], emb[:, g.slot, :], start=True, stop=True
                          ).then_inc(s_h1, 1)
                A.wait_ge(s_h1, g.upto(0))
                if g.old(2):
                    A.wait_ge(s_h2, g.upto(-2))
                A.activation(h1[:, g.r2, :], bank[B_H1][:, 0:2 * P], ACT.Silu, bias=b0[:]).then_inc(s_silu1, 1)

            def hidden2(g):
                PE.wait_ge(s_silu1, g.upto(0))
                if g.old(1):
                    PE.wait_ge(s_silu2, g.upto(-1))
                for h in range(2):
                    m = PE.matmul(bank[B_H2][0:RH, h * 2 * P:(h + 1) * 2 * P], w1[:, h, :], h1[:, g.r2, :],
                                  start=True, stop=True)
                m.then_inc(s_h2, 1)
                A.wait_ge(s_h2, g.upto(0))
                if g.old(2):
                    A.wait_ge(s_w, g.upto(-2))
                A.activation(h2[0:RH, g.r2, :], bank[B_H2][0:RH, :], ACT.Silu, bias=b1[:]).then_inc(s_silu2, 1)

            def weights(g):
                PE.wait_ge(s_silu2, g.upto(0))
                if g.old(2):
                    PE.wait_ge(s_msg, g.upto(-2))
                for i in range(GROUP):
                    m = PE.matmul(bank[B_W[g.r2]][:, i * P:(i + 1) * P], h2[:, g.r2, i * P:(i + 1) * P], w2[:],
                                  start=True, stop=True)
                m.then_inc(s_w, 1)

            def scalars(g):
                return ps.rows[:, g.slot, :, 0:MUL]

            def vectors(g):
                return ps.rows[:, g.slot, :, MUL:].rearrange("p i (c k) -> p i c k", c=3)

            def direction(g):
                return rhat[:, ds(g.n * GROUP, GROUP), :].unsqueeze(3).to_broadcast([P, GROUP, 3, MUL])

            def three(t):
                return t.unsqueeze(2).to_broadcast([P, GROUP, 3, MUL])

            def by_direction(g):
                ps.have_rows(V, g)
                if g.old(1):
                    V.wait_ge(s_u, g.upto(-1))
                V.tensor_tensor(u_c[:], vectors(g), direction(g), ALU.mult).then_inc(s_u_c, 1)

            def by_scalars(g):
                V.wait_ge(s_w, g.upto(0))
                if g.old(2):
                    ps.summed(V, g, -2)
                    V.wait_ge(s_msg, g.upto(-2))
                V.tensor_tensor(msg[:, g.r2, :, 0:MUL], quad(B_W[g.r2])[:, :, 0:MUL], scalars(g), ALU.mult)
                V.tensor_tensor(msg[:, g.r2, :, W2:], quad(B_W[g.r2])[:, :, MUL:2 * MUL], scalars(g), ALU.mult
                                ).then_inc(s_by_s, 1)

            def dot(g):
                V.wait_ge(s_u_c, g.upto(0))
                if g.old(1):
                    V.wait_ge(s_msg, g.upto(-1))
                V.tensor_reduce(u[:], u_c[:].rearrange("p i c k -> p i k c"), AX.X, ALU.add).then_inc(s_u, 1)

            def by_c(g):
                return msg[:, g.r2, :, 2 * MUL:W2].rearrange("p i (c s k) -> p i c s k", c=3, s=2)

            def m1(g):
                V.wait_ge(s_by_s, g.upto(0))
                V.tensor_tensor(by_c(g)[:, :, :, 0, :], three(msg[:, g.r2, :, W2:]), direction(g), ALU.mult)

            def m2(g):
                V.tensor_tensor(by_c(g)[:, :, :, 1, :], three(quad(B_W[g.r2])[:, :, 2 * MUL:3 * MUL]), vectors(g),
                                ALU.mult)

            def m3(g):
                V.wait_ge(s_u, g.upto(0))
                V.tensor_tensor(msg[:, g.r2, :, MUL:2 * MUL], quad(B_W[g.r2])[:, :, 3 * MUL:], u[:], ALU.mult
                                ).then_inc(s_msg, 1)

            def sums(g):
                PE.wait_ge(s_msg, g.upto(0))
                PE.wait_ge(ps.s_sel, g.upto(0))
                ps.scatter(g, lambda i: [(0, msg[:, g.r2, i, 0:W2])])

            ps.run([(0, gather), (3, weights), (2, hidden2), (4, sums), (1, hidden1),
                    (2, distance), (2, at_zero), (3, by_direction), (3, by_scalars), (3, dot), (4, ps.add(0)), (3, m1),
                    (4, ps.add(1)), (3, m2), (4, ps.add(2)), (3, m3), (4, ps.add(3))])

    def edges3_max():
        with Phase(nc, "e3m") as ctx:
            ps = EdgePass(ctx, fs_t, D, D, local_last_d)
            reset = ps.sb("reset", [P, SLOTS, GROUP * P])
            run = ps.sb("run", [P, 2, GROUP * P])
            back = ps.sb("back", [P, 2, GROUP, P])
            s_reset = [ps.sem(f"reset{u}") for u in range(SLOTS)]
            s_f, s_run, s_b, s_back, start = (ps.sem(n) for n in ("f", "run", "b", "back", "start"))
            B_F, B_B = (4, 5), (6, 7)
            V.memset(run[:], LOW).then_inc(start, 1)
            V.wait_ge(start, 1)

            def gather(g):
                ps.gather(g, s_f)
                if g.old(SLOTS):
                    SP.wait_ge(s_run, g.upto(-SLOTS))
                SP.dma_start(reset[:, g.slot, :], reset_d[ds(g.n, 1), :].to_broadcast([P, GROUP * P])
                             ).then_inc(s_reset[g.slot], 16)

            def forward(g):
                ps.have_rows(PE, g)
                if g.old(2):
                    PE.wait_ge(s_run, g.upto(-2))
                for i in range(GROUP):
                    m = PE.transpose(bank[B_F[g.r2]][:, i * P:(i + 1) * P], ps.rows[:, g.slot, i, :], ident[:])
                m.then_inc(s_f, 1)
                ps.select(g)
                V.wait_ge(s_f, g.upto(0))
                V.wait_ge(s_reset[g.slot], (g.round + 1) * 16)
                if g.old(1):
                    V.wait_ge(s_run, g.upto(-1))
                if g.old(2):
                    V.wait_ge(s_b, g.upto(-2))
                V.tensor_tensor_scan(run[:, g.r2, :], reset[:, g.slot, :], bank[B_F[g.r2]],
                                     run[:, 1 - g.r2, GROUP * P - 1:GROUP * P], ALU.add, ALU.max
                                     ).then_inc(s_run, 1)

            def backward(g):
                PE.wait_ge(s_run, g.upto(0))
                if g.old(2):
                    PE.wait_ge(s_back, g.upto(-2))
                for i in range(GROUP):
                    m = PE.transpose(bank[B_B[g.r2]][:, i * P:(i + 1) * P], run[:, g.r2, i * P:(i + 1) * P],
                                     ident[:])
                m.then_inc(s_b, 1)
                A.wait_ge(s_b, g.upto(0))
                if g.old(2):
                    ps.summed(A, g, -2)
                A.activation(back[:, g.r2].rearrange("p i d -> p (i d)"), bank[B_B[g.r2]], ACT.Copy
                             ).then_inc(s_back, 1)

            def sums(g):
                PE.wait_ge(s_back, g.upto(0))
                PE.wait_ge(ps.s_sel, g.upto(0))
                ps.scatter(g, lambda i: [(0, back[:, g.r2, i, :])])

            ps.run([(0, gather), (0, forward), (1, backward), (2, sums), (2, ps.add(0)), (2, ps.add(1)),
                    (2, ps.add(2)), (2, ps.add(3))])

    def edges3(at_dst):
        with Phase(nc, "e3") as ctx:
            ps = EdgePass(ctx, fsv_t, 2 * D, W3, local_d)
            B_T, B_D, B_M = 4, (5, 6), 7
            edge = ps.sb("edge", [P, GROUP, D])
            diff = ps.sb("diff", [P, 2, GROUP, D])
            msg = ps.sb("msg", [P, 2, GROUP, W3])
            s_d, s_m, s_a, s_e, s_diff, s_exp, s_msg = (ps.sem(n) for n in
                                                        ("d", "m", "a", "e", "diff", "exp", "msg"))
            turned = Turned(ps, B_T, s_m)
            distance, at_zero = ps.selector()

            def gather(g):
                ps.gather(g, s_msg)

            def to_edges(g):
                tiles = ps.tiles(g, PE_ENGINE)
                PE.wait_ge(turned.s_copied, g.upto(0))
                for n_bank, cols, sem, s_read, k in ((B_D[g.r2], slice(0, D), s_d, s_a, 2),
                                                     (B_M, slice(D, 2 * D), s_m, s_diff, 1)):
                    if g.old(k):
                        PE.wait_ge(s_read, g.upto(-k))
                    for i in range(GROUP):
                        m = PE.matmul(bank[n_bank][:, i * P:(i + 1) * P], turned.sel_t[:, g.r2, i, :],
                                      at_dst[:, ds(tiles[i], 1), cols].rearrange("p a d -> p (a d)"),
                                      start=True, stop=True)
                    m.then_inc(sem, 1)

            def both_ends(g):
                ps.have_rows(V, g)
                V.wait_ge(s_d, g.upto(0))
                if g.old(1):
                    V.wait_ge(s_e, g.upto(-1))
                V.tensor_tensor(edge[:], ps.rows[:, g.slot, :, 0:D], quad(B_D[g.r2]), ALU.add).then_inc(s_a, 1)

            def leaky(g):
                V.wait_ge(s_a, g.upto(0))
                if g.old(2):
                    V.wait_ge(s_exp, g.upto(-2))
                V.scalar_tensor_tensor(out=diff[:, g.r2], in0=edge[:], scalar=0.2, in1=edge[:],
                                       op0=ALU.mult, op1=ALU.max).then_inc(s_e, 1)

            def exps(g):
                V.wait_ge(s_e, g.upto(0))
                V.wait_ge(s_m, g.upto(0))
                V.tensor_tensor(diff[:, g.r2], diff[:, g.r2], quad(B_M), ALU.subtract).then_inc(s_diff, 1)
                A.wait_ge(s_diff, g.upto(0))
                if g.old(2):
                    ps.summed(A, g, -2)
                A.activation(msg[:, g.r2, :, D:2 * D], diff[:, g.r2], ACT.Exp).then_inc(s_exp, 1)

            def message(g):
                V.wait_ge(s_exp, g.upto(0))
                V.tensor_tensor(msg[:, g.r2, :, 0:D], ps.rows[:, g.slot, :, D:2 * D], msg[:, g.r2, :, D:2 * D],
                                ALU.mult).then_inc(s_msg, 1)

            def sums(g):
                PE.wait_ge(s_msg, g.upto(0))
                ps.scatter(g, lambda i: [(0, msg[:, g.r2, i, :])])

            ps.run([(0, gather), (2, to_edges), (0, distance), (1, turned.turn), (0, at_zero),
                    (4, ps.add(0)), (3, message), (4, ps.add(1)), (2, both_ends), (4, ps.add(2)), (2, leaky),
                    (4, ps.add(3)), (2, exps), (3, sums)])

    with root:
        setup()
        with nc.sbuf_tensor("queries", [P, N_TILES, D], F32) as queries:
            project0(queries)
            edges0(queries)
        with nc.sbuf_tensor("inv_root_deg", [P, N_TILES], F32) as inv_root_deg:
            after0(inv_root_deg)
            edges1()
            after1(inv_root_deg)
        edges2()
        with nc.sbuf_tensor("at_dst", [P, N_TILES, 2 * D], F32) as at_dst:
            after2(at_dst)
            edges3_max()
            maxima(at_dst)
            edges3(at_dst)
        after3()


_WEIGHTS = ["L0_gnn_Wq", "L0_gnn_bq", "L0_gnn_Wk", "L0_gnn_bk", "L0_gnn_Wv", "L0_gnn_bv",
            "L1_gnn_W1n", "L1_gnn_b1n", "L1_gnn_W2n", "L1_gnn_b2n", "L1_gnn_W1e", "L1_gnn_b1e",
            "L1_gnn_W2e", "L1_gnn_b2e", "L1_gnn_rms_w", "L2_gnn_W_up0", "L2_gnn_W_up1",
            "L2_gnn_mlp_w0", "L2_gnn_mlp_b0", "L2_gnn_mlp_w1", "L2_gnn_mlp_b1", "L2_gnn_mlp_w2",
            "L2_gnn_mlp_b2", "L2_gnn_W_out0", "L2_gnn_W_out1", "L3_gnn_b_src", "L3_gnn_b_dst", "L3_gnn_b_v"]


def kernel(**inputs):
    import numpy as np
    import concourse.bacc as bacc
    from concourse import mybir as _mybir
    from concourse.bass_utils import run_bass_kernel_spmd as run

    get = lambda name: np.asarray(inputs[name])
    pad = N_CHUNKS * P - N_EDGES

    def chunks(v, fill):
        v = np.concatenate([v, np.full((pad,) + v.shape[1:], fill, v.dtype)])
        return v.reshape((N_CHUNKS, P) + v.shape[1:])

    dst = get("dst")
    ends = np.concatenate([np.full((1,), -1, dst.dtype), dst, np.full((pad + 1,), FAR, dst.dtype)])
    arrays = {
        "x": get("x"),
        "int_rows": np.concatenate([np.stack([ends[c * P:c * P + P + 2] for c in range(N_CHUNKS)]),
                                    chunks(get("src"), 0)], axis=1),
        "float_rows": np.concatenate([chunks(get("edge_attr_3"), 0).transpose(0, 2, 1).reshape(N_CHUNKS, 3 * P),
                                      chunks(get("edge_weight"), 0)], axis=1),
        "attr_rows": np.ascontiguousarray(chunks(get("edge_attr_64"), 0).transpose(0, 2, 1)),
        "gin_eps": get("L1_gnn_gin_eps").reshape(1, 1),
        "W_src_t": np.ascontiguousarray(get("L3_gnn_W_src").T),
        "W_dst_t": np.ascontiguousarray(get("L3_gnn_W_dst").T),
        "W_v_t": np.ascontiguousarray(get("L3_gnn_W_v").T),
    }
    arrays.update({name: get(name) for name in _WEIGHTS})

    nc = bacc.Bacc("TRN2", target_bir_lowering=False, num_devices=1)
    aps = {name: nc.dram_tensor(f"in_{name}", v.shape, _mybir.dt.from_np(v.dtype), kind="ExternalInput").ap()
           for name, v in arrays.items()}
    aps["out"] = nc.dram_tensor("out_x", (N_NODES, D), F32, kind="ExternalOutput").ap()
    build(nc, aps)
    r = run(nc, [{f"in_{name}": np.ascontiguousarray(v) for name, v in arrays.items()}], core_ids=[0])
    return r.results[0]["out_x"]
```
